# Optimizing a Trainium2 kernel written in Bass

```python
import numpy as np
import jax
import jax.numpy as jnp

def _softmax(x, axis=-1):
    return jax.nn.softmax(x, axis=axis)

def _gelu(x):
    return jax.nn.gelu(x, approximate=True)

def _silu(x):
    return jax.nn.silu(x)

def _sigmoid(x):
    return jax.nn.sigmoid(x)

def _layernorm(x, axis=-1, eps=1e-05):
    m = jnp.mean(x, axis=axis, keepdims=True)
    v = jnp.var(x, axis=axis, keepdims=True)
    return (x - m) / jnp.sqrt(v + eps)

def _scatter_add(tgt, idx, src, axis=0):
    return tgt.at[idx].add(src)

def _segment_sum(src, seg, n):
    return jax.ops.segment_sum(src, seg, n)
kernel_name = 'mk_macaron_d2_jaxref_r8_cccbdd'

def setup_inputs(seed: int=0):
    np.random.seed(seed)
    _w = jnp.asarray

    def _L0_attn_setup():
        import jax, jax.numpy as jnp
        import numpy as np
        import math
        D_MODEL = 128
        D_QUERY = 64
        key = jax.random.key(seed)
        k1, k2, k3, k4 = jax.random.split(key, 4)
        X = jax.random.normal(k1, (4, 512, D_MODEL), dtype=jnp.float32)
        Wq = jax.random.normal(k2, (D_MODEL, D_QUERY), dtype=jnp.float32) * (1.0 / math.sqrt(D_MODEL))
        Wk = jax.random.normal(k3, (D_MODEL, D_QUERY), dtype=jnp.float32) * (1.0 / math.sqrt(D_MODEL))
        Wv = jax.random.normal(k4, (D_MODEL, D_MODEL), dtype=jnp.float32) * (1.0 / math.sqrt(D_MODEL))
        return {'X': X, 'Wq': Wq, 'Wk': Wk, 'Wv': Wv}
    _L0_attn_in = _L0_attn_setup()

    def _L0_ffn_setup():
        import jax, jax.numpy as jnp
        import numpy as np
        B, S, H = (2, 256, 128)
        I = 64
        E_R, E_Z = (32, 8)
        E_T = E_R + E_Z
        K = 6
        SCALE = 2.5
        W_INIT = 0.02
        key = jax.random.key(seed)
        k0, k1, k2, k3 = jax.random.split(key, 4)
        return {'hidden_states': jax.random.normal(k0, (B, S, H), jnp.float32), 'classifier_weight': jax.random.normal(k1, (E_T, H), jnp.float32) * W_INIT, 'e_score_correction_bias': jnp.zeros((E_T,), jnp.float32), 'gate_up_proj': jax.random.normal(k2, (E_T, 2 * I, H), jnp.float32) * W_INIT, 'down_proj': jax.random.normal(k3, (E_R, H, I), jnp.float32) * W_INIT}
    _L0_ffn_in = _L0_ffn_setup()

    def _L1_attn_setup():
        import jax, jax.numpy as jnp
        import numpy as np
        from jax import lax
        RWKV_K_CLAMP = 60.0
        RWKV_K_EPS = 1e-08
        key = jax.random.key(seed)
        ks = jax.random.split(key, 12)
        B, T, C = (4, 128, 128)
        s = 1.0 / np.sqrt(C)
        return {'xq': jax.random.normal(ks[0], (B, T, C), jnp.float32), 'xk': jax.random.normal(ks[1], (B, T, C), jnp.float32), 'xv': jax.random.normal(ks[2], (B, T, C), jnp.float32), 'time_decay': jax.random.normal(ks[3], (C, 1), jnp.float32) * 0.1, 'time_first': jnp.full((C, 1), np.log(0.3), jnp.float32), 'time_mix_k': jax.random.uniform(ks[4], (1, 1, C), jnp.float32), 'time_mix_v': jax.random.uniform(ks[5], (1, 1, C), jnp.float32), 'time_mix_r': jax.random.uniform(ks[6], (1, 1, C), jnp.float32), 'Wk': jax.random.normal(ks[7], (C, C), jnp.float32) * s, 'Wv': jax.random.normal(ks[8], (C, C), jnp.float32) * s, 'Wr': jax.random.normal(ks[9], (C, C), jnp.float32) * s, 'Wo': jax.random.normal(ks[10], (C, C), jnp.float32) * s}
    _L1_attn_in = _L1_attn_setup()

    def _L1_ffn_setup():
        import jax, jax.numpy as jnp
        import numpy as np
        B, S, D, H, F, E = (2, 128, 128, 16, 256, 8)
        HD = D // H

        def _ln(x, g, b, eps=1e-05):
            m = x.mean(-1, keepdims=True)
            v = ((x - m) ** 2).mean(-1, keepdims=True)
            return (x - m) / jnp.sqrt(v + eps) * g + b
        key = jax.random.key(seed)
        ks = jax.random.split(key, 12)
        rn = lambda k, shp, s=0.02: jax.random.normal(k, shp, jnp.float32) * s
        return {'src': jax.random.normal(ks[0], (B, S, D), jnp.float32), 'q_w': rn(ks[1], (D, D)), 'k_w': rn(ks[2], (D, D)), 'v_w': rn(ks[3], (D, D)), 'out_w': rn(ks[4], (D, D)), 'gate_w': rn(ks[5], (D, D)), 'gate_b': rn(ks[6], (D,)), 'scale_w': rn(ks[7], (H, HD)), 'n1_g': jnp.ones((D,), jnp.float32), 'n1_b': jnp.zeros((D,), jnp.float32), 'n2_g': jnp.ones((D,), jnp.float32), 'n2_b': jnp.zeros((D,), jnp.float32), 'moe_gate_w': rn(ks[8], (D, E)), 'moe_gate_b': jnp.zeros((E,), jnp.float32), 'w1': rn(ks[9], (E, D, F)), 'b1': jnp.zeros((E, F), jnp.float32), 'ln_g': jnp.ones((E, F), jnp.float32), 'ln_b': jnp.zeros((E, F), jnp.float32), 'w2': rn(ks[10], (E, F, D)), 'b2': jnp.zeros((E, D), jnp.float32), 'res_scale': jnp.ones((E,), jnp.float32)}
    _L1_ffn_in = _L1_ffn_setup()
    _d = {'L0_attn_X': _L0_attn_in['X'], 'L0_attn_Wq': _L0_attn_in['Wq'], 'L0_attn_Wk': _L0_attn_in['Wk'], 'L0_attn_Wv': _L0_attn_in['Wv'], 'L0_ffn_classifier_weight': _L0_ffn_in['classifier_weight'], 'L0_ffn_e_score_correction_bias': _L0_ffn_in['e_score_correction_bias'], 'L0_ffn_gate_up_proj': _L0_ffn_in['gate_up_proj'], 'L0_ffn_down_proj': _L0_ffn_in['down_proj'], 'L1_attn_xk': _L1_attn_in['xk'], 'L1_attn_xv': _L1_attn_in['xv'], 'L1_attn_time_decay': _L1_attn_in['time_decay'], 'L1_attn_time_first': _L1_attn_in['time_first'], 'L1_attn_time_mix_k': _L1_attn_in['time_mix_k'], 'L1_attn_time_mix_v': _L1_attn_in['time_mix_v'], 'L1_attn_time_mix_r': _L1_attn_in['time_mix_r'], 'L1_attn_Wk': _L1_attn_in['Wk'], 'L1_attn_Wv': _L1_attn_in['Wv'], 'L1_attn_Wr': _L1_attn_in['Wr'], 'L1_attn_Wo': _L1_attn_in['Wo'], 'L1_ffn_q_w': _L1_ffn_in['q_w'], 'L1_ffn_k_w': _L1_ffn_in['k_w'], 'L1_ffn_v_w': _L1_ffn_in['v_w'], 'L1_ffn_out_w': _L1_ffn_in['out_w'], 'L1_ffn_gate_w': _L1_ffn_in['gate_w'], 'L1_ffn_gate_b': _L1_ffn_in['gate_b'], 'L1_ffn_scale_w': _L1_ffn_in['scale_w'], 'L1_ffn_n1_g': _L1_ffn_in['n1_g'], 'L1_ffn_n1_b': _L1_ffn_in['n1_b'], 'L1_ffn_n2_g': _L1_ffn_in['n2_g'], 'L1_ffn_n2_b': _L1_ffn_in['n2_b'], 'L1_ffn_moe_gate_w': _L1_ffn_in['moe_gate_w'], 'L1_ffn_moe_gate_b': _L1_ffn_in['moe_gate_b'], 'L1_ffn_w1': _L1_ffn_in['w1'], 'L1_ffn_b1': _L1_ffn_in['b1'], 'L1_ffn_ln_g': _L1_ffn_in['ln_g'], 'L1_ffn_ln_b': _L1_ffn_in['ln_b'], 'L1_ffn_w2': _L1_ffn_in['w2'], 'L1_ffn_b2': _L1_ffn_in['b2'], 'L1_ffn_res_scale': _L1_ffn_in['res_scale']}
    _x0 = _d['L0_attn_X']
    _d['L0_attn_X'] = jax.random.normal(jax.random.fold_in(jax.random.key(seed), 1), (32, 256, 128), dtype=_x0.dtype)
    del _x0
    return _d

def reference(L0_attn_X, L0_attn_Wq, L0_attn_Wk, L0_attn_Wv, L0_ffn_classifier_weight, L0_ffn_e_score_correction_bias, L0_ffn_gate_up_proj, L0_ffn_down_proj, L1_attn_xk, L1_attn_xv, L1_attn_time_decay, L1_attn_time_first, L1_attn_time_mix_k, L1_attn_time_mix_v, L1_attn_time_mix_r, L1_attn_Wk, L1_attn_Wv, L1_attn_Wr, L1_attn_Wo, L1_ffn_q_w, L1_ffn_k_w, L1_ffn_v_w, L1_ffn_out_w, L1_ffn_gate_w, L1_ffn_gate_b, L1_ffn_scale_w, L1_ffn_n1_g, L1_ffn_n1_b, L1_ffn_n2_g, L1_ffn_n2_b, L1_ffn_moe_gate_w, L1_ffn_moe_gate_b, L1_ffn_w1, L1_ffn_b1, L1_ffn_ln_g, L1_ffn_ln_b, L1_ffn_w2, L1_ffn_b2, L1_ffn_res_scale):

    def _L0_attn_ref(X, Wq, Wk, Wv):
        import jax, jax.numpy as jnp
        import numpy as np
        import math
        D_MODEL = 128
        D_QUERY = 64
        B, T, _ = X.shape
        Q = X @ Wq
        K = X @ Wk
        V = X @ Wv
        scores = jnp.einsum('btd,bsd->bts', Q, K)
        causal = jnp.tril(jnp.ones((T, T), dtype=bool))
        scores = jnp.where(causal[None, :, :], scores, -jnp.inf)
        attn = jax.nn.softmax(scores / math.sqrt(D_QUERY), axis=2)
        return attn @ V

    def _L0_ffn_ref(hidden_states, classifier_weight, e_score_correction_bias, gate_up_proj, down_proj):
        import jax, jax.numpy as jnp
        import numpy as np
        B, S, H = (2, 256, 128)
        I = 64
        E_R, E_Z = (32, 8)
        E_T = E_R + E_Z
        K = 6
        SCALE = 2.5
        W_INIT = 0.02
        orig_shape = hidden_states.shape
        x = hidden_states.reshape(-1, H).astype(jnp.float32)
        T = x.shape[0]
        logits = x @ classifier_weight.T
        scores = jax.nn.softmax(logits, axis=-1)
        _, topk_idx = jax.lax.top_k(scores + e_score_correction_bias[None, :], K)
        topk_w = jnp.take_along_axis(scores, topk_idx, axis=1) * SCALE
        w_full = jnp.zeros((T, E_T), jnp.float32).at[jnp.arange(T)[:, None], topk_idx].add(topk_w)
        zero_w = w_full[:, E_R:].sum(axis=-1, keepdims=True)
        out0 = x * zero_w
        routed_w = w_full[:, :E_R].T

        def body(out, xs):
            Wgu, Wd, we = xs
            gate, up = jnp.split(x @ Wgu.T, 2, axis=-1)
            y = jax.nn.silu(gate) * up @ Wd.T
            return (out + we[:, None] * y, None)
        out, _ = jax.lax.scan(body, out0, (gate_up_proj[:E_R], down_proj, routed_w))
        return out.reshape(orig_shape).astype(hidden_states.dtype)

    def _L1_attn_ref(xq, xk, xv, time_decay, time_first, time_mix_k, time_mix_v, time_mix_r, Wk, Wv, Wr, Wo):
        import jax, jax.numpy as jnp
        import numpy as np
        from jax import lax
        RWKV_K_CLAMP = 60.0
        RWKV_K_EPS = 1e-08
        B, T, C = xq.shape
        x = xq
        xx = jnp.pad(x, ((0, 0), (1, 0), (0, 0)))[:, :T]
        k = jnp.einsum('btc,dc->btd', x * time_mix_k + xx * (1 - time_mix_k), Wk)
        v = jnp.einsum('btc,dc->btd', x * time_mix_v + xx * (1 - time_mix_v), Wv)
        r = jnp.einsum('btc,dc->btd', x * time_mix_r + xx * (1 - time_mix_r), Wr)
        sr = jax.nn.sigmoid(r)
        kc = jnp.exp(jnp.minimum(k, RWKV_K_CLAMP)).transpose(0, 2, 1)
        vc = v.transpose(0, 2, 1)
        kv = kc * vc
        curve = jnp.arange(T - 1, dtype=jnp.float32) - (T - 2)
        time_w = jnp.concatenate([jnp.exp(time_decay) * curve[None, :], time_first], axis=-1)
        w = jnp.exp(time_w)[:, None, :]

        def dconv(a):
            ap = jnp.pad(a, ((0, 0), (0, 0), (T - 1, 0)))
            return lax.conv_general_dilated(ap, w, (1,), 'VALID', feature_group_count=C, dimension_numbers=('NCH', 'OIH', 'NCH'))
        wkv = dconv(kv)
        wk = dconv(kc) + RWKV_K_EPS
        out = sr * (wkv / wk).transpose(0, 2, 1)
        return jnp.einsum('btc,dc->btd', out, Wo)

    def _L1_ffn_ref(src, q_w, k_w, v_w, out_w, gate_w, gate_b, scale_w, n1_g, n1_b, n2_g, n2_b, moe_gate_w, moe_gate_b, w1, b1, ln_g, ln_b, w2, b2, res_scale):
        import jax, jax.numpy as jnp
        import numpy as np
        B, S, D, H, F, E = (2, 128, 128, 16, 256, 8)
        HD = D // H

        def _ln(x, g, b, eps=1e-05):
            m = x.mean(-1, keepdims=True)
            v = ((x - m) ** 2).mean(-1, keepdims=True)
            return (x - m) / jnp.sqrt(v + eps) * g + b
        b, s, d = src.shape
        h = scale_w.shape[0]
        hd = d // h
        q = (src @ q_w).reshape(b, s, h, hd).transpose(0, 2, 1, 3)
        k = (src @ k_w).reshape(b, s, h, hd).transpose(0, 2, 1, 3)
        v = (src @ v_w).reshape(b, s, h, hd).transpose(0, 2, 1, 3)
        scores = jnp.einsum('bhqd,bhkd->bhqk', q, k) / np.float32(np.sqrt(hd))
        scale = jax.nn.sigmoid(jnp.einsum('bhsd,hd->bhs', q, scale_w)) * 2.0
        scores = scores * scale[..., None]
        aw = jax.nn.softmax(scores, axis=-1)
        out = jnp.einsum('bhqk,bhkd->bhqd', aw, v).transpose(0, 2, 1, 3).reshape(b, s, d)
        gate = jax.nn.sigmoid(out @ gate_w + gate_b)
        attn = out * gate @ out_w
        x = _ln(src + attn, n1_g, n1_b)
        xr = x.reshape(-1, d)
        n = xr.shape[0]
        logits = xr @ moe_gate_w + moe_gate_b
        top_v, top_i = jax.lax.top_k(logits, 2)
        wts = jax.nn.softmax(top_v, axis=-1)
        chosen = jnp.max(top_i, axis=-1)

        def expert(W1, B1, G, Bt, W2, B2, rsc):
            hh = xr @ W1 + B1
            hh = jax.nn.gelu(_ln(hh, G, Bt), approximate=False)
            return (hh @ W2 + B2) * rsc + xr
        outs = jax.vmap(expert)(w1, b1, ln_g, ln_b, w2, b2, res_scale)
        sel = jnp.take_along_axis(outs.transpose(1, 0, 2), chosen[:, None, None], axis=1)[:, 0]
        moe = sel * jnp.sum(wts, axis=-1, keepdims=True)
        return _ln(x + moe.reshape(b, s, d), n2_g, n2_b)
    x = L0_attn_X
    x = x + 0.5 * _L0_ffn_ref(_layernorm(x, axis=-1), L0_ffn_classifier_weight, L0_ffn_e_score_correction_bias, L0_ffn_gate_up_proj, L0_ffn_down_proj)
    x = x + _L0_attn_ref(_layernorm(x, axis=-1), L0_attn_Wq, L0_attn_Wk, L0_attn_Wv)
    x = x + 0.5 * _L0_ffn_ref(_layernorm(x, axis=-1), L0_ffn_classifier_weight, L0_ffn_e_score_correction_bias, L0_ffn_gate_up_proj, L0_ffn_down_proj)
    x = x + 0.5 * _L1_ffn_ref(_layernorm(x, axis=-1), L1_ffn_q_w, L1_ffn_k_w, L1_ffn_v_w, L1_ffn_out_w, L1_ffn_gate_w, L1_ffn_gate_b, L1_ffn_scale_w, L1_ffn_n1_g, L1_ffn_n1_b, L1_ffn_n2_g, L1_ffn_n2_b, L1_ffn_moe_gate_w, L1_ffn_moe_gate_b, L1_ffn_w1, L1_ffn_b1, L1_ffn_ln_g, L1_ffn_ln_b, L1_ffn_w2, L1_ffn_b2, L1_ffn_res_scale)
    x = x + _L1_attn_ref(_layernorm(x, axis=-1), L1_attn_xk, L1_attn_xv, L1_attn_time_decay, L1_attn_time_first, L1_attn_time_mix_k, L1_attn_time_mix_v, L1_attn_time_mix_r, L1_attn_Wk, L1_attn_Wv, L1_attn_Wr, L1_attn_Wo)
    x = x + 0.5 * _L1_ffn_ref(_layernorm(x, axis=-1), L1_ffn_q_w, L1_ffn_k_w, L1_ffn_v_w, L1_ffn_out_w, L1_ffn_gate_w, L1_ffn_gate_b, L1_ffn_scale_w, L1_ffn_n1_g, L1_ffn_n1_b, L1_ffn_n2_g, L1_ffn_n2_b, L1_ffn_moe_gate_w, L1_ffn_moe_gate_b, L1_ffn_w1, L1_ffn_b1, L1_ffn_ln_g, L1_ffn_ln_b, L1_ffn_w2, L1_ffn_b2, L1_ffn_res_scale)
    return x

_drawn_inputs = setup_inputs


def setup_inputs(seed=0):
    import zlib

    import numpy as np

    out = dict(_drawn_inputs(seed))
    spreads = {'L0_ffn_e_score_correction_bias': (0.0, 0.1),
     'L1_attn_time_first': (-1.2039728164672852, 0.6),
     'L1_ffn_n1_g': (1.0, 0.2),
     'L1_ffn_n1_b': (0.0, 0.1),
     'L1_ffn_n2_g': (1.0, 0.2),
     'L1_ffn_n2_b': (0.0, 0.1),
     'L1_ffn_moe_gate_b': (0.0, 0.1),
     'L1_ffn_b1': (0.0, 0.313),
     'L1_ffn_ln_g': (1.0, 0.6),
     'L1_ffn_ln_b': (0.0, 0.8),
     'L1_ffn_b2': (0.0, 0.281),
     'L1_ffn_res_scale': (1.0, 0.6)}
    factors = {'L0_ffn_classifier_weight': 4.055,
     'L0_ffn_gate_up_proj': 8.0,
     'L0_ffn_down_proj': 8.0,
     'L1_attn_time_decay': 5.665,
     'L1_ffn_q_w': 8.0,
     'L1_ffn_k_w': 8.0,
     'L1_ffn_v_w': 8.0,
     'L1_ffn_out_w': 8.0,
     'L1_ffn_gate_w': 8.0,
     'L1_ffn_gate_b': 8.0,
     'L1_ffn_scale_w': 8.0}
    for name, (base, spread) in spreads.items():
        noise = np.random.default_rng([zlib.crc32(name.encode()), seed]).standard_normal(out[name].shape)
        drawn = base * np.exp(spread * noise) if base else spread * noise
        out[name] = jnp.asarray(drawn.astype(out[name].dtype))
    for name, factor in factors.items():
        out[name] = (out[name] * factor).astype(out[name].dtype)
    return out
```

```python
from contextlib import ExitStack, contextmanager

import concourse.bass as bass
from concourse import mybir

F32 = mybir.dt.float32
F32R = mybir.dt.float32r
BF16 = mybir.dt.bfloat16
I32 = mybir.dt.int32
ALU = mybir.AluOpType
ACT = mybir.ActivationFunctionType
AX = mybir.AxisListType

P = 128
D = 128
EPS = 1e-5
BIG = 3e38
RSQRT_SEED = 1597463007.0


def after(eng, sem, count):
    if isinstance(count, int) and count <= 0:
        return
    eng.wait_ge(sem, count)


@contextmanager
def semaphores(nc, phase, names):
    sems = [nc.alloc_semaphore(f"{k}_{phase}") for k in names]
    yield dict(zip(names, sems))
    nc.clear_and_free_semaphores(sems)
    nc.all_engine_barrier()


class Chain:

    def __init__(self, eng, sem, per, turn=None):
        self.eng, self.sem, self.per, self.turn = eng, sem, per, turn

    def begin(self, round_):
        self.base, self.n = round_ * self.per, 0

    def step(self, ins):
        self.n += 1
        ins.then_inc(self.sem, 1)
        self.eng.wait_ge(self.sem, self.base + self.n)

    def step_apart(self, ins):
        self.step(ins)
        self.eng.sem_inc(self.turn, 1)

    def end(self):
        assert self.n == self.per, (self.n, self.per)


PEELED = 3


def slots(eng, n, body):
    turns = max(0, (n - 1 - PEELED) // 2)
    looped = range(PEELED, PEELED + 2 * turns)
    for t in range(-1, n + 1):
        if t not in looped:
            body(t, t % 2, t > 0, 0 <= t < n, t + 1 < n)
        elif t == PEELED:
            with eng.Fori(0, turns) as i:
                body(2 * i + PEELED, PEELED % 2, True, True, True)
                body(2 * i + PEELED + 1, 1 - PEELED % 2, True, True, True)


RSQRT_STEPS = 11


def rsqrt(v, step, y, a, t):
    step(v.tensor_scalar(t.bitcast(I32), a.bitcast(I32), 1, None, ALU.logical_shift_right))
    step(v.tensor_scalar(y.bitcast(I32), t.bitcast(I32), -1.0, RSQRT_SEED, ALU.mult, ALU.add))
    for _ in range(3):
        step(v.scalar_tensor_tensor(t, y, -0.5, y, ALU.mult, ALU.mult))
        step(v.tensor_tensor(t, t, a, ALU.mult))
        step(v.scalar_tensor_tensor(y, t, 1.5, y, ALU.add, ALU.mult))


def moments(v, step, n, st, mean, var, t):
    step(v.tensor_tensor(mean, st[1], st[4], ALU.add))
    step(v.tensor_scalar(mean, mean, 0.5, None, ALU.mult))
    step(v.tensor_tensor(t, st[1], st[4], ALU.subtract))
    step(v.scalar_tensor_tensor(t, t, 0.25, t, ALU.mult, ALU.mult))
    step(v.tensor_tensor(var, st[2], st[5], ALU.add))
    step(v.tensor_scalar(var, var, 1.0 / n, EPS, ALU.mult, ALU.add))
    step(v.tensor_tensor(var, var, t, ALU.add))


MOMENT_STEPS = 7


class Core:

    def __init__(self, nc, ctx, tiles):
        def sb(name, shape, dt=F32):
            return ctx.enter_context(nc.sbuf_tensor(name, shape, dt))

        self.nc, self.tiles = nc, tiles
        self.X = sb("X", [P, tiles, D])
        self.stats = sb("stats", [P, tiles, 6])
        self.mean = sb("mean", [P, tiles, 1])
        self.rstd = sb("rstd", [P, tiles, 1])
        self.ident = sb("ident", [P, P])
        self.identb = sb("identb", [P, P], BF16)


def load_phase(nc, K, x_dram):
    with ExitStack() as c:
        ones = c.enter_context(nc.sbuf_tensor("ones_sq", [P, P], F32))
        loads = 4 if K.tiles % 4 == 0 else 1
        s = c.enter_context(semaphores(nc, "load", ["ones_set", "ident_set"] + [f"x_loaded{i}" for i in range(loads)]))
        block = c.enter_context(nc.Block())
        per = K.tiles // loads
        xs = x_dram.rearrange("b (t p) d -> p (b t) d", p=P)

        @block.sync
        def _(sp):
            for i in range(loads):
                sp.dma_start(K.X[:, i * per:(i + 1) * per, :], xs[:, i * per:(i + 1) * per, :]).then_inc(s[f"x_loaded{i}"], 16)

        @block.gpsimd
        def _(pool):
            pool.memset(ones[:], 1.0).then_inc(s["ones_set"], 1)
            pool.wait_ge(s["ones_set"], 1)
            pool.affine_select(out=K.ident[:], in_=ones[:], compare_op=ALU.is_equal, fill=0.0, base=0,
                               pattern=[[-1, P]], channel_multiplier=1).then_inc(s["ident_set"], 1)
            pool.wait_ge(s["ident_set"], 1)
            pool.tensor_copy(K.identb[:], K.ident[:])

        @block.vector
        def _(v):
            for i in range(loads):
                v.wait_ge(s[f"x_loaded{i}"], 16)
                for t in range(i * per, (i + 1) * per):
                    v.bn_stats(K.stats[:, t, :], K.X[:, t, :])


def norm_phase(nc, K, name):
    with ExitStack() as c:
        var = c.enter_context(nc.sbuf_tensor(f"var_{name}", [P, K.tiles, 1], F32))
        t = c.enter_context(nc.sbuf_tensor(f"t_{name}", [P, K.tiles, 1], F32))
        s = c.enter_context(semaphores(nc, name, ("norm_chain",)))
        block = c.enter_context(nc.Block())

        @block.vector
        def _(v):
            ch = Chain(v, s["norm_chain"], MOMENT_STEPS + RSQRT_STEPS)
            ch.begin(0)
            st = [K.stats[:, :, i:i + 1] for i in range(6)]
            moments(v, ch.step, D, st, K.mean[:], var[:], t[:])
            rsqrt(v, ch.step, K.rstd[:], var[:], t[:])
            ch.end()



def l0_ffn_weights(nc, K, ctx, cls_w, cls_b, gate_up, down):
    ET, H = cls_w.shape
    ER, _, I = down.shape
    pairs = ER // 2

    def sb(name, shape, dt=F32):
        return ctx.enter_context(nc.sbuf_tensor(name, shape, dt))

    K.ER, K.ET, K.I, K.pairs = ER, ET, I, pairs
    K.wg = sb("wg", [P, ER, I])
    K.wu = sb("wu", [P, ER, I])
    K.wd = sb("wd", [P, pairs, D])
    K.wc = sb("wc", [P, ET])
    K.bias = sb("cls_bias", [P, ET])
    K.sel = sb("sel", [3 * ER, pairs, P], BF16)
    GB = 8
    with ExitStack() as c:
        raw_gu = c.enter_context(nc.sbuf_tensor("raw_gu", [P, ER, H], F32))
        raw_d = c.enter_context(nc.sbuf_tensor("raw_d", [P, ER, I], F32))
        raw_c = c.enter_context(nc.sbuf_tensor("raw_c", [ET, H], F32))
        ps = [c.enter_context(nc.psum_tensor(f"ps_w{i}", [P, 4, P], F32)) for i in range(2)]
        s = c.enter_context(semaphores(nc, "w0", ("gu_loaded", "d_loaded", "c_loaded", "b_loaded", "turned", "copied",
                                                  "sel_step")))
        block = c.enter_context(nc.Block())
        jobs = ER // 4 + pairs // 4 + 1

        @block.sync
        def _(sp):
            sp.dma_start(raw_gu[:], gate_up[0:ER].rearrange("e f d -> f e d")).then_inc(s["gu_loaded"], 16)
            sp.dma_start(raw_c[:], cls_w).then_inc(s["c_loaded"], 16)
            sp.dma_start(K.bias[:], cls_b.rearrange("(a e) -> a e", a=1).to_broadcast([P, ET])).then_inc(s["b_loaded"], 16)
            sp.wait_ge(s["b_loaded"], 16)

        @block.gpsimd
        def _(pool):
            pool.memset(K.sel[:], 0.0).then_inc(s["sel_step"], 1)
            v = K.sel[:].rearrange("k p (h m) -> k p h m", h=2)
            for b in range(3):
                pool.wait_ge(s["sel_step"], b + 1)
                pool.affine_select(out=v, in_=v, compare_op=ALU.not_equal, fill=1.0, base=-ER * b,
                                   pattern=[[-2, pairs], [-1, 2], [0, P // 2]], channel_multiplier=1).then_inc(s["sel_step"], 1)

        @block.tensor
        def _(pe):
            pe.wait_ge(s["gu_loaded"], 16)
            pe.wait_ge(s["d_loaded"], 16)
            pe.wait_ge(s["c_loaded"], 16)
            for j in range(jobs):
                after(pe, s["copied"], j - 1)
                for i in range(4):
                    if j < ER // 4:
                        m = pe.transpose(ps[j % 2][:, i, :], raw_gu[:, 4 * j + i, :], K.ident[:])
                    elif j < jobs - 1:
                        p = 4 * (j - ER // 4) + i
                        m = pe.transpose(ps[j % 2][:, i, :], raw_d[:, 2 * p:2 * p + 2, :].rearrange("p e f -> p (e f)"), K.ident[:])
                    elif i == 0:
                        m = pe.transpose(ps[j % 2][:, 0, 0:ET], raw_c[:], K.ident[0:ET, 0:ET])
                m.then_inc(s["turned"], 1)

        @block.vector
        def _(v):
            for j in range(jobs):
                v.wait_ge(s["turned"], j + 1)
                if j < ER // 4:
                    v.tensor_copy(K.wg[:, 4 * j:4 * j + 4, :], ps[j % 2][:, :, 0:I])
                    v.tensor_copy(K.wu[:, 4 * j:4 * j + 4, :], ps[j % 2][:, :, I:2 * I]).then_inc(s["copied"], 1)
                elif j < jobs - 1:
                    p = 4 * (j - ER // 4)
                    v.tensor_copy(K.wd[:, p:p + 4, :], ps[j % 2][:]).then_inc(s["copied"], 1)
                else:
                    v.tensor_copy(K.wc[:], ps[j % 2][:, 0, 0:ET]).then_inc(s["copied"], 1)

        @block.scalar
        def _(act):
            act.dma_start(raw_d[:], down.rearrange("e d f -> d e f")).then_inc(s["d_loaded"], 16)


def l0_ffn(nc, K, name):
    ER, ET, pairs = K.ER, K.ET, K.pairs
    G = 4
    N = G * P
    n = K.tiles // G
    TOPK, SCALE = 6, 2.5
    PAD = 8 - TOPK
    with ExitStack() as c:
        sb = lambda nm, s, dt=F32: c.enter_context(nc.sbuf_tensor(f"{nm}_{name}", s, dt))
        ps = lambda nm, s, dt=F32: c.enter_context(nc.psum_tensor(f"{nm}_{name}", s, dt))
        xn = [sb(f"xn{i}", [P, G, D]) for i in range(2)]
        xT = [sb(f"xT{i}", [P, N]) for i in range(2)]
        wparts = sb("wparts", [P, G, 3 * ER], BF16)
        wT = [sb(f"wT{i}", [3 * ER, N], BF16) for i in range(2)]
        zero_w = [sb(f"zero_w{i}", [P, G]) for i in range(2)]
        logit, expd, score = sb("logit", [P, G, ET]), sb("expd", [P, G, ET]), sb("score", [P, G, ET])
        biased, struck = sb("biased", [P, G, ET + PAD]), sb("struck", [P, G, ET + PAD])
        top8, w, rest = sb("top8", [P, G, 8]), sb("w", [P, G, ET]), sb("rest", [P, G, ER])
        rmax, rsum, rinv = sb("rmax", [P, G]), sb("rsum", [P, G]), sb("rinv", [P, G])
        silu = [sb(f"silu{i}", [P, N]) for i in range(2)]
        gated = [sb(f"gated{i}", [P, N]) for i in range(2)]
        hid = [sb(f"hid{i}", [P, N]) for i in range(2)]
        outT, y = sb("outT", [P, N]), sb("y", [P, G, D])
        pg = [ps(f"pg{i}", [P, N]) for i in range(2)]
        pu = [ps(f"pu{i}", [P, N]) for i in range(2)]
        pw = [ps(f"pw{i}", [P, N]) for i in range(2)]
        po, pm = ps("po", [P, N]), ps("pm", [P, N])
        pmb = pm[:].bitcast(BF16)
        s = c.enter_context(semaphores(nc, name, (
            "pad_set", "xn_ready", "xn_turned", "xT_ready", "logits_done", "logits_read", "exp_done", "parts_ready",
            "parts_turned", "wT_ready", "gate_done", "pair_done", "silu_done", "gated_done", "hid_done", "down_done",
            "outT_ready", "out_turned", "out_read", "route_chain", "out_chain", "turn")))
        block = c.enter_context(nc.Block())

        @block.tensor
        def _(pe):
            def body(t, par, prev, cur, nxt):
                for p in range(pairs):
                    if cur:
                        k = t * pairs + p
                        b = p % 2
                        if p == 0:
                            pe.wait_ge(s["wT_ready"], t + 1)
                        after(pe, s["silu_done"], k - 1)
                        pe.matmul(pg[b][:], K.wg[:, 2 * p:2 * p + 2, :], xT[par][:], start=True,
                                  stop=True).then_inc(s["gate_done"], 1)
                        after(pe, s["hid_done"], k - 1)
                        pe.matmul(pu[b][:], K.wu[:, 2 * p:2 * p + 2, :], xT[par][:], start=True, stop=True)
                        pe.matmul(pw[b][:], K.sel[:, p, :], wT[par][:], start=True,
                                  stop=True).then_inc(s["pair_done"], 1)
                        if p >= 2:
                            if p == 2:
                                after(pe, s["outT_ready"], t)
                            down(t, p - 2)
                    if prev and p == 2:
                        pe.wait_ge(s["outT_ready"], t)
                        for j in range(G):
                            m = pe.transpose(pm[:, j * P:(j + 1) * P], outT[:, j * P:(j + 1) * P], K.ident[:])
                        m.then_inc(s["out_turned"], 1)
                    if nxt and p == 5:
                        pe.wait_ge(s["xn_ready"], t + 2)
                        after(pe, s["out_read"], t)
                        for j in range(G):
                            m = pe.transpose(pm[:, j * P:(j + 1) * P], xn[1 - par][:, j, :], K.ident[:])
                        m.then_inc(s["xn_turned"], 1)
                    if nxt and p == 7:
                        pe.wait_ge(s["xT_ready"], t + 2)
                        for j in range(G):
                            m = pe.matmul(pm[:, j * ET:(j + 1) * ET], xT[1 - par][:, j * P:(j + 1) * P], K.wc[:],
                                          start=True, stop=True)
                        m.then_inc(s["logits_done"], 1)
                    if nxt and p == 13:
                        pe.wait_ge(s["parts_ready"], t + 2)
                        for j in range(G):
                            m = pe.transpose(pmb[0:3 * ER, j * P:(j + 1) * P], wparts[:, j, :], K.identb[:])
                        m.then_inc(s["parts_turned"], 1)

                if cur:
                    down(t, pairs - 2)
                    down(t, pairs - 1)

            def down(t, p):
                k = t * pairs + p
                pe.wait_ge(s["hid_done"], k + 1)
                pe.matmul(po[:], K.wd[:, p, :], hid[p % 2][:], start=(p == 0), stop=(p == pairs - 1)).then_inc(s["down_done"], 1)

            slots(pe, n, body)

        @block.scalar
        def _(act):
            def body(t, par, prev, cur, nxt):
                for p in range(pairs):
                    if prev and p == 0:
                        pe_done = t * pairs
                        act.wait_ge(s["down_done"], pe_done)
                        after(act, s["out_turned"], t - 1)
                        act.copy(outT[:], po[:]).then_inc(s["outT_ready"], 1)
                    if cur:
                        k = t * pairs + p
                        act.wait_ge(s["gate_done"], k + 1)
                        after(act, s["gated_done"], k - 1)
                        act.activation(silu[p % 2][:], pg[p % 2][:], ACT.Silu).then_inc(s["silu_done"], 1)
                    if nxt and p == 6:
                        act.wait_ge(s["xn_turned"], t + 2)
                        act.copy(xT[1 - par][:], pm[:]).then_inc(s["xT_ready"], 1)
                    if nxt and p == 9:
                        act.wait_ge(s["logits_read"], t + 2)
                        act.activation(expd[:], logit[:], ACT.Exp).then_inc(s["exp_done"], 1)
                    if nxt and p == 14:
                        act.wait_ge(s["parts_turned"], t + 2)
                        act.copy(wT[1 - par][:], pmb[0:3 * ER, 0:N]).then_inc(s["wT_ready"], 1)

            slots(act, n, body)

        @block.vector
        def _(v):
            route = Chain(v, s["route_chain"], 13, s["turn"])
            out = Chain(v, s["out_chain"], 2, s["turn"])
            v.memset(biased[:], BIG).then_inc(s["pad_set"], 1)
            v.wait_ge(s["pad_set"], 1)

            def gate(t, p):
                k = t * pairs + p
                v.wait_ge(s["silu_done"], k + 1)
                v.wait_ge(s["pair_done"], k + 1)
                v.tensor_tensor(gated[p % 2][:], silu[p % 2][:], pu[p % 2][:], ALU.mult).then_inc(s["gated_done"], 1)

            def weigh(t, p):
                k = t * pairs + p
                v.wait_ge(s["gated_done"], k + 1)
                after(v, s["down_done"], k - 1)
                v.tensor_tensor(hid[p % 2][:], gated[p % 2][:], pw[p % 2][:], ALU.mult).then_inc(s["hid_done"], 1)

            def finish(t, par):
                out.begin(t)
                v.wait_ge(s["out_turned"], t + 1)
                for j in range(G):
                    m = v.scalar_tensor_tensor(y[:, j, :], xn[par][:, j, :], zero_w[par][:, j:j + 1],
                                               pm[:, j * P:(j + 1) * P], ALU.mult, ALU.add)
                m.then_inc(s["out_read"], 1)
                v.wait_ge(s["out_read"], t + 1)
                out.step_apart(v.scalar_tensor_tensor(K.X[:, bass.ds(t * G, G), :], y[:], 0.5 * SCALE,
                                                      K.X[:, bass.ds(t * G, G), :], ALU.mult, ALU.add))
                for j in range(G):
                    m = v.bn_stats(K.stats[:, t * G + j, :], K.X[:, t * G + j, :])
                out.step(m)
                out.end()

            def norm(t, par):
                for j in range(G):
                    m = v.tensor_scalar(xn[par][:, j, :], K.X[:, t * G + j, :], K.mean[:, t * G + j, :],
                                        K.rstd[:, t * G + j, :], ALU.subtract, ALU.mult)
                m.then_inc(s["xn_ready"], 1)

            def center(t):
                route.begin(t)
                pl = pm[:, 0:G * ET].rearrange("p (g e) -> p g e", g=G)
                v.wait_ge(s["logits_done"], t + 1)
                route.step(v.tensor_reduce(rmax[:], pl, AX.X, ALU.max))
                v.tensor_tensor(logit[:], pl, rmax[:, :, None].to_broadcast([P, G, ET]),
                                ALU.subtract).then_inc(s["logits_read"], 1)

            def topk(t, par):
                v.wait_ge(s["exp_done"], t + 1)
                route.step(v.tensor_reduce(rsum[:], expd[:], AX.X, ALU.add))
                route.step(v.reciprocal(rinv[:], rsum[:]))
                route.step(v.tensor_tensor(score[:], expd[:], rinv[:, :, None].to_broadcast([P, G, ET]), ALU.mult))
                route.step_apart(v.tensor_tensor(biased[:, :, 0:ET], score[:],
                                                 K.bias[:, None, :].to_broadcast([P, G, ET]), ALU.add))
                for j in range(G):
                    m = v.max(top8[:, j, :], biased[:, j, :])
                route.step_apart(m)
                for j in range(G):
                    m = v.match_replace(struck[:, j, :], top8[:, j, :], biased[:, j, :], -BIG)
                route.step(m)
                route.step(v.scalar_tensor_tensor(w[:], struck[:, :, 0:ET], -BIG / 2, score[:], ALU.is_le, ALU.mult))
                route.step(v.tensor_reduce(zero_w[par][:], w[:, :, ER:ET], AX.X, ALU.add))
                route.step(v.tensor_copy(wparts[:, :, 0:ER], w[:, :, 0:ER]))
                route.step(v.tensor_tensor(rest[:], w[:, :, 0:ER], wparts[:, :, 0:ER], ALU.subtract))
                route.step(v.tensor_copy(wparts[:, :, ER:2 * ER], rest[:]))
                route.step(v.tensor_tensor(rest[:], rest[:], wparts[:, :, ER:2 * ER], ALU.subtract))
                v.tensor_copy(wparts[:, :, 2 * ER:3 * ER], rest[:]).then_inc(s["parts_ready"], 1)
                route.end()

            def body(t, par, prev, cur, nxt):
                for p in range(pairs):
                    if cur:
                        if p >= 1:
                            weigh(t, p - 1)
                        gate(t, p)
                    if prev and p == 3:
                        finish(t - 1, 1 - par)
                    if nxt and p == 4:
                        norm(t + 1, 1 - par)
                    if nxt and p == 8:
                        center(t + 1)
                    if nxt and p == 10:
                        topk(t + 1, 1 - par)
                if cur:
                    weigh(t, pairs - 1)

            slots(v, n, body)



def l0_attention(nc, K, wq_d, wk_d, wv_d, seq, name):
    DQ = wq_d.shape[1]
    R = seq // P
    assert R == 2
    n = K.tiles // R
    W = P * (R * (R + 1) // 2)
    with ExitStack() as c:
        sb = lambda nm, s, dt=F32: c.enter_context(nc.sbuf_tensor(f"{nm}_{name}", s, dt))
        ps = lambda nm, s, dt=F32: c.enter_context(nc.psum_tensor(f"{nm}_{name}", s, dt))
        wq, wk, wv = sb("wq", [P, DQ]), sb("wk", [P, DQ]), sb("wv", [P, D])
        mask = sb("mask", [P, W])
        xn, xT = sb("xn", [P, R, D]), sb("xT", [P, seq])
        qk = sb("qk", [DQ, 2, seq])
        val = [sb(f"val{i}", [P, R, D]) for i in range(2)]
        sc, probs, probsT = sb("sc", [P, W]), sb("probs", [P, W]), sb("probsT", [P, W])
        nmax, sums, rinv = sb("nmax", [P, R]), sb("sums", [P, R]), sb("rinv", [P, R])
        px, pqk, pv = ps("px", [P, seq]), ps("pqk", [DQ, 2, seq]), ps("pv", [P, R, D])
        pS, pT, pO = ps("pS", [P, W]), ps("pT", [P, W]), ps("pO", [P, R, D])
        s = c.enter_context(semaphores(nc, name, (
            "w_loaded", "mask_zero", "mask_set", "wq_scaled", "xn_ready", "xn_turned", "xT_ready", "qkv_done", "qk_ready",
            "v_ready", "scores_done", "masked", "max_ready", "exp_done", "probs_turned", "probsT_ready",
            "out_done", "inv_ready", "x_written", "x_done", "turn")))
        block = c.enter_context(nc.Block())

        @block.sync
        def _(sp):
            sp.dma_start(wq[:], wq_d).then_inc(s["w_loaded"], 16)
            sp.dma_start(wk[:], wk_d).then_inc(s["w_loaded"], 16)
            sp.dma_start(wv[:], wv_d).then_inc(s["w_loaded"], 16)

        @block.gpsimd
        def _(pool):
            pool.memset(mask[:], 0.0).then_inc(s["mask_zero"], 1)
            pool.wait_ge(s["mask_zero"], 1)
            for col in (0, 2 * P):
                m = pool.affine_select(out=mask[:, col:col + P], in_=mask[:, col:col + P], compare_op=ALU.is_ge,
                                       fill=-BIG, base=0, pattern=[[-1, P]], channel_multiplier=1)
            m.then_inc(s["mask_set"], 1)

        @block.tensor
        def _(pe):
            def body(t, par, prev, cur, nxt):
                if cur:
                    pe.wait_ge(s["qk_ready"], t + 1)
                    after(pe, s["masked"], t)
                    pe.matmul(pS[:, 0:P], qk[:, 0, 0:P], qk[:, 1, 0:P], start=True, stop=True)
                    pe.matmul(pS[:, P:W], qk[:, 0, P:seq], qk[:, 1, :], start=True,
                              stop=True).then_inc(s["scores_done"], 1)
                if nxt:
                    pe.wait_ge(s["xn_ready"], t + 2)
                    for j in range(R):
                        m = pe.transpose(px[:, j * P:(j + 1) * P], xn[:, j, :], K.ident[:])
                    m.then_inc(s["xn_turned"], 1)
                    pe.wait_ge(s["xT_ready"], t + 2)
                    if isinstance(t, int) and t == -1:
                        pe.wait_ge(s["wq_scaled"], 1)
                    pe.matmul(pqk[:, 0, :], wq[:], xT[:], start=True, stop=True)
                    pe.matmul(pqk[:, 1, :], wk[:], xT[:], start=True, stop=True)
                    after(pe, s["v_ready"], t + 1)
                    for j in range(R):
                        m = pe.matmul(pv[:, j, :], xT[:, j * P:(j + 1) * P], wv[:], start=True, stop=True)
                    m.then_inc(s["qkv_done"], 1)
                if cur:
                    pe.wait_ge(s["exp_done"], t + 1)
                    for j in range(W // P):
                        m = pe.transpose(pT[:, j * P:(j + 1) * P], probs[:, j * P:(j + 1) * P], K.ident[:])
                    m.then_inc(s["probs_turned"], 1)
                    pe.wait_ge(s["probsT_ready"], t + 1)
                    pe.wait_ge(s["v_ready"], t + 1)
                    after(pe, s["x_written"], t)
                    pe.matmul(pO[:, 0, :], probsT[:, 0:P], val[par][:, 0, :], start=True, stop=True)
                    pe.matmul(pO[:, 1, :], probsT[:, P:2 * P], val[par][:, 0, :], start=True, stop=False)
                    pe.matmul(pO[:, 1, :], probsT[:, 2 * P:W], val[par][:, 1, :], start=False,
                              stop=True).then_inc(s["out_done"], 1)

            slots(pe, n, body)

        @block.scalar
        def _(act):
            def body(t, par, prev, cur, nxt):
                if cur:
                    act.wait_ge(s["max_ready"], t + 1)
                    act.activation(probs[:, 0:P], sc[:, 0:P], ACT.Exp, bias=nmax[:, 0:1], accum_out=sums[:, 0:1])
                    act.activation(probs[:, P:W], sc[:, P:W], ACT.Exp, bias=nmax[:, 1:2],
                                   accum_out=sums[:, 1:2]).then_inc(s["exp_done"], 1)
                if nxt:
                    act.wait_ge(s["xn_turned"], t + 2)
                    act.copy(xT[:], px[:]).then_inc(s["xT_ready"], 1)
                    act.wait_ge(s["qkv_done"], t + 2)
                    act.copy(qk[:], pqk[:]).then_inc(s["qk_ready"], 1)
                if cur:
                    act.wait_ge(s["probs_turned"], t + 1)
                    act.copy(probsT[:], pT[:]).then_inc(s["probsT_ready"], 1)

            slots(act, n, body)

        @block.vector
        def _(v):
            v.wait_ge(s["w_loaded"], 48)
            v.tensor_scalar(wq[:], wq[:], float(DQ) ** -0.5, None, ALU.mult).then_inc(s["wq_scaled"], 1)
            v.wait_ge(s["mask_set"], 1)

            def body(t, par, prev, cur, nxt):
                if nxt:
                    for j in range(R):
                        i = (t + 1) * R + j
                        m = v.tensor_scalar(xn[:, j, :], K.X[:, i, :], K.mean[:, i, :], K.rstd[:, i, :],
                                            ALU.subtract, ALU.mult)
                    m.then_inc(s["xn_ready"], 1)
                if cur:
                    v.wait_ge(s["scores_done"], t + 1)
                    v.tensor_tensor(sc[:], pS[:], mask[:], ALU.add).then_inc(s["masked"], 1)
                    v.wait_ge(s["masked"], t + 1)
                    v.tensor_reduce(nmax[:, 0:1], sc[:, 0:P], AX.X, ALU.max, negate=True)
                    v.tensor_reduce(nmax[:, 1:2], sc[:, P:W], AX.X, ALU.max, negate=True).then_inc(s["max_ready"], 1)
                if nxt:
                    v.wait_ge(s["qkv_done"], t + 2)
                    v.tensor_copy(val[1 - par][:], pv[:]).then_inc(s["v_ready"], 1)
                if cur:
                    v.wait_ge(s["exp_done"], t + 1)
                    v.reciprocal(rinv[:], sums[:]).then_inc(s["inv_ready"], 1)
                    v.wait_ge(s["inv_ready"], t + 1)
                    v.wait_ge(s["out_done"], t + 1)
                    for j in range(R):
                        m = v.scalar_tensor_tensor(K.X[:, t * R + j, :], pO[:, j, :], rinv[:, j:j + 1],
                                                   K.X[:, t * R + j, :], ALU.mult, ALU.add)
                    m.then_inc(s["x_written"], 1)
                    v.wait_ge(s["x_written"], t + 1)
                    v.sem_inc(s["turn"], 1)
                    for j in range(R):
                        m = v.bn_stats(K.stats[:, t * R + j, :], K.X[:, t * R + j, :])
                    m.then_inc(s["x_done"], 1)

            slots(v, n, body)



def rwkv(nc, K, T, seq, name):
    R = seq // P
    n = K.tiles // R
    CLAMP, KEPS = 60.0, 1e-8
    with ExitStack() as c:
        sb = lambda nm, s, dt=F32: c.enter_context(nc.sbuf_tensor(f"{nm}_{name}", s, dt))
        ps = lambda nm, s, dt=F32: c.enter_context(nc.psum_tensor(f"{nm}_{name}", s, dt))
        raw = sb("raw", [P, 4, P])
        wT = sb("wT", [P, 4, P])
        mix, omix = sb("mix", [P, 3]), sb("omix", [P, 3])
        tdec, first, decay = sb("tdec", [P, 1]), sb("first", [P, 1]), sb("decay", [P, 1])
        decays = sb("decays", [P, seq])
        xn = sb("xn", [P, R, D])
        xs = [sb(f"xs{i}", [P, seq + 1]) for i in range(2)]
        part, mixed = sb("part", [P, 3, seq]), sb("mixed", [P, 3, seq])
        kmin, kc, kv, th = sb("kmin", [P, seq]), sb("kc", [P, seq]), sb("kv", [P, seq]), sb("th", [P, seq])
        sk, skv = sb("sk", [P, seq + 1]), sb("skv", [P, seq + 1])
        den, num, inv, o = sb("den", [P, seq]), sb("num", [P, seq]), sb("inv", [P, seq]), sb("o", [P, seq])
        px, pkv, pr, pO, pw = ps("px", [P, seq]), ps("pkv", [P, 2, seq]), ps("pr", [P, seq]), ps("pO", [P, R, D]), ps("pw", [P, 4, P])
        s = c.enter_context(semaphores(nc, name, (
            "loaded", "w_turned", "w_ready", "setup", "set_chain", "xn_ready", "xn_turned", "xs_ready", "parts", "mixed_ready",
            "proj_done", "kmin_ready", "kc_ready", "th_ready", "chain", "o_ready", "out_done", "x_written", "x_done", "turn")))
        block = c.enter_context(nc.Block())

        @block.sync
        def _(sp):
            for i, w in enumerate(("Wk", "Wv", "Wr", "Wo")):
                sp.dma_start(raw[:, i, :], T[f"L1_attn_{w}"]).then_inc(s["loaded"], 16)
            for i, w in enumerate(("k", "v", "r")):
                sp.dma_start(mix[:, i:i + 1], T[f"L1_attn_time_mix_{w}"].rearrange("a b c -> c (a b)")).then_inc(s["loaded"], 16)
            sp.dma_start(tdec[:], T["L1_attn_time_decay"]).then_inc(s["loaded"], 16)
            sp.dma_start(first[:], T["L1_attn_time_first"]).then_inc(s["loaded"], 16)

        LOADS = 16 * 9

        @block.tensor
        def _(pe):
            pe.wait_ge(s["loaded"], LOADS)
            for i in range(4):
                m = pe.transpose(pw[:, i, :], raw[:, i, :], K.ident[:])
            m.then_inc(s["w_turned"], 1)

            def body(t, par, prev, cur, nxt):
                if nxt:
                    pe.wait_ge(s["xn_ready"], t + 2)
                    after(pe, s["xs_ready"], t + 1)
                    for j in range(R):
                        m = pe.transpose(px[:, j * P:(j + 1) * P], xn[:, j, :], K.ident[:])
                    m.then_inc(s["xn_turned"], 1)
                if cur:
                    if isinstance(t, int) and t == 0:
                        pe.wait_ge(s["w_ready"], 1)
                    pe.wait_ge(s["mixed_ready"], t + 1)
                    for i in range(2):
                        pe.matmul(pkv[:, i, :], wT[:, i, :], mixed[:, i, :], start=True, stop=True)
                    pe.matmul(pr[:], wT[:, 2, :], mixed[:, 2, :], start=True, stop=True).then_inc(s["proj_done"], 1)
                    pe.wait_ge(s["o_ready"], t + 1)
                    for j in range(R):
                        m = pe.matmul(pO[:, j, :], o[:, j * P:(j + 1) * P], wT[:, 3, :], start=True, stop=True)
                    m.then_inc(s["out_done"], 1)

            slots(pe, n, body)

        @block.scalar
        def _(act):
            act.wait_ge(s["loaded"], LOADS)
            act.activation(tdec[:], tdec[:], ACT.Exp).then_inc(s["set_chain"], 1)
            act.wait_ge(s["set_chain"], 1)
            act.activation(decay[:], tdec[:], ACT.Exp, scale=-1.0)
            act.activation(first[:], first[:], ACT.Exp).then_inc(s["setup"], 1)
            act.wait_ge(s["w_turned"], 1)
            act.copy(wT[:], pw[:]).then_inc(s["w_ready"], 1)

            def body(t, par, prev, cur, nxt):
                if nxt:
                    act.wait_ge(s["xn_turned"], t + 2)
                    after(act, s["mixed_ready"], t)
                    act.copy(xs[1 - par][:, 1:seq + 1], px[:]).then_inc(s["xs_ready"], 1)
                if cur:
                    act.wait_ge(s["proj_done"], t + 1)
                    after(act, s["o_ready"], t)
                    act.activation(th[:], pr[:], ACT.Tanh, scale=0.5).then_inc(s["th_ready"], 1)
                    act.wait_ge(s["kmin_ready"], t + 1)
                    act.activation(kc[:], kmin[:], ACT.Exp).then_inc(s["kc_ready"], 1)

            slots(act, n, body)

        @block.vector
        def _(v):
            for i in range(2):
                v.memset(xs[i][:, 0:1], 0.0)
            v.memset(sk[:, 0:1], 0.0)
            v.memset(skv[:, 0:1], 0.0)
            v.wait_ge(s["loaded"], LOADS)
            v.tensor_scalar(omix[:], mix[:], -1.0, 1.0, ALU.mult, ALU.add)
            v.wait_ge(s["setup"], 1)
            v.tensor_copy(decays[:], decay[:].to_broadcast([P, seq])).then_inc(s["set_chain"], 1)
            v.wait_ge(s["set_chain"], 2)
            ch = Chain(v, s["chain"], 5, s["turn"])

            def body(t, par, prev, cur, nxt):
                if nxt:
                    after(v, s["xn_turned"], t + 1)
                    for j in range(R):
                        i = (t + 1) * R + j
                        m = v.tensor_scalar(xn[:, j, :], K.X[:, i, :], K.mean[:, i, :], K.rstd[:, i, :],
                                            ALU.subtract, ALU.mult)
                    m.then_inc(s["xn_ready"], 1)
                if not cur:
                    return
                v.wait_ge(s["xs_ready"], t + 1)
                for i in range(3):
                    m = v.tensor_scalar(part[:, i, :], xs[par][:, 1:seq + 1], mix[:, i:i + 1], None, ALU.mult)
                m.then_inc(s["parts"], 1)
                v.wait_ge(s["parts"], t + 1)
                for i in range(3):
                    m = v.scalar_tensor_tensor(mixed[:, i, :], xs[par][:, 0:seq], omix[:, i:i + 1], part[:, i, :],
                                               ALU.mult, ALU.add)
                m.then_inc(s["mixed_ready"], 1)
                v.wait_ge(s["proj_done"], t + 1)
                v.tensor_scalar(kmin[:], pkv[:, 0, :], CLAMP, None, ALU.min).then_inc(s["kmin_ready"], 1)
                v.wait_ge(s["kc_ready"], t + 1)
                v.tensor_tensor_scan(sk[:, 1:seq + 1], decays[:], kc[:], 0.0, ALU.mult, ALU.add)
                ch.begin(t)
                ch.step(v.tensor_tensor(kv[:], kc[:], pkv[:, 1, :], ALU.mult))
                v.scalar_tensor_tensor(den[:], kc[:], first[:], sk[:, 0:seq], ALU.mult, ALU.add)
                ch.step(v.tensor_tensor_scan(skv[:, 1:seq + 1], decays[:], kv[:], 0.0, ALU.mult, ALU.add))
                v.tensor_scalar(den[:], den[:], KEPS, None, ALU.add)
                ch.step(v.scalar_tensor_tensor(num[:], kv[:], first[:], skv[:, 0:seq], ALU.mult, ALU.add))
                v.wait_ge(s["th_ready"], t + 1)
                v.scalar_tensor_tensor(num[:], th[:], 1.0, num[:], ALU.add, ALU.mult)
                ch.step(v.reciprocal(inv[:], den[:]))
                v.scalar_tensor_tensor(o[:], num[:], 0.5, inv[:], ALU.mult, ALU.mult).then_inc(s["o_ready"], 1)
                v.wait_ge(s["out_done"], t + 1)
                ch.step_apart(v.tensor_tensor(K.X[:, bass.ds(t * R, R), :], pO[:], K.X[:, bass.ds(t * R, R), :], ALU.add))
                for j in range(R):
                    m = v.bn_stats(K.stats[:, t * R + j, :], K.X[:, t * R + j, :])
                m.then_inc(s["x_done"], 1)
                ch.end()

            slots(v, n, body)



HEADS_A_GROUP = 4
ROWS = P // HEADS_A_GROUP


def l1_ffn(nc, K, T, seq, name):
    with ExitStack() as c:
        Y = c.enter_context(nc.sbuf_tensor(f"Y_{name}", [P, K.tiles, D], F32))
        l1_attention(nc, K, Y, T, seq, name + "a")
        norm_phase(nc, K, name + "n")
        l1_experts(nc, K, Y, T, name + "e")


def l1_attention(nc, K, Y, T, seq, name):
    H, HD = T["L1_ffn_scale_w"].shape
    R = seq // P
    assert R == 2 and H * HD == D and 3 * HD < ROWS
    n = K.tiles // R
    NG = H // HEADS_A_GROUP
    HG = HEADS_A_GROUP
    MAXROW = 3 * HD
    SM = float(HD) ** -0.5
    LAG = 4
    with ExitStack() as c:
        sb = lambda nm, s, dt=F32: c.enter_context(nc.sbuf_tensor(f"{nm}_{name}", s, dt))
        ps = lambda nm, s, dt=F32: c.enter_context(nc.psum_tensor(f"{nm}_{name}", s, dt))
        raw = sb("raw", [P, 2, D])
        wq, wk, wz = sb("wq", [P, H, ROWS]), sb("wk", [P, H, ROWS]), sb("wz", [P, H, ROWS])
        wv, wo, wgate, gb = sb("wv", [P, D]), sb("wo", [P, D]), sb("wgate", [P, D]), sb("gb", [P, 1])
        sw, swq, swsum = sb("sw", [P, H, HD]), sb("swq", [P, H, HD]), sb("swsum", [P, H])
        rows = sb("rows", [P, ROWS])
        qlow, klow, one = sb("qlow", [P, 1]), sb("klow", [P, 1]), sb("one", [P, 1])
        xn, xT = sb("xn", [P, R, D]), sb("xT", [P, seq])
        th, qs = sb("th", [P, NG, seq]), sb("qs", [P, NG, seq])
        qr, kr = sb("qr", [P, NG, seq], F32R), sb("kr", [P, NG, seq], F32R)
        qa = sb("qa", [P, NG, seq], F32R)
        kw = sb("kw", [P, NG, seq], F32R)
        qb = [sb(f"qb{i}", [P, NG, seq], F32R) for i in range(2)]
        keysD = [sb(f"keysD{i}", [P, NG, HG, seq], F32R) for i in range(2)]
        va = [sb(f"va{i}", [P, R, H, ROWS]) for i in range(2)]
        nmax, mx = sb("nmax", [P, NG, R, HG]), sb("mx", [P, R, H, ROWS])
        probs = [sb(f"probs{i}", [P, R, seq]) for i in range(2)]
        av = sb("av", [P, NG, seq])
        rden, on, onT = sb("rden", [P, R, H]), sb("on", [P, R, D]), sb("onT", [P, seq])
        tg, og = sb("tg", [P, seq]), sb("og", [P, seq])
        p1 = ps("p1", [P, 2, 512])
        p2 = [ps(f"p2{i}", [P, R, seq]) for i in range(2)]
        pav = ps("pav", [P, NG, seq])
        pm = ps("pm", [P, NG, seq])
        s = c.enter_context(semaphores(nc, name, (
            "loaded", "set_chain", "pool_chain", "w_set", "zeros_set", "xn_ready", "xn_turned", "xT_ready", "z_done",
            "th_ready", "q_done", "qs_ready", "qr_ready", "qa_ready", "k_done", "kr_ready", "kw_ready", "keys_ready",
            "v_done", "v_ready", "smax_done", "nmax_done", "mx_ready", "mx_turned", "qb_ready",
            "scores_done", "exp_done", "av_done", "av_ready", "av_turned", "rden_ready", "on_ready", "on_turned",
            "onT_ready", "gate_done", "tg_ready", "og_ready", "attn_done", "y_written", "y_done", "turn", "pturn")))
        block = c.enter_context(nc.Block())
        LOADS = 16 * 7

        @block.sync
        def _(sp):
            sp.dma_start(raw[:, 0, :], T["L1_ffn_q_w"]).then_inc(s["loaded"], 16)
            sp.dma_start(raw[:, 1, :], T["L1_ffn_k_w"]).then_inc(s["loaded"], 16)
            sp.dma_start(wv[:], T["L1_ffn_v_w"]).then_inc(s["loaded"], 16)
            sp.dma_start(wo[:], T["L1_ffn_out_w"]).then_inc(s["loaded"], 16)
            sp.dma_start(wgate[:], T["L1_ffn_gate_w"]).then_inc(s["loaded"], 16)
            sp.dma_start(gb[:], T["L1_ffn_gate_b"].rearrange("(d a) -> d a", a=1)).then_inc(s["loaded"], 16)
            sp.dma_start(sw[:], T["L1_ffn_scale_w"].rearrange("(a h) d -> a h d", a=1).to_broadcast([P, H, HD])).then_inc(s["loaded"], 16)

        @block.gpsimd
        def _(pool):
            pool.memset(rows[:], 0.0)
            for k in range(2):
                pool.memset(keysD[k][:].bitcast(F32), 0.0)
                pool.memset(va[k][:], 0.0)
            pool.memset(mx[:], 0.0).then_inc(s["pool_chain"], 1)
            for h in range(HG):
                pool.wait_ge(s["pool_chain"], h + 1)
                pool.affine_select(out=rows[:], in_=rows[:], compare_op=ALU.not_equal, fill=1.0, base=-ROWS * h,
                                   pattern=[[-1, ROWS]], channel_multiplier=1).then_inc(s["pool_chain"], 1)

            def body(t, par, prev, cur, nxt):
                if nxt:
                    pool.wait_ge(s["kw_ready"], t + 2)
                    after(pool, s["exp_done"], t * H)
                    pool.sem_inc(s["pturn"], 1)
                    for i in range(HG):
                        m = pool.tensor_copy(keysD[1 - par][ROWS * i:ROWS * (i + 1), :, i, :],
                                             kw[ROWS * i:ROWS * (i + 1), :, :])
                    m.then_inc(s["keys_ready"], 1)

            slots(pool, n, body)

        @block.tensor
        def _(pe):
            def project(dst, w):
                for g in range(NG):
                    m = pe.matmul(dst[:, g, :], w[:, g * HG:(g + 1) * HG, :], xT[:], start=True, stop=True)
                return m

            def form_max(t, par, u):
                g, pair, r = u // 4, u // 2 % 2, u % 2
                if u == 0:
                    pe.wait_ge(s["qa_ready"], t + 1)
                    pe.wait_ge(s["keys_ready"], t + 1)
                after(pe, s["nmax_done"], t * 16 + u - 1)
                pe.matmul(p1[:, u % 2, :], qa[:, g, r * P:(r + 1) * P], keysD[par][:, g, 2 * pair:2 * pair + 2, :],
                          start=True, stop=True).then_inc(s["smax_done"], 1)

            def turn_max(t, g):
                pe.wait_ge(s["mx_ready"], t * NG + g + 1)
                if g == 0:
                    pe.wait_ge(s["kr_ready"], t + 1)
                    pe.wait_ge(s["kw_ready"], t + 1)
                    pe.wait_ge(s["v_ready"], t + 1)
                if g % 2:
                    pe.wait_ge(s["qb_ready"], t * NG + g)
                for r in range(R):
                    m = pe.transpose(pm[:, g, r * P:(r + 1) * P], mx[:, r, g * HG:(g + 1) * HG, :], K.ident[:])
                m.then_inc(s["mx_turned"], 1)

            def scores(t, par, h):
                g, i, k = h // HG, h % HG, t * H + h
                if i == 0:
                    pe.wait_ge(s["qb_ready"], t * NG + g + 1)
                after(pe, s["exp_done"], k - 1)
                for kt in range(R):
                    m = pe.matmul(p2[h % 2][:, kt, :], keysD[par][:, g, i, kt * P:(kt + 1) * P], qb[par][:, g, :],
                                  start=True, stop=True)
                m.then_inc(s["scores_done"], 1)

            def weigh(t, par, h):
                g, i, k = h // HG, h % HG, t * H + h
                pe.wait_ge(s["exp_done"], k + 1)
                if h == 0:
                    after(pe, s["av_ready"], t)
                for kt in range(R):
                    m = pe.matmul(pav[ROWS * i:ROWS * (i + 1), g, :], va[par][:, kt, h, :], probs[h % 2][:, kt, :],
                                  start=(kt == 0), stop=(kt == R - 1))
                m.then_inc(s["av_done"], 1)

            def body(t, par, prev, cur, nxt):
                unit, turned = 0, 0
                for h in range(H):
                    if prev and h == 0:
                        pe.wait_ge(s["av_ready"], t)
                        after(pe, s["nmax_done"], 16 * t + 16 if cur else 16 * t)
                        after(pe, s["y_written"], t - 1)
                        for g in range(NG):
                            for r in range(R):
                                m = pe.transpose(p1[:, r, g * P:(g + 1) * P], av[:, g, r * P:(r + 1) * P], K.ident[:])
                        m.then_inc(s["av_turned"], 1)
                    if nxt and h == 0:
                        pe.wait_ge(s["xn_ready"], t + 2)
                        after(pe, s["qb_ready"], NG * (t + 1))
                        for r in range(R):
                            m = pe.transpose(pm[:, 0, r * P:(r + 1) * P], xn[:, r, :], K.ident[:])
                        m.then_inc(s["xn_turned"], 1)
                    if cur:
                        scores(t, par, h)
                        if h >= 1:
                            weigh(t, par, h - 1)
                    if nxt and h == 0:
                        pe.wait_ge(s["xT_ready"], t + 2)
                        project(pm, wz).then_inc(s["z_done"], 1)
                    if prev and h == 1:
                        pe.wait_ge(s["on_ready"], t)
                        for r in range(R):
                            m = pe.transpose(p1[:, 0, r * P:(r + 1) * P], on[:, r, :], K.ident[:])
                        m.then_inc(s["on_turned"], 1)
                    if nxt and h == 1:
                        pe.wait_ge(s["th_ready"], t + 2)
                        project(pm, wq).then_inc(s["q_done"], 1)
                    if prev and h == 2:
                        pe.wait_ge(s["onT_ready"], t)
                        pe.matmul(p1[:, 1, 0:seq], wgate[:], onT[:], start=True, stop=True).then_inc(s["gate_done"], 1)
                    if nxt and h == 2:
                        pe.wait_ge(s["qs_ready"], t + 2)
                        project(pm, wk).then_inc(s["k_done"], 1)
                    if prev and h == 3:
                        pe.wait_ge(s["og_ready"], t)
                        for r in range(R):
                            m = pe.matmul(p1[:, 0, r * P:(r + 1) * P], og[:, r * P:(r + 1) * P], wo[:], start=True, stop=True)
                        m.then_inc(s["attn_done"], 1)
                    if nxt and h == 3:
                        pe.wait_ge(s["kw_ready"], t + 2)
                        for r in range(R):
                            m = pe.matmul(pm[:, 0, r * P:(r + 1) * P], xT[:, r * P:(r + 1) * P], wv[:], start=True, stop=True)
                        m.then_inc(s["v_done"], 1)
                    if nxt and h >= LAG:
                        if h == LAG and prev:
                            pe.wait_ge(s["y_written"], t)
                        while unit < 16 and unit < -(-(h - LAG + 1) * 16 // (H - LAG)):
                            form_max(t + 1, 1 - par, unit)
                            unit += 1
                            if unit >= 6 and (unit - 6) % 4 == 0:
                                turn_max(t + 1, turned)
                                turned += 1
                if nxt:
                    turn_max(t + 1, NG - 1)
                if cur:
                    weigh(t, par, H - 1)

            pe.wait_ge(s["loaded"], LOADS)
            pe.wait_ge(s["w_set"], 1)
            slots(pe, n, body)

        @block.scalar
        def _(act):
            act.wait_ge(s["w_set"], 1)

            def body(t, par, prev, cur, nxt):
                for h in range(H):
                    if prev and h == 0:
                        act.wait_ge(s["av_done"], t * H)
                        after(act, s["av_turned"], t - 1)
                        act.copy(av[:], pav[:]).then_inc(s["av_ready"], 1)
                    if nxt and h == 0:
                        act.wait_ge(s["xn_turned"], t + 2)
                        after(act, s["v_done"], t + 1)
                        act.copy(xT[:], pm[:, 0, :]).then_inc(s["xT_ready"], 1)
                    if cur:
                        k = t * H + h
                        act.wait_ge(s["scores_done"], k + 1)
                        after(act, s["av_done"], k - 1)
                        act.activation(probs[h % 2][:], p2[h % 2][:], ACT.Exp, scale=SM).then_inc(s["exp_done"], 1)
                    if nxt and h == 0:
                        act.wait_ge(s["z_done"], t + 2)
                        act.activation(th[:], pm[:], ACT.Tanh, scale=0.5).then_inc(s["th_ready"], 1)
                    if prev and h == 1:
                        act.wait_ge(s["on_turned"], t)
                        act.copy(onT[:], p1[:, 0, 0:seq]).then_inc(s["onT_ready"], 1)
                    if nxt and h == 1:
                        act.wait_ge(s["qs_ready"], t + 2)
                        act.copy(qr[:], qs[:]).then_inc(s["qr_ready"], 1)
                    if prev and h == 2:
                        act.wait_ge(s["gate_done"], t)
                        act.activation(tg[:], p1[:, 1, 0:seq], ACT.Tanh, bias=gb[:], scale=0.5).then_inc(s["tg_ready"], 1)
                    if nxt and h == 2:
                        act.wait_ge(s["k_done"], t + 2)
                        act.activation(kr[:], pm[:], ACT.Identity, bias=one[:]).then_inc(s["kr_ready"], 1)

            slots(act, n, body)

        @block.vector
        def _(v):
            setup = Chain(v, s["set_chain"], 2)
            setup.begin(0)
            v.wait_ge(s["loaded"], LOADS)
            v.wait_ge(s["pool_chain"], HG + 1)
            v.memset(wq[:], 0.0)
            v.memset(wk[:], 0.0)
            v.memset(wz[:], 0.0)
            for i in range(2):
                v.memset(va[i][:, :, :, HD:HD + 1], 1.0)
            v.tensor_scalar(wo[:], wo[:], 0.5, None, ALU.mult)
            v.tensor_scalar(gb[:], gb[:], 0.5, None, ALU.mult)
            v.tensor_reduce(qlow[:], rows[:, HD:2 * HD], AX.X, ALU.add, negate=True)
            v.tensor_reduce(klow[:], rows[:, 2 * HD:3 * HD], AX.X, ALU.add, negate=True)
            v.tensor_copy(one[:], rows[:, MAXROW:MAXROW + 1])
            setup.step(v.tensor_tensor(swq[:], sw[:], raw[:, 0, :].rearrange("p (h d) -> p h d", h=H), ALU.mult))
            v.tensor_tensor(klow[:], klow[:], one[:], ALU.add)
            setup.step(v.tensor_reduce(swsum[:], swq[:], AX.X, ALU.add))
            for r in range(3):
                v.tensor_copy(wq[:, :, r * HD:(r + 1) * HD], raw[:, 0, :].rearrange("p (h d) -> p h d", h=H))
                v.tensor_copy(wk[:, :, r * HD:(r + 1) * HD], raw[:, 1, :].rearrange("p (h d) -> p h d", h=H))
                m = v.tensor_copy(wz[:, :, r * HD:(r + 1) * HD], swsum[:, :, None].to_broadcast([P, H, HD]))
            m.then_inc(s["w_set"], 1)

            def body(t, par, prev, cur, nxt):
                if prev:
                    pv = p1[:].rearrange("p r (h w) -> p r h w", h=H)
                    v.wait_ge(s["av_turned"], t)
                    v.reciprocal(rden[:], pv[:, :, :, HD]).then_inc(s["rden_ready"], 1)
                    v.wait_ge(s["rden_ready"], t)
                    for r in range(R):
                        m = v.tensor_tensor(on[:, r, :].rearrange("p (h d) -> p h d", h=H), pv[:, r, :, 0:HD],
                                            rden[:, r, :, None].to_broadcast([P, H, HD]), ALU.mult)
                    m.then_inc(s["on_ready"], 1)
                if nxt:
                    after(v, s["xn_turned"], t + 1)
                    for r in range(R):
                        i = (t + 1) * R + r
                        for dst in (Y[:, i, :], xn[:, r, :]):
                            m = v.tensor_scalar(dst, K.X[:, i, :], K.mean[:, i, :], K.rstd[:, i, :],
                                                ALU.subtract, ALU.mult)
                    m.then_inc(s["xn_ready"], 1)
                    v.wait_ge(s["q_done"], t + 2)
                    for b in range(2):
                        m = v.scalar_tensor_tensor(qs[:, 2 * b:2 * b + 2, :], th[:, 2 * b:2 * b + 2, :], 1.0,
                                                   pm[:, 2 * b:2 * b + 2, :], ALU.add, ALU.mult)
                    m.then_inc(s["qs_ready"], 1)
                if prev:
                    v.wait_ge(s["tg_ready"], t)
                    v.scalar_tensor_tensor(og[:], tg[:], 1.0, onT[:], ALU.add, ALU.mult).then_inc(s["og_ready"], 1)
                if nxt:
                    v.wait_ge(s["qr_ready"], t + 2)
                    for b in range(2):
                        m = v.scalar_tensor_tensor(qa[:, 2 * b:2 * b + 2, :], qr[:, 2 * b:2 * b + 2, :].bitcast(F32), qlow[:],
                                                   qs[:, 2 * b:2 * b + 2, :], ALU.mult, ALU.add)
                    m.then_inc(s["qa_ready"], 1)
                    v.wait_ge(s["kr_ready"], t + 2)
                    after(v, s["keys_ready"], t + 1)
                    for b in range(2):
                        m = v.scalar_tensor_tensor(kw[:, 2 * b:2 * b + 2, :], kr[:, 2 * b:2 * b + 2, :].bitcast(F32), klow[:],
                                                   pm[:, 2 * b:2 * b + 2, :], ALU.mult, ALU.add)
                    m.then_inc(s["kw_ready"], 1)
                    v.wait_ge(s["v_done"], t + 2)
                    v.tensor_copy(va[1 - par][:, :, :, 0:HD],
                                  pm[:, 0, :].rearrange("p (r h d) -> p r h d", r=R, h=H)).then_inc(s["v_ready"], 1)
                if prev:
                    v.wait_ge(s["attn_done"], t)
                    v.tensor_tensor(Y[:, bass.ds((t - 1) * R, R), :], p1[:, 0, 0:seq].rearrange("p (r d) -> p r d", r=R),
                                    Y[:, bass.ds((t - 1) * R, R), :], ALU.add).then_inc(s["y_written"], 1)
                    v.wait_ge(s["y_written"], t)
                    v.sem_inc(s["turn"], 1)
                    for r in range(R):
                        m = v.bn_stats(K.stats[:, (t - 1) * R + r, :], Y[:, (t - 1) * R + r, :])
                    m.then_inc(s["y_done"], 1)
                if nxt:
                    for u in range(16):
                        g, pair, r = u // 4, u // 2 % 2, u % 2
                        v.wait_ge(s["smax_done"], (t + 1) * 16 + u + 1)
                        v.tensor_reduce(nmax[:, g, r, 2 * pair:2 * pair + 2],
                                        p1[:, u % 2, :].rearrange("p (h k) -> p h k", h=2), AX.X, ALU.max,
                                        negate=True).then_inc(s["nmax_done"], 1)
                        if u % 4 == 3:
                            v.wait_ge(s["nmax_done"], (t + 1) * 16 + u + 1)
                            v.tensor_copy(mx[:, :, g * HG:(g + 1) * HG, MAXROW], nmax[:, g, :, :]).then_inc(s["mx_ready"], 1)
                        if u >= 6 and (u - 6) % 4 == 1:
                            fill((t + 1), 1 - par, (u - 6) // 4)
                    fill((t + 1), 1 - par, NG - 1)

            def fill(t, par, g):
                v.wait_ge(s["mx_turned"], t * NG + g + 1)
                v.tensor_tensor(qb[par][:, g, :], pm[:, g, :], qa[:, g, :].bitcast(F32), ALU.add).then_inc(s["qb_ready"], 1)

            slots(v, n, body)


def l1_experts(nc, K, Y, T, name):
    E, _, F = T["L1_ffn_w1"].shape
    G = 4
    N = G * P
    n = K.tiles // G
    FC = F // P
    TABS = 3 * F + D + 1
    PAD = 6
    EC = 512 // F
    with ExitStack() as c:
        sb = lambda nm, s, dt=F32: c.enter_context(nc.sbuf_tensor(f"{nm}_{name}", s, dt))
        ps = lambda nm, s, dt=F32: c.enter_context(nc.psum_tensor(f"{nm}_{name}", s, dt))
        w1, w2 = sb("w1", [P, E, F]), sb("w2", [P, FC, E, D])
        wr, br = sb("wr", [P, E]), sb("br", [P, E])
        tabf = sb("tabf", [96, TABS])
        tab3 = sb("tab3", [96, TABS], BF16)
        n1g, n1b, n2g, n2b = (sb(k, [P, D]) for k in ("n1g", "n1b", "n2g", "n2b"))
        iota = sb("iota", [P, E])
        x1 = [sb(f"x1{i}", [P, G, D]) for i in range(2)]
        x1T = [sb(f"x1T{i}", [P, N]) for i in range(2)]
        logit, struck = sb("logit", [P, G, E + PAD]), sb("struck", [P, G, E + PAD])
        top8, index, chosen = sb("top8", [P, G, 8]), sb("index", [P, G, E]), sb("chosen", [P, G])
        dv, ev, den, wsum = sb("dv", [P, G]), sb("ev", [P, G]), sb("den", [P, G]), [sb(f"wsum{i}", [P, G]) for i in range(2)]
        hot = [sb(f"hot{i}", [P, G, E]) for i in range(2)]
        hot3 = sb("hot3", [P, G, 96], BF16)
        hotT = [sb(f"hotT{i}", [96, N], BF16) for i in range(2)]
        tab = [sb(f"tab{i}", [P, G, TABS]) for i in range(2)]
        h = sb("h", [P, G, F])
        hodd = [sb(f"hodd{i}", [P, F]) for i in range(2)]
        gl = sb("gl", [P, G, F])
        glT = sb("glT", [P, FC, N])
        st, mean, var, rstd, tt = sb("st", [P, G, 6]), sb("mean", [P, G, 1]), sb("var", [P, G, 1]), sb("rstd", [P, G, 1]), sb("tt", [P, G, 1])
        y, yodd = sb("y", [P, G, D]), [sb(f"yodd{i}", [P, D]) for i in range(2)]
        ph = [ps(f"ph{i}", [P, EC, F]) for i in range(2)]
        pt = ps("pt", [P, 2, 512])
        py = ps("py", [P, 2, 4, D])
        pm = ps("pm", [P, N])
        pmb = pm[:].bitcast(BF16)
        s = c.enter_context(semaphores(nc, name, (
            "loaded", "pool_chain", "set_chain", "w_set", "x1_ready", "x1_turned", "x1T_ready", "logits_done", "dv_ready",
            "ev_ready", "hot_ready", "hot_turned", "hotT_ready", "tab_done", "tab_ready", "h_done", "h_read", "h_chain",
            "h_ready", "gl_ready", "gl_turned", "glT_ready", "y_done", "y_read", "y_chain", "norm_chain", "route_chain",
            "fin_chain", "x_done", "turn", "hsum", "ysum", "pre_chain")))
        block = c.enter_context(nc.Block())
        tabs_d = [("L1_ffn_b1", 0, F), ("L1_ffn_ln_g", F, F), ("L1_ffn_ln_b", 2 * F, F), ("L1_ffn_b2", 3 * F, D)]
        LOADS = 16 * (4 + 3 * 5 + 5)

        @block.sync
        def _(sp):
            sp.dma_start(w1[:], T["L1_ffn_w1"].rearrange("e d f -> d e f")).then_inc(s["loaded"], 16)
            sp.dma_start(wr[:], T["L1_ffn_moe_gate_w"]).then_inc(s["loaded"], 16)
            sp.dma_start(w2[:, 0, :, :], T["L1_ffn_w2"][:, 0:P, :].rearrange("e f d -> f e d")).then_inc(s["loaded"], 16)
            for dst, k in ((br, "moe_gate_b"), (n1g, "n1_g"), (n1b, "n1_b"), (n2g, "n2_g"), (n2b, "n2_b")):
                sp.dma_start(dst[:], T[f"L1_ffn_{k}"].rearrange("(a d) -> a d", a=1).to_broadcast([P, dst.shape[1]])).then_inc(s["loaded"], 16)

        @block.gpsimd
        def _(pool):
            pool.memset(tabf[:], 0.0).then_inc(s["pool_chain"], 1)
            pool.memset(hot3[:], 0.0)
            pool.iota(iota[:], pattern=[[1, E]], base=0, channel_multiplier=0, allow_small_or_imprecise_dtypes=True).then_inc(s["pool_chain"], 1)

        @block.tensor
        def _(pe):
            pe.wait_ge(s["w_set"], 1)

            def first(t, par, j):
                after(pe, s["tab_ready"], t * G + j)
                if j == 0:
                    pe.wait_ge(s["hotT_ready"], t + 1)
                pe.matmul(pt[:, 0, :], hotT[par][:, j * P:(j + 1) * P], tab3[:, 0:512], start=True, stop=True)
                pe.matmul(pt[:, 1, 0:TABS - 512], hotT[par][:, j * P:(j + 1) * P], tab3[:, 512:TABS], start=True,
                          stop=True).then_inc(s["tab_done"], 1)
                for b in range(E // EC):
                    k = (t * G + j) * (E // EC) + b
                    after(pe, s["h_read"], k - 1)
                    pe.matmul(ph[b % 2][:], x1T[par][:, j * P:(j + 1) * P], w1[:, EC * b:EC * (b + 1), :], start=True,
                              stop=True).then_inc(s["h_done"], 1)

            def second(t, j):
                for b in range(2):
                    k = (t * G + j) * 2 + b
                    after(pe, s["y_read"], k - 1)
                    for k2 in range(FC):
                        m = pe.matmul(py[:, b, :, :], glT[:, k2, j * P:(j + 1) * P], w2[:, k2, 4 * b:4 * b + 4, :],
                                      start=(k2 == 0), stop=(k2 == FC - 1))
                    m.then_inc(s["y_done"], 1)

            def body(t, par, prev, cur, nxt):
                for j in range(G):
                    if cur:
                        first(t, par, j)
                    if prev and j == 0:
                        pe.wait_ge(s["gl_ready"], t)
                        after(pe, s["y_read"], (t - 1) * G * 2)
                        for k2 in range(FC):
                            for q in range(G):
                                m = pe.transpose(py[:, k2, q, :], gl[:, q, k2 * P:(k2 + 1) * P], K.ident[:])
                        m.then_inc(s["gl_turned"], 1)
                        pe.wait_ge(s["glT_ready"], t)
                    if prev and j < 2:
                        second(t - 1, 2 * j)
                        second(t - 1, 2 * j + 1)
                    if nxt and j == 2:
                        pe.wait_ge(s["x1_ready"], t + 2)
                        after(pe, s["hotT_ready"], t + 1)
                        for q in range(G):
                            m = pe.transpose(pm[:, q * P:(q + 1) * P], x1[1 - par][:, q, :], K.ident[:])
                        m.then_inc(s["x1_turned"], 1)
                if nxt:
                    pe.wait_ge(s["x1T_ready"], t + 2)
                    for q in range(G):
                        m = pe.matmul(pm[:, q * E:(q + 1) * E], x1T[1 - par][:, q * P:(q + 1) * P], wr[:], start=True, stop=True)
                    m.then_inc(s["logits_done"], 1)
                    pe.wait_ge(s["hot_ready"], t + 2)
                    for q in range(G):
                        m = pe.transpose(pmb[0:96, q * P:(q + 1) * P], hot3[:, q, :], K.identb[:])
                    m.then_inc(s["hot_turned"], 1)

            slots(pe, n, body)

        @block.scalar
        def _(act):
            act.dma_start(w2[:, 1, :, :], T["L1_ffn_w2"][:, P:2 * P, :].rearrange("e f d -> f e d")).then_inc(s["loaded"], 16)
            act.wait_ge(s["pool_chain"], 2)
            for q in range(3):
                for k, o, w in tabs_d:
                    act.dma_start(tabf[32 * q:32 * q + E, o:o + w], T[k]).then_inc(s["loaded"], 16)
                act.dma_start(tabf[32 * q:32 * q + E, TABS - 1:TABS], T["L1_ffn_res_scale"].rearrange("(e a) -> e a", a=1)).then_inc(s["loaded"], 16)

            def body(t, par, prev, cur, nxt):
                for j in range(G):
                    if cur:
                        act.wait_ge(s["tab_done"], t * G + j + 1)
                        act.copy(tab[par][:, j, 0:512], pt[:, 0, :])
                        act.copy(tab[par][:, j, 512:TABS], pt[:, 1, 0:TABS - 512]).then_inc(s["tab_ready"], 1)
                    if prev and j == 0:
                        act.wait_ge(s["gl_turned"], t)
                        after(act, s["y_done"], (t - 1) * G * 2)
                        act.copy(glT[:], py[:].rearrange("p c q d -> p c (q d)")).then_inc(s["glT_ready"], 1)
                    if nxt and j == 2:
                        act.wait_ge(s["x1_turned"], t + 2)
                        act.copy(x1T[1 - par][:], pm[:]).then_inc(s["x1T_ready"], 1)
                if nxt:
                    act.wait_ge(s["dv_ready"], t + 2)
                    act.activation(ev[:], dv[:], ACT.Exp).then_inc(s["ev_ready"], 1)
                    act.wait_ge(s["hot_turned"], t + 2)
                    act.copy(hotT[1 - par][:], pmb[0:96, 0:N]).then_inc(s["hotT_ready"], 1)
                if cur:
                    act.wait_ge(s["h_ready"], t + 1)
                    act.activation(gl[:], h[:], ACT.Gelu).then_inc(s["gl_ready"], 1)

            slots(act, n, body)

        @block.vector
        def _(v):
            v.memset(logit[:], BIG)
            v.wait_ge(s["loaded"], LOADS)
            setup = Chain(v, s["set_chain"], 4)
            setup.begin(0)
            v.wait_ge(s["pool_chain"], 2)
            lo, hi = slice(32, 64), slice(64, 96)
            setup.step(v.tensor_copy(tab3[:], tabf[:]))
            v.tensor_tensor(tabf[lo, :], tabf[lo, :], tab3[lo, :], ALU.subtract)
            setup.step(v.tensor_tensor(tabf[hi, :], tabf[hi, :], tab3[hi, :], ALU.subtract))
            v.tensor_copy(tab3[lo, :], tabf[lo, :])
            setup.step(v.tensor_copy(tab3[hi, :], tabf[hi, :]))
            setup.step(v.tensor_tensor(tabf[hi, :], tabf[hi, :], tab3[hi, :], ALU.subtract))
            v.tensor_copy(tab3[hi, :], tabf[hi, :]).then_inc(s["w_set"], 1)
            hch = Chain(v, s["norm_chain"], 1 + MOMENT_STEPS + RSQRT_STEPS + 2, s["turn"])
            fch = Chain(v, s["fin_chain"], 3 + MOMENT_STEPS + RSQRT_STEPS + 5, s["turn"])
            rch = Chain(v, s["route_chain"], 9, s["turn"])
            pch = Chain(v, s["pre_chain"], 2)

            def pick_h(t, par, j):
                v.wait_ge(s["tab_ready"], t * G + j + 1)
                if j == 0:
                    after(v, s["gl_ready"], t)
                for b in range(E // EC):
                    k = (t * G + j) * (E // EC) + b
                    v.wait_ge(s["h_done"], k + 1)
                    if b:
                        v.wait_ge(s["h_read"], k)
                    e = EC * b
                    src = ph[b % 2]
                    v.scalar_tensor_tensor(h[:, j, :], src[:, 0, :], hot[par][:, j, e:e + 1],
                                           tab[par][:, j, 0:F] if b == 0 else h[:, j, :], ALU.mult, ALU.add)
                    if b == 0:
                        m = v.tensor_scalar(hodd[j % 2][:], src[:, 1, :], hot[par][:, j, e + 1:e + 2], None, ALU.mult)
                    else:
                        m = v.scalar_tensor_tensor(hodd[j % 2][:], src[:, 1, :], hot[par][:, j, e + 1:e + 2], hodd[j % 2][:], ALU.mult, ALU.add)
                    m.then_inc(s["h_read"], 1)
                v.wait_ge(s["h_read"], (t * G + j + 1) * (E // EC))
                v.tensor_tensor(h[:, j, :], h[:, j, :], hodd[j % 2][:], ALU.add).then_inc(s["hsum"], 1)

            def pick_y(t, par, j):
                tb = tab[par]
                for b in range(2):
                    k = (t * G + j) * 2 + b
                    v.wait_ge(s["y_done"], k + 1)
                    for q in range(0, 4, 2):
                        e = 4 * b + q
                        first = b == 0 and q == 0
                        if not first:
                            v.wait_ge(s["y_chain"], (t * G + j) * 4 + 2 * b + q // 2)
                        v.scalar_tensor_tensor(y[:, j, :], py[:, b, q, :], hot[par][:, j, e:e + 1],
                                               tb[:, j, 3 * F:3 * F + D] if first else y[:, j, :], ALU.mult, ALU.add)
                        if first:
                            m = v.tensor_scalar(yodd[j % 2][:], py[:, b, q + 1, :], hot[par][:, j, e + 1:e + 2], None, ALU.mult)
                        else:
                            m = v.scalar_tensor_tensor(yodd[j % 2][:], py[:, b, q + 1, :], hot[par][:, j, e + 1:e + 2], yodd[j % 2][:], ALU.mult, ALU.add)
                        m.then_inc(s["y_chain"], 1)
                    v.wait_ge(s["y_chain"], (t * G + j) * 4 + 2 * b + 2)
                    if b == 0:
                        v.sem_inc(s["y_read"], 1)
                    else:
                        v.tensor_tensor(y[:, j, :], y[:, j, :], yodd[j % 2][:], ALU.add).then_inc(s["y_read"], 1)

            def inner_norm(t, par):
                hch.begin(t)
                v.wait_ge(s["hsum"], (t + 1) * G)
                for j in range(G):
                    m = v.bn_stats(st[:, j, :], h[:, j, :])
                hch.step(m)
                moments(v, hch.step, F, [st[:, :, i:i + 1] for i in range(6)], mean[:], var[:], tt[:])
                rsqrt(v, hch.step, rstd[:], var[:], tt[:])
                for j in range(G):
                    m = v.tensor_scalar(h[:, j, :], h[:, j, :], mean[:, j, :], rstd[:, j, :], ALU.subtract, ALU.mult)
                hch.step(m)
                hch.step(v.tensor_tensor(h[:], h[:], tab[par][:, :, F:2 * F], ALU.mult))
                v.tensor_tensor(h[:], h[:], tab[par][:, :, 2 * F:3 * F], ALU.add).then_inc(s["h_ready"], 1)
                hch.end()

            def finish(t, par):
                fch.begin(t)
                v.wait_ge(s["y_read"], (t + 1) * G * 2)
                for j in range(G):
                    m = v.scalar_tensor_tensor(y[:, j, :], y[:, j, :], tab[par][:, j, TABS - 1:TABS], x1[par][:, j, :], ALU.mult, ALU.add)
                fch.step(m)
                for j in range(G):
                    m = v.scalar_tensor_tensor(y[:, j, :], y[:, j, :], wsum[par][:, j:j + 1], x1[par][:, j, :], ALU.mult, ALU.add)
                fch.step_apart(m)
                for j in range(G):
                    m = v.bn_stats(st[:, j, :], y[:, j, :])
                fch.step(m)
                moments(v, fch.step, D, [st[:, :, i:i + 1] for i in range(6)], mean[:], var[:], tt[:])
                rsqrt(v, fch.step, rstd[:], var[:], tt[:])
                for j in range(G):
                    m = v.tensor_scalar(y[:, j, :], y[:, j, :], mean[:, j, :], rstd[:, j, :], ALU.subtract, ALU.mult)
                fch.step(m)
                fch.step(v.tensor_tensor(y[:], y[:], n2g[:, None, :].to_broadcast([P, G, D]), ALU.mult))
                fch.step(v.tensor_tensor(y[:], y[:], n2b[:, None, :].to_broadcast([P, G, D]), ALU.add))
                fch.step_apart(v.scalar_tensor_tensor(K.X[:, bass.ds(t * G, G), :], y[:], 0.5, K.X[:, bass.ds(t * G, G), :],
                                                      ALU.mult, ALU.add))
                for j in range(G):
                    m = v.bn_stats(K.stats[:, t * G + j, :], K.X[:, t * G + j, :])
                fch.step(m)
                fch.end()

            def norm1(t, par):
                pch.begin(t)
                for j in range(G):
                    m = v.tensor_scalar(x1[par][:, j, :], Y[:, t * G + j, :], K.mean[:, t * G + j, :],
                                        K.rstd[:, t * G + j, :], ALU.subtract, ALU.mult)
                pch.step(m)
                pch.step(v.tensor_tensor(x1[par][:], x1[par][:], n1g[:, None, :].to_broadcast([P, G, D]), ALU.mult))
                v.tensor_tensor(x1[par][:], x1[par][:], n1b[:, None, :].to_broadcast([P, G, D]), ALU.add).then_inc(s["x1_ready"], 1)
                pch.end()

            def top2(t, par):
                rch.begin(t)
                v.wait_ge(s["logits_done"], t + 1)
                rch.step_apart(v.tensor_tensor(logit[:, :, 0:E], pm[:, 0:G * E].rearrange("p (g e) -> p g e", g=G),
                                               br[:, None, :].to_broadcast([P, G, E]), ALU.add))
                for j in range(G):
                    m = v.max(top8[:, j, :], logit[:, j, :])
                rch.step_apart(m)
                for j in range(G):
                    m = v.match_replace(struck[:, j, :], top8[:, j, :], logit[:, j, :], -BIG)
                rch.step(m)
                v.tensor_tensor(dv[:], top8[:, :, 7], top8[:, :, 6], ALU.subtract).then_inc(s["dv_ready"], 1)
                rch.step(v.scalar_tensor_tensor(index[:], struck[:, :, 0:E], -BIG / 2, iota[:, None, :].to_broadcast([P, G, E]),
                                                ALU.is_le, ALU.mult))
                rch.step(v.tensor_reduce(chosen[:], index[:], AX.X, ALU.max))
                rch.step(v.tensor_tensor(hot[par][:], iota[:, None, :].to_broadcast([P, G, E]),
                                         chosen[:, :, None].to_broadcast([P, G, E]), ALU.is_equal))
                for q in range(3):
                    m = v.tensor_copy(hot3[:, :, 32 * q:32 * q + E], hot[par][:])
                m.then_inc(s["hot_ready"], 1)
                v.wait_ge(s["ev_ready"], t + 1)
                rch.step(v.tensor_scalar(den[:], ev[:], 1.0, None, ALU.add))
                rch.step(v.reciprocal(den[:], den[:]))
                rch.step(v.tensor_tensor(wsum[par][:], ev[:], den[:], ALU.mult))
                v.tensor_tensor(wsum[par][:], wsum[par][:], den[:], ALU.add)
                rch.end()

            def body(t, par, prev, cur, nxt):
                for j in range(G):
                    if cur:
                        pick_h(t, par, j)
                    if prev and j < 2:
                        pick_y(t - 1, 1 - par, 2 * j)
                        pick_y(t - 1, 1 - par, 2 * j + 1)
                    if prev and j == 1:
                        finish(t - 1, 1 - par)
                    if nxt and j == 1:
                        norm1(t + 1, 1 - par)
                if nxt:
                    top2(t + 1, 1 - par)
                if cur:
                    inner_norm(t, par)

            slots(v, n, body)



def macaron_kernel(nc, T, out):
    x = T["L0_attn_X"]
    B, S, _ = x.shape
    with ExitStack() as ctx:
        K = Core(nc, ctx, B * S // P)
        load_phase(nc, K, x)
        with ExitStack() as weights:
            l0_ffn_weights(nc, K, weights, T["L0_ffn_classifier_weight"], T["L0_ffn_e_score_correction_bias"],
                           T["L0_ffn_gate_up_proj"], T["L0_ffn_down_proj"])
            norm_phase(nc, K, "n1")
            l0_ffn(nc, K, "f1")
            norm_phase(nc, K, "n2")
            l0_attention(nc, K, T["L0_attn_Wq"], T["L0_attn_Wk"], T["L0_attn_Wv"], S, "a1")
            norm_phase(nc, K, "n3")
            l0_ffn(nc, K, "f2")
        norm_phase(nc, K, "n4")
        l1_ffn(nc, K, T, S, "g1")
        norm_phase(nc, K, "n5")
        rwkv(nc, K, T, S, "r1")
        norm_phase(nc, K, "n6")
        l1_ffn(nc, K, T, S, "g2")
        store_phase(nc, K, out)


def store_phase(nc, K, out):
    with ExitStack() as c:
        s = c.enter_context(semaphores(nc, "store", ("stored",)))
        block = c.enter_context(nc.Block())

        @block.sync
        def _(sp):
            sp.dma_start(out.rearrange("b (t p) d -> p (b t) d", p=P), K.X[:]).then_inc(s["stored"], 16)
            sp.wait_ge(s["stored"], 16)


_INS = ["L0_attn_X", "L0_attn_Wq", "L0_attn_Wk", "L0_attn_Wv", "L0_ffn_classifier_weight",
        "L0_ffn_e_score_correction_bias", "L0_ffn_gate_up_proj", "L0_ffn_down_proj", "L1_attn_xk", "L1_attn_xv",
        "L1_attn_time_decay", "L1_attn_time_first", "L1_attn_time_mix_k", "L1_attn_time_mix_v",
        "L1_attn_time_mix_r", "L1_attn_Wk", "L1_attn_Wv", "L1_attn_Wr", "L1_attn_Wo", "L1_ffn_q_w", "L1_ffn_k_w",
        "L1_ffn_v_w", "L1_ffn_out_w", "L1_ffn_gate_w", "L1_ffn_gate_b", "L1_ffn_scale_w", "L1_ffn_n1_g",
        "L1_ffn_n1_b", "L1_ffn_n2_g", "L1_ffn_n2_b", "L1_ffn_moe_gate_w", "L1_ffn_moe_gate_b", "L1_ffn_w1",
        "L1_ffn_b1", "L1_ffn_ln_g", "L1_ffn_ln_b", "L1_ffn_w2", "L1_ffn_b2", "L1_ffn_res_scale"]


def kernel(**inputs):
    import numpy as _np
    import concourse.bacc as _bacc
    from concourse import mybir as _mybir
    from concourse.bass_utils import run_bass_kernel_spmd as _run

    nc = _bacc.Bacc("TRN2", target_bir_lowering=False, num_devices=1)
    arrays, args = {}, {}
    for name in _INS:
        if name in ("L1_attn_xk", "L1_attn_xv"):
            continue
        a = _np.ascontiguousarray(inputs[name])
        arrays[f"in_{name}_dram"] = a
        args[name] = nc.dram_tensor(f"in_{name}_dram", a.shape, _mybir.dt.from_np(a.dtype), kind="ExternalInput").ap()
    shape = inputs["L0_attn_X"].shape
    out = nc.dram_tensor("out_0_dram", shape, _mybir.dt.float32, kind="ExternalOutput").ap()
    macaron_kernel(nc, args, out)
    r = _run(nc, [arrays], core_ids=[0])
    return r.results[0]["out_0_dram"]
```

```python
from contextlib import ExitStack, contextmanager

import concourse.bass as bass
from concourse import mybir

F32 = mybir.dt.float32
F32R = mybir.dt.float32r
BF16 = mybir.dt.bfloat16
I32 = mybir.dt.int32
ALU = mybir.AluOpType
ACT = mybir.ActivationFunctionType
AX = mybir.AxisListType

P = 128
D = 128
EPS = 1e-5
BIG = 3e38
RSQRT_SEED = 1597463007.0


def after(eng, sem, count):
    if isinstance(count, int) and count <= 0:
        return
    eng.wait_ge(sem, count)


@contextmanager
def semaphores(nc, phase, names):
    sems = [nc.alloc_semaphore(f"{k}_{phase}") for k in names]
    yield dict(zip(names, sems))
    nc.clear_and_free_semaphores(sems)
    nc.all_engine_barrier()


class Chain:

    def __init__(self, eng, sem, per, turn=None):
        self.eng, self.sem, self.per, self.turn = eng, sem, per, turn

    def begin(self, round_):
        self.base, self.n = round_ * self.per, 0

    def step(self, ins):
        self.n += 1
        ins.then_inc(self.sem, 1)
        self.eng.wait_ge(self.sem, self.base + self.n)

    def step_apart(self, ins):
        self.step(ins)
        self.eng.sem_inc(self.turn, 1)

    def end(self):
        assert self.n == self.per, (self.n, self.per)


PEELED = 3


def slots(eng, n, body, ahead=1):
    turns = max(0, (n - ahead - PEELED) // 2)
    looped = range(PEELED, PEELED + 2 * turns)
    more = (True,) * (ahead - 1)
    for t in range(-ahead, n + 1):
        if t not in looped:
            body(t, t % 2, t > 0, 0 <= t < n, *(0 <= t + k < n for k in range(1, ahead + 1)))
        elif t == PEELED:
            with eng.Fori(0, turns) as i:
                body(2 * i + PEELED, PEELED % 2, True, True, True, *more)
                body(2 * i + PEELED + 1, 1 - PEELED % 2, True, True, True, *more)


RSQRT_STEPS = 11


def rsqrt(v, step, y, a, t):
    step(v.tensor_scalar(t.bitcast(I32), a.bitcast(I32), 1, None, ALU.logical_shift_right))
    step(v.tensor_scalar(y.bitcast(I32), t.bitcast(I32), -1.0, RSQRT_SEED, ALU.mult, ALU.add))
    for _ in range(3):
        step(v.scalar_tensor_tensor(t, y, -0.5, y, ALU.mult, ALU.mult))
        step(v.tensor_tensor(t, t, a, ALU.mult))
        step(v.scalar_tensor_tensor(y, t, 1.5, y, ALU.add, ALU.mult))


def moments(v, step, n, st, mean, var, t):
    step(v.tensor_tensor(mean, st[1], st[4], ALU.add))
    step(v.tensor_scalar(mean, mean, 0.5, None, ALU.mult))
    step(v.tensor_tensor(t, st[1], st[4], ALU.subtract))
    step(v.scalar_tensor_tensor(t, t, 0.25, t, ALU.mult, ALU.mult))
    step(v.tensor_tensor(var, st[2], st[5], ALU.add))
    step(v.tensor_scalar(var, var, 1.0 / n, EPS, ALU.mult, ALU.add))
    step(v.tensor_tensor(var, var, t, ALU.add))


MOMENT_STEPS = 7


class Core:

    def __init__(self, nc, ctx, tiles):
        def sb(name, shape, dt=F32):
            return ctx.enter_context(nc.sbuf_tensor(name, shape, dt))

        self.nc, self.tiles = nc, tiles
        self.X = sb("X", [P, tiles, D])
        self.stats = sb("stats", [P, tiles, 6])
        self.mean = sb("mean", [P, tiles, 1])
        self.rstd = sb("rstd", [P, tiles, 1])
        self.ident = sb("ident", [P, P])
        self.identb = sb("identb", [P, P], BF16)


def load_phase(nc, K, x_dram):
    with ExitStack() as c:
        ones = c.enter_context(nc.sbuf_tensor("ones_sq", [P, P], F32))
        loads = 4 if K.tiles % 4 == 0 else 1
        s = c.enter_context(semaphores(nc, "load", ["ones_set", "ident_set"] + [f"x_loaded{i}" for i in range(loads)]))
        block = c.enter_context(nc.Block())
        per = K.tiles // loads
        xs = x_dram.rearrange("b (t p) d -> p (b t) d", p=P)

        @block.sync
        def _(sp):
            for i in range(loads):
                sp.dma_start(K.X[:, i * per:(i + 1) * per, :], xs[:, i * per:(i + 1) * per, :]).then_inc(s[f"x_loaded{i}"], 16)

        @block.gpsimd
        def _(pool):
            pool.memset(ones[:], 1.0).then_inc(s["ones_set"], 1)
            pool.wait_ge(s["ones_set"], 1)
            pool.affine_select(out=K.ident[:], in_=ones[:], compare_op=ALU.is_equal, fill=0.0, base=0,
                               pattern=[[-1, P]], channel_multiplier=1).then_inc(s["ident_set"], 1)
            pool.wait_ge(s["ident_set"], 1)
            pool.tensor_copy(K.identb[:], K.ident[:])

        @block.vector
        def _(v):
            for i in range(loads):
                v.wait_ge(s[f"x_loaded{i}"], 16)
                for t in range(i * per, (i + 1) * per):
                    v.bn_stats(K.stats[:, t, :], K.X[:, t, :])


def norm_phase(nc, K, name):
    with ExitStack() as c:
        var = c.enter_context(nc.sbuf_tensor(f"var_{name}", [P, K.tiles, 1], F32))
        t = c.enter_context(nc.sbuf_tensor(f"t_{name}", [P, K.tiles, 1], F32))
        s = c.enter_context(semaphores(nc, name, ("norm_chain",)))
        block = c.enter_context(nc.Block())

        @block.vector
        def _(v):
            ch = Chain(v, s["norm_chain"], MOMENT_STEPS + RSQRT_STEPS)
            ch.begin(0)
            st = [K.stats[:, :, i:i + 1] for i in range(6)]
            moments(v, ch.step, D, st, K.mean[:], var[:], t[:])
            rsqrt(v, ch.step, K.rstd[:], var[:], t[:])
            ch.end()



def l0_ffn_weights(nc, K, ctx, cls_w, cls_b, gate_up, down):
    ET, H = cls_w.shape
    ER, _, I = down.shape
    pairs = ER // 2

    def sb(name, shape, dt=F32):
        return ctx.enter_context(nc.sbuf_tensor(name, shape, dt))

    K.ER, K.ET, K.I, K.pairs = ER, ET, I, pairs
    K.wg = sb("wg", [P, ER, I])
    K.wu = sb("wu", [P, ER, I])
    K.wd = sb("wd", [P, pairs, D])
    K.wc = sb("wc", [P, ET])
    K.bias = sb("cls_bias", [P, ET])
    K.sel = sb("sel", [3 * ER, pairs, P], BF16)
    GB = 8
    with ExitStack() as c:
        raw_gu = c.enter_context(nc.sbuf_tensor("raw_gu", [P, ER, H], F32))
        raw_d = c.enter_context(nc.sbuf_tensor("raw_d", [P, ER, I], F32))
        raw_c = c.enter_context(nc.sbuf_tensor("raw_c", [ET, H], F32))
        ps = [c.enter_context(nc.psum_tensor(f"ps_w{i}", [P, 4, P], F32)) for i in range(2)]
        s = c.enter_context(semaphores(nc, "w0", ("gu_loaded", "d_loaded", "c_loaded", "b_loaded", "turned", "copied",
                                                  "sel_step")))
        block = c.enter_context(nc.Block())
        jobs = ER // 4 + pairs // 4 + 1

        @block.sync
        def _(sp):
            sp.dma_start(raw_gu[:], gate_up[0:ER].rearrange("e f d -> f e d")).then_inc(s["gu_loaded"], 16)
            sp.dma_start(raw_c[:], cls_w).then_inc(s["c_loaded"], 16)
            sp.dma_start(K.bias[:], cls_b.rearrange("(a e) -> a e", a=1).to_broadcast([P, ET])).then_inc(s["b_loaded"], 16)
            sp.wait_ge(s["b_loaded"], 16)

        @block.gpsimd
        def _(pool):
            pool.memset(K.sel[:], 0.0).then_inc(s["sel_step"], 1)
            v = K.sel[:].rearrange("k p (h m) -> k p h m", h=2)
            for b in range(3):
                pool.wait_ge(s["sel_step"], b + 1)
                pool.affine_select(out=v, in_=v, compare_op=ALU.not_equal, fill=1.0, base=-ER * b,
                                   pattern=[[-2, pairs], [-1, 2], [0, P // 2]], channel_multiplier=1).then_inc(s["sel_step"], 1)

        @block.tensor
        def _(pe):
            pe.wait_ge(s["gu_loaded"], 16)
            pe.wait_ge(s["d_loaded"], 16)
            pe.wait_ge(s["c_loaded"], 16)
            for j in range(jobs):
                after(pe, s["copied"], j - 1)
                for i in range(4):
                    if j < ER // 4:
                        m = pe.transpose(ps[j % 2][:, i, :], raw_gu[:, 4 * j + i, :], K.ident[:])
                    elif j < jobs - 1:
                        p = 4 * (j - ER // 4) + i
                        m = pe.transpose(ps[j % 2][:, i, :], raw_d[:, 2 * p:2 * p + 2, :].rearrange("p e f -> p (e f)"), K.ident[:])
                    elif i == 0:
                        m = pe.transpose(ps[j % 2][:, 0, 0:ET], raw_c[:], K.ident[0:ET, 0:ET])
                m.then_inc(s["turned"], 1)

        @block.vector
        def _(v):
            for j in range(jobs):
                v.wait_ge(s["turned"], j + 1)
                if j < ER // 4:
                    v.tensor_copy(K.wg[:, 4 * j:4 * j + 4, :], ps[j % 2][:, :, 0:I])
                    v.tensor_copy(K.wu[:, 4 * j:4 * j + 4, :], ps[j % 2][:, :, I:2 * I]).then_inc(s["copied"], 1)
                elif j < jobs - 1:
                    p = 4 * (j - ER // 4)
                    v.tensor_copy(K.wd[:, p:p + 4, :], ps[j % 2][:]).then_inc(s["copied"], 1)
                else:
                    v.tensor_copy(K.wc[:], ps[j % 2][:, 0, 0:ET]).then_inc(s["copied"], 1)

        @block.scalar
        def _(act):
            act.dma_start(raw_d[:], down.rearrange("e d f -> d e f")).then_inc(s["d_loaded"], 16)


def l0_ffn(nc, K, name):
    ER, ET, pairs = K.ER, K.ET, K.pairs
    G = 4
    N = G * P
    n = K.tiles // G
    TOPK, SCALE = 6, 2.5
    PAD = 8 - TOPK
    with ExitStack() as c:
        sb = lambda nm, s, dt=F32: c.enter_context(nc.sbuf_tensor(f"{nm}_{name}", s, dt))
        ps = lambda nm, s, dt=F32: c.enter_context(nc.psum_tensor(f"{nm}_{name}", s, dt))
        xn = [sb(f"xn{i}", [P, G, D]) for i in range(2)]
        xT = [sb(f"xT{i}", [P, N]) for i in range(2)]
        wparts = sb("wparts", [P, G, 3 * ER], BF16)
        wT = [sb(f"wT{i}", [3 * ER, N], BF16) for i in range(2)]
        zero_w = [sb(f"zero_w{i}", [P, G]) for i in range(2)]
        logit, expd, score = sb("logit", [P, G, ET]), sb("expd", [P, G, ET]), sb("score", [P, G, ET])
        biased, struck = sb("biased", [P, G, ET + PAD]), sb("struck", [P, G, ET + PAD])
        top8, w, rest = sb("top8", [P, G, 8]), sb("w", [P, G, ET]), sb("rest", [P, G, ER])
        rmax, rsum, rinv = sb("rmax", [P, G]), sb("rsum", [P, G]), sb("rinv", [P, G])
        silu = [sb(f"silu{i}", [P, N]) for i in range(2)]
        gated = [sb(f"gated{i}", [P, N]) for i in range(2)]
        hid = [sb(f"hid{i}", [P, N]) for i in range(2)]
        outT, y = sb("outT", [P, N]), sb("y", [P, G, D])
        pg = [ps(f"pg{i}", [P, N]) for i in range(2)]
        pu = [ps(f"pu{i}", [P, N]) for i in range(2)]
        pw = [ps(f"pw{i}", [P, N]) for i in range(2)]
        po, pm = ps("po", [P, N]), ps("pm", [P, N])
        pmb = pm[:].bitcast(BF16)
        s = c.enter_context(semaphores(nc, name, (
            "pad_set", "xn_ready", "xn_turned", "xT_ready", "logits_done", "logits_read", "exp_done", "parts_ready",
            "parts_turned", "wT_ready", "gate_done", "pair_done", "silu_done", "gated_done", "hid_done", "down_done",
            "outT_ready", "out_turned", "out_read", "route_chain", "out_chain", "turn")))
        block = c.enter_context(nc.Block())

        @block.tensor
        def _(pe):
            def body(t, par, prev, cur, nxt):
                for p in range(pairs):
                    if cur:
                        k = t * pairs + p
                        b = p % 2
                        if p == 0:
                            pe.wait_ge(s["wT_ready"], t + 1)
                        after(pe, s["silu_done"], k - 1)
                        pe.matmul(pg[b][:], K.wg[:, 2 * p:2 * p + 2, :], xT[par][:], start=True,
                                  stop=True).then_inc(s["gate_done"], 1)
                        after(pe, s["hid_done"], k - 1)
                        pe.matmul(pu[b][:], K.wu[:, 2 * p:2 * p + 2, :], xT[par][:], start=True, stop=True)
                        pe.matmul(pw[b][:], K.sel[:, p, :], wT[par][:], start=True,
                                  stop=True).then_inc(s["pair_done"], 1)
                        if p >= 2:
                            if p == 2:
                                after(pe, s["outT_ready"], t)
                            down(t, p - 2)
                    if prev and p == 2:
                        pe.wait_ge(s["outT_ready"], t)
                        for j in range(G):
                            m = pe.transpose(pm[:, j * P:(j + 1) * P], outT[:, j * P:(j + 1) * P], K.ident[:])
                        m.then_inc(s["out_turned"], 1)
                    if nxt and p == 5:
                        pe.wait_ge(s["xn_ready"], t + 2)
                        after(pe, s["out_read"], t)
                        for j in range(G):
                            m = pe.transpose(pm[:, j * P:(j + 1) * P], xn[1 - par][:, j, :], K.ident[:])
                        m.then_inc(s["xn_turned"], 1)
                    if nxt and p == 7:
                        pe.wait_ge(s["xT_ready"], t + 2)
                        for j in range(G):
                            m = pe.matmul(pm[:, j * ET:(j + 1) * ET], xT[1 - par][:, j * P:(j + 1) * P], K.wc[:],
                                          start=True, stop=True)
                        m.then_inc(s["logits_done"], 1)
                    if nxt and p == 13:
                        pe.wait_ge(s["parts_ready"], t + 2)
                        for j in range(G):
                            m = pe.transpose(pmb[0:3 * ER, j * P:(j + 1) * P], wparts[:, j, :], K.identb[:])
                        m.then_inc(s["parts_turned"], 1)

                if cur:
                    down(t, pairs - 2)
                    down(t, pairs - 1)

            def down(t, p):
                k = t * pairs + p
                pe.wait_ge(s["hid_done"], k + 1)
                pe.matmul(po[:], K.wd[:, p, :], hid[p % 2][:], start=(p == 0), stop=(p == pairs - 1)).then_inc(s["down_done"], 1)

            slots(pe, n, body)

        @block.scalar
        def _(act):
            def body(t, par, prev, cur, nxt):
                for p in range(pairs):
                    if prev and p == 0:
                        pe_done = t * pairs
                        act.wait_ge(s["down_done"], pe_done)
                        after(act, s["out_turned"], t - 1)
                        act.copy(outT[:], po[:]).then_inc(s["outT_ready"], 1)
                    if cur:
                        k = t * pairs + p
                        act.wait_ge(s["gate_done"], k + 1)
                        after(act, s["gated_done"], k - 1)
                        act.activation(silu[p % 2][:], pg[p % 2][:], ACT.Silu).then_inc(s["silu_done"], 1)
                    if nxt and p == 6:
                        act.wait_ge(s["xn_turned"], t + 2)
                        act.copy(xT[1 - par][:], pm[:]).then_inc(s["xT_ready"], 1)
                    if nxt and p == 9:
                        act.wait_ge(s["logits_read"], t + 2)
                        act.activation(expd[:], logit[:], ACT.Exp).then_inc(s["exp_done"], 1)
                    if nxt and p == 14:
                        act.wait_ge(s["parts_turned"], t + 2)
                        act.copy(wT[1 - par][:], pmb[0:3 * ER, 0:N]).then_inc(s["wT_ready"], 1)

            slots(act, n, body)

        @block.vector
        def _(v):
            route = Chain(v, s["route_chain"], 13, s["turn"])
            out = Chain(v, s["out_chain"], 2, s["turn"])
            v.memset(biased[:], BIG).then_inc(s["pad_set"], 1)
            v.wait_ge(s["pad_set"], 1)

            def gate(t, p):
                k = t * pairs + p
                v.wait_ge(s["silu_done"], k + 1)
                v.wait_ge(s["pair_done"], k + 1)
                v.tensor_tensor(gated[p % 2][:], silu[p % 2][:], pu[p % 2][:], ALU.mult).then_inc(s["gated_done"], 1)

            def weigh(t, p):
                k = t * pairs + p
                v.wait_ge(s["gated_done"], k + 1)
                after(v, s["down_done"], k - 1)
                v.tensor_tensor(hid[p % 2][:], gated[p % 2][:], pw[p % 2][:], ALU.mult).then_inc(s["hid_done"], 1)

            def finish(t, par):
                out.begin(t)
                v.wait_ge(s["out_turned"], t + 1)
                for j in range(G):
                    m = v.scalar_tensor_tensor(y[:, j, :], xn[par][:, j, :], zero_w[par][:, j:j + 1],
                                               pm[:, j * P:(j + 1) * P], ALU.mult, ALU.add)
                m.then_inc(s["out_read"], 1)
                v.wait_ge(s["out_read"], t + 1)
                out.step_apart(v.scalar_tensor_tensor(K.X[:, bass.ds(t * G, G), :], y[:], 0.5 * SCALE,
                                                      K.X[:, bass.ds(t * G, G), :], ALU.mult, ALU.add))
                for j in range(G):
                    m = v.bn_stats(K.stats[:, t * G + j, :], K.X[:, t * G + j, :])
                out.step(m)
                out.end()

            def norm(t, par):
                for j in range(G):
                    m = v.tensor_scalar(xn[par][:, j, :], K.X[:, t * G + j, :], K.mean[:, t * G + j, :],
                                        K.rstd[:, t * G + j, :], ALU.subtract, ALU.mult)
                m.then_inc(s["xn_ready"], 1)

            def center(t):
                route.begin(t)
                pl = pm[:, 0:G * ET].rearrange("p (g e) -> p g e", g=G)
                v.wait_ge(s["logits_done"], t + 1)
                route.step(v.tensor_reduce(rmax[:], pl, AX.X, ALU.max))
                v.tensor_tensor(logit[:], pl, rmax[:, :, None].to_broadcast([P, G, ET]),
                                ALU.subtract).then_inc(s["logits_read"], 1)

            def topk(t, par):
                v.wait_ge(s["exp_done"], t + 1)
                route.step(v.tensor_reduce(rsum[:], expd[:], AX.X, ALU.add))
                route.step(v.reciprocal(rinv[:], rsum[:]))
                route.step(v.tensor_tensor(score[:], expd[:], rinv[:, :, None].to_broadcast([P, G, ET]), ALU.mult))
                route.step_apart(v.tensor_tensor(biased[:, :, 0:ET], score[:],
                                                 K.bias[:, None, :].to_broadcast([P, G, ET]), ALU.add))
                for j in range(G):
                    m = v.max(top8[:, j, :], biased[:, j, :])
                route.step_apart(m)
                for j in range(G):
                    m = v.match_replace(struck[:, j, :], top8[:, j, :], biased[:, j, :], -BIG)
                route.step(m)
                route.step(v.scalar_tensor_tensor(w[:], struck[:, :, 0:ET], -BIG / 2, score[:], ALU.is_le, ALU.mult))
                route.step(v.tensor_reduce(zero_w[par][:], w[:, :, ER:ET], AX.X, ALU.add))
                route.step(v.tensor_copy(wparts[:, :, 0:ER], w[:, :, 0:ER]))
                route.step(v.tensor_tensor(rest[:], w[:, :, 0:ER], wparts[:, :, 0:ER], ALU.subtract))
                route.step(v.tensor_copy(wparts[:, :, ER:2 * ER], rest[:]))
                route.step(v.tensor_tensor(rest[:], rest[:], wparts[:, :, ER:2 * ER], ALU.subtract))
                v.tensor_copy(wparts[:, :, 2 * ER:3 * ER], rest[:]).then_inc(s["parts_ready"], 1)
                route.end()

            def body(t, par, prev, cur, nxt):
                for p in range(pairs):
                    if cur:
                        if p >= 1:
                            weigh(t, p - 1)
                        gate(t, p)
                    if prev and p == 3:
                        finish(t - 1, 1 - par)
                    if nxt and p == 4:
                        norm(t + 1, 1 - par)
                    if nxt and p == 8:
                        center(t + 1)
                    if nxt and p == 10:
                        topk(t + 1, 1 - par)
                if cur:
                    weigh(t, pairs - 1)

            slots(v, n, body)



def l0_attention(nc, K, wq_d, wk_d, wv_d, seq, name):
    DQ = wq_d.shape[1]
    R = seq // P
    assert R == 2
    n = K.tiles // R
    W = P * (R * (R + 1) // 2)
    with ExitStack() as c:
        sb = lambda nm, s, dt=F32: c.enter_context(nc.sbuf_tensor(f"{nm}_{name}", s, dt))
        ps = lambda nm, s, dt=F32: c.enter_context(nc.psum_tensor(f"{nm}_{name}", s, dt))
        wq, wk, wv = sb("wq", [P, DQ]), sb("wk", [P, DQ]), sb("wv", [P, D])
        mask = sb("mask", [P, W])
        xn, xT = sb("xn", [P, R, D]), sb("xT", [P, seq])
        qk = sb("qk", [DQ, 2, seq])
        val = [sb(f"val{i}", [P, R, D]) for i in range(2)]
        sc, probs, probsT = sb("sc", [P, W]), sb("probs", [P, W]), sb("probsT", [P, W])
        nmax, sums, rinv = sb("nmax", [P, R]), sb("sums", [P, R]), sb("rinv", [P, R])
        px, pqk, pv = ps("px", [P, seq]), ps("pqk", [DQ, 2, seq]), ps("pv", [P, R, D])
        pS, pT, pO = ps("pS", [P, W]), ps("pT", [P, W]), ps("pO", [P, R, D])
        s = c.enter_context(semaphores(nc, name, (
            "w_loaded", "mask_zero", "mask_set", "wq_scaled", "xn_ready", "xn_turned", "xT_ready", "qkv_done", "qk_ready",
            "v_ready", "scores_done", "masked", "max_ready", "exp_done", "probs_turned", "probsT_ready",
            "out_done", "inv_ready", "x_written", "x_done", "turn")))
        block = c.enter_context(nc.Block())

        @block.sync
        def _(sp):
            sp.dma_start(wq[:], wq_d).then_inc(s["w_loaded"], 16)
            sp.dma_start(wk[:], wk_d).then_inc(s["w_loaded"], 16)
            sp.dma_start(wv[:], wv_d).then_inc(s["w_loaded"], 16)

        @block.gpsimd
        def _(pool):
            pool.memset(mask[:], 0.0).then_inc(s["mask_zero"], 1)
            pool.wait_ge(s["mask_zero"], 1)
            for col in (0, 2 * P):
                m = pool.affine_select(out=mask[:, col:col + P], in_=mask[:, col:col + P], compare_op=ALU.is_ge,
                                       fill=-BIG, base=0, pattern=[[-1, P]], channel_multiplier=1)
            m.then_inc(s["mask_set"], 1)

        @block.tensor
        def _(pe):
            def body(t, par, prev, cur, nxt):
                if cur:
                    pe.wait_ge(s["qk_ready"], t + 1)
                    after(pe, s["masked"], t)
                    pe.matmul(pS[:, 0:P], qk[:, 0, 0:P], qk[:, 1, 0:P], start=True, stop=True)
                    pe.matmul(pS[:, P:W], qk[:, 0, P:seq], qk[:, 1, :], start=True,
                              stop=True).then_inc(s["scores_done"], 1)
                if nxt:
                    pe.wait_ge(s["xn_ready"], t + 2)
                    for j in range(R):
                        m = pe.transpose(px[:, j * P:(j + 1) * P], xn[:, j, :], K.ident[:])
                    m.then_inc(s["xn_turned"], 1)
                    pe.wait_ge(s["xT_ready"], t + 2)
                    if isinstance(t, int) and t == -1:
                        pe.wait_ge(s["wq_scaled"], 1)
                    pe.matmul(pqk[:, 0, :], wq[:], xT[:], start=True, stop=True)
                    pe.matmul(pqk[:, 1, :], wk[:], xT[:], start=True, stop=True)
                    after(pe, s["v_ready"], t + 1)
                    for j in range(R):
                        m = pe.matmul(pv[:, j, :], xT[:, j * P:(j + 1) * P], wv[:], start=True, stop=True)
                    m.then_inc(s["qkv_done"], 1)
                if cur:
                    pe.wait_ge(s["exp_done"], t + 1)
                    for j in range(W // P):
                        m = pe.transpose(pT[:, j * P:(j + 1) * P], probs[:, j * P:(j + 1) * P], K.ident[:])
                    m.then_inc(s["probs_turned"], 1)
                    pe.wait_ge(s["probsT_ready"], t + 1)
                    pe.wait_ge(s["v_ready"], t + 1)
                    after(pe, s["x_written"], t)
                    pe.matmul(pO[:, 0, :], probsT[:, 0:P], val[par][:, 0, :], start=True, stop=True)
                    pe.matmul(pO[:, 1, :], probsT[:, P:2 * P], val[par][:, 0, :], start=True, stop=False)
                    pe.matmul(pO[:, 1, :], probsT[:, 2 * P:W], val[par][:, 1, :], start=False,
                              stop=True).then_inc(s["out_done"], 1)

            slots(pe, n, body)

        @block.scalar
        def _(act):
            def body(t, par, prev, cur, nxt):
                if cur:
                    act.wait_ge(s["max_ready"], t + 1)
                    act.activation(probs[:, 0:P], sc[:, 0:P], ACT.Exp, bias=nmax[:, 0:1], accum_out=sums[:, 0:1])
                    act.activation(probs[:, P:W], sc[:, P:W], ACT.Exp, bias=nmax[:, 1:2],
                                   accum_out=sums[:, 1:2]).then_inc(s["exp_done"], 1)
                if nxt:
                    act.wait_ge(s["xn_turned"], t + 2)
                    act.copy(xT[:], px[:]).then_inc(s["xT_ready"], 1)
                    act.wait_ge(s["qkv_done"], t + 2)
                    act.copy(qk[:], pqk[:]).then_inc(s["qk_ready"], 1)
                if cur:
                    act.wait_ge(s["probs_turned"], t + 1)
                    act.copy(probsT[:], pT[:]).then_inc(s["probsT_ready"], 1)

            slots(act, n, body)

        @block.vector
        def _(v):
            v.wait_ge(s["w_loaded"], 48)
            v.tensor_scalar(wq[:], wq[:], float(DQ) ** -0.5, None, ALU.mult).then_inc(s["wq_scaled"], 1)
            v.wait_ge(s["mask_set"], 1)

            def body(t, par, prev, cur, nxt):
                if nxt:
                    for j in range(R):
                        i = (t + 1) * R + j
                        m = v.tensor_scalar(xn[:, j, :], K.X[:, i, :], K.mean[:, i, :], K.rstd[:, i, :],
                                            ALU.subtract, ALU.mult)
                    m.then_inc(s["xn_ready"], 1)
                if cur:
                    v.wait_ge(s["scores_done"], t + 1)
                    v.tensor_tensor(sc[:], pS[:], mask[:], ALU.add).then_inc(s["masked"], 1)
                    v.wait_ge(s["masked"], t + 1)
                    v.tensor_reduce(nmax[:, 0:1], sc[:, 0:P], AX.X, ALU.max, negate=True)
                    v.tensor_reduce(nmax[:, 1:2], sc[:, P:W], AX.X, ALU.max, negate=True).then_inc(s["max_ready"], 1)
                if nxt:
                    v.wait_ge(s["qkv_done"], t + 2)
                    v.tensor_copy(val[1 - par][:], pv[:]).then_inc(s["v_ready"], 1)
                if cur:
                    v.wait_ge(s["exp_done"], t + 1)
                    v.reciprocal(rinv[:], sums[:]).then_inc(s["inv_ready"], 1)
                    v.wait_ge(s["inv_ready"], t + 1)
                    v.wait_ge(s["out_done"], t + 1)
                    for j in range(R):
                        m = v.scalar_tensor_tensor(K.X[:, t * R + j, :], pO[:, j, :], rinv[:, j:j + 1],
                                                   K.X[:, t * R + j, :], ALU.mult, ALU.add)
                    m.then_inc(s["x_written"], 1)
                    v.wait_ge(s["x_written"], t + 1)
                    v.sem_inc(s["turn"], 1)
                    for j in range(R):
                        m = v.bn_stats(K.stats[:, t * R + j, :], K.X[:, t * R + j, :])
                    m.then_inc(s["x_done"], 1)

            slots(v, n, body)



def rwkv(nc, K, T, seq, name):
    R = seq // P
    n = K.tiles // R
    CLAMP, KEPS = 60.0, 1e-8
    with ExitStack() as c:
        sb = lambda nm, s, dt=F32: c.enter_context(nc.sbuf_tensor(f"{nm}_{name}", s, dt))
        ps = lambda nm, s, dt=F32: c.enter_context(nc.psum_tensor(f"{nm}_{name}", s, dt))
        raw = sb("raw", [P, 4, P])
        wT = sb("wT", [P, 4, P])
        mix, omix = sb("mix", [P, 3]), sb("omix", [P, 3])
        tdec, first, decay = sb("tdec", [P, 1]), sb("first", [P, 1]), sb("decay", [P, 1])
        decays = sb("decays", [P, seq])
        xn = sb("xn", [P, R, D])
        xs = [sb(f"xs{i}", [P, seq + 1]) for i in range(2)]
        part, mixed = sb("part", [P, 3, seq]), sb("mixed", [P, 3, seq])
        kmin, kc, kv, th = sb("kmin", [P, seq]), sb("kc", [P, seq]), sb("kv", [P, seq]), sb("th", [P, seq])
        sk, skv = sb("sk", [P, seq + 1]), sb("skv", [P, seq + 1])
        den, num, inv, o = sb("den", [P, seq]), sb("num", [P, seq]), sb("inv", [P, seq]), sb("o", [P, seq])
        px, pkv, pr, pO, pw = ps("px", [P, seq]), ps("pkv", [P, 2, seq]), ps("pr", [P, seq]), ps("pO", [P, R, D]), ps("pw", [P, 4, P])
        s = c.enter_context(semaphores(nc, name, (
            "loaded", "w_turned", "w_ready", "setup", "set_chain", "xn_ready", "xn_turned", "xs_ready", "parts", "mixed_ready",
            "proj_done", "kmin_ready", "kc_ready", "th_ready", "chain", "o_ready", "out_done", "x_written", "x_done", "turn")))
        block = c.enter_context(nc.Block())

        @block.sync
        def _(sp):
            for i, w in enumerate(("Wk", "Wv", "Wr", "Wo")):
                sp.dma_start(raw[:, i, :], T[f"L1_attn_{w}"]).then_inc(s["loaded"], 16)
            for i, w in enumerate(("k", "v", "r")):
                sp.dma_start(mix[:, i:i + 1], T[f"L1_attn_time_mix_{w}"].rearrange("a b c -> c (a b)")).then_inc(s["loaded"], 16)
            sp.dma_start(tdec[:], T["L1_attn_time_decay"]).then_inc(s["loaded"], 16)
            sp.dma_start(first[:], T["L1_attn_time_first"]).then_inc(s["loaded"], 16)

        LOADS = 16 * 9

        @block.tensor
        def _(pe):
            pe.wait_ge(s["loaded"], LOADS)
            for i in range(4):
                m = pe.transpose(pw[:, i, :], raw[:, i, :], K.ident[:])
            m.then_inc(s["w_turned"], 1)

            def body(t, par, prev, cur, nxt):
                if nxt:
                    pe.wait_ge(s["xn_ready"], t + 2)
                    after(pe, s["xs_ready"], t + 1)
                    for j in range(R):
                        m = pe.transpose(px[:, j * P:(j + 1) * P], xn[:, j, :], K.ident[:])
                    m.then_inc(s["xn_turned"], 1)
                if cur:
                    if isinstance(t, int) and t == 0:
                        pe.wait_ge(s["w_ready"], 1)
                    pe.wait_ge(s["mixed_ready"], t + 1)
                    for i in range(2):
                        pe.matmul(pkv[:, i, :], wT[:, i, :], mixed[:, i, :], start=True, stop=True)
                    pe.matmul(pr[:], wT[:, 2, :], mixed[:, 2, :], start=True, stop=True).then_inc(s["proj_done"], 1)
                    pe.wait_ge(s["o_ready"], t + 1)
                    for j in range(R):
                        m = pe.matmul(pO[:, j, :], o[:, j * P:(j + 1) * P], wT[:, 3, :], start=True, stop=True)
                    m.then_inc(s["out_done"], 1)

            slots(pe, n, body)

        @block.scalar
        def _(act):
            act.wait_ge(s["loaded"], LOADS)
            act.activation(tdec[:], tdec[:], ACT.Exp).then_inc(s["set_chain"], 1)
            act.wait_ge(s["set_chain"], 1)
            act.activation(decay[:], tdec[:], ACT.Exp, scale=-1.0)
            act.activation(first[:], first[:], ACT.Exp).then_inc(s["setup"], 1)
            act.wait_ge(s["w_turned"], 1)
            act.copy(wT[:], pw[:]).then_inc(s["w_ready"], 1)

            def body(t, par, prev, cur, nxt):
                if nxt:
                    act.wait_ge(s["xn_turned"], t + 2)
                    after(act, s["mixed_ready"], t)
                    act.copy(xs[1 - par][:, 1:seq + 1], px[:]).then_inc(s["xs_ready"], 1)
                if cur:
                    act.wait_ge(s["proj_done"], t + 1)
                    after(act, s["o_ready"], t)
                    act.activation(th[:], pr[:], ACT.Tanh, scale=0.5).then_inc(s["th_ready"], 1)
                    act.wait_ge(s["kmin_ready"], t + 1)
                    act.activation(kc[:], kmin[:], ACT.Exp).then_inc(s["kc_ready"], 1)

            slots(act, n, body)

        @block.vector
        def _(v):
            for i in range(2):
                v.memset(xs[i][:, 0:1], 0.0)
            v.memset(sk[:, 0:1], 0.0)
            v.memset(skv[:, 0:1], 0.0)
            v.wait_ge(s["loaded"], LOADS)
            v.tensor_scalar(omix[:], mix[:], -1.0, 1.0, ALU.mult, ALU.add)
            v.wait_ge(s["setup"], 1)
            v.tensor_copy(decays[:], decay[:].to_broadcast([P, seq])).then_inc(s["set_chain"], 1)
            v.wait_ge(s["set_chain"], 2)
            ch = Chain(v, s["chain"], 5, s["turn"])

            def body(t, par, prev, cur, nxt):
                if nxt:
                    after(v, s["xn_turned"], t + 1)
                    for j in range(R):
                        i = (t + 1) * R + j
                        m = v.tensor_scalar(xn[:, j, :], K.X[:, i, :], K.mean[:, i, :], K.rstd[:, i, :],
                                            ALU.subtract, ALU.mult)
                    m.then_inc(s["xn_ready"], 1)
                if not cur:
                    return
                v.wait_ge(s["xs_ready"], t + 1)
                for i in range(3):
                    m = v.tensor_scalar(part[:, i, :], xs[par][:, 1:seq + 1], mix[:, i:i + 1], None, ALU.mult)
                m.then_inc(s["parts"], 1)
                v.wait_ge(s["parts"], t + 1)
                for i in range(3):
                    m = v.scalar_tensor_tensor(mixed[:, i, :], xs[par][:, 0:seq], omix[:, i:i + 1], part[:, i, :],
                                               ALU.mult, ALU.add)
                m.then_inc(s["mixed_ready"], 1)
                v.wait_ge(s["proj_done"], t + 1)
                v.tensor_scalar(kmin[:], pkv[:, 0, :], CLAMP, None, ALU.min).then_inc(s["kmin_ready"], 1)
                v.wait_ge(s["kc_ready"], t + 1)
                v.tensor_tensor_scan(sk[:, 1:seq + 1], decays[:], kc[:], 0.0, ALU.mult, ALU.add)
                ch.begin(t)
                ch.step(v.tensor_tensor(kv[:], kc[:], pkv[:, 1, :], ALU.mult))
                v.scalar_tensor_tensor(den[:], kc[:], first[:], sk[:, 0:seq], ALU.mult, ALU.add)
                ch.step(v.tensor_tensor_scan(skv[:, 1:seq + 1], decays[:], kv[:], 0.0, ALU.mult, ALU.add))
                v.tensor_scalar(den[:], den[:], KEPS, None, ALU.add)
                ch.step(v.scalar_tensor_tensor(num[:], kv[:], first[:], skv[:, 0:seq], ALU.mult, ALU.add))
                v.wait_ge(s["th_ready"], t + 1)
                v.scalar_tensor_tensor(num[:], th[:], 1.0, num[:], ALU.add, ALU.mult)
                ch.step(v.reciprocal(inv[:], den[:]))
                v.scalar_tensor_tensor(o[:], num[:], 0.5, inv[:], ALU.mult, ALU.mult).then_inc(s["o_ready"], 1)
                v.wait_ge(s["out_done"], t + 1)
                ch.step_apart(v.tensor_tensor(K.X[:, bass.ds(t * R, R), :], pO[:], K.X[:, bass.ds(t * R, R), :], ALU.add))
                for j in range(R):
                    m = v.bn_stats(K.stats[:, t * R + j, :], K.X[:, t * R + j, :])
                m.then_inc(s["x_done"], 1)
                ch.end()

            slots(v, n, body)



HEADS_A_GROUP = 4
ROWS = P // HEADS_A_GROUP


def l1_ffn(nc, K, T, seq, name):
    with ExitStack() as c:
        Y = c.enter_context(nc.sbuf_tensor(f"Y_{name}", [P, K.tiles, D], F32))
        l1_attention(nc, K, Y, T, seq, name + "a")
        norm_phase(nc, K, name + "n")
        l1_experts(nc, K, Y, T, name + "e")


def l1_attention(nc, K, Y, T, seq, name):
    H, HD = T["L1_ffn_scale_w"].shape
    R = seq // P
    assert R == 2 and H * HD == D and 3 * HD < ROWS
    n = K.tiles // R
    NG = H // HEADS_A_GROUP
    HG = HEADS_A_GROUP
    MAXROW = 3 * HD
    SM = float(HD) ** -0.5
    with ExitStack() as c:
        sb = lambda nm, s, dt=F32: c.enter_context(nc.sbuf_tensor(f"{nm}_{name}", s, dt))
        ps = lambda nm, s, dt=F32: c.enter_context(nc.psum_tensor(f"{nm}_{name}", s, dt))
        raw = sb("raw", [P, 2, D])
        wq, wk, wz = sb("wq", [P, H, ROWS]), sb("wk", [P, H, ROWS]), sb("wz", [P, H, ROWS])
        wv, wo, wgate, gb = sb("wv", [P, D]), sb("wo", [P, D]), sb("wgate", [P, D]), sb("gb", [P, 1])
        sw, swq, swsum = sb("sw", [P, H, HD]), sb("swq", [P, H, HD]), sb("swsum", [P, H])
        rows = sb("rows", [P, ROWS])
        qlow, klow, one = sb("qlow", [P, 1]), sb("klow", [P, 1]), sb("one", [P, 1])
        xn, xT = sb("xn", [P, R, D]), sb("xT", [P, seq])
        th, qs = sb("th", [P, NG, seq]), sb("qs", [P, NG, seq])
        qr, kr = sb("qr", [P, NG, seq], F32R), sb("kr", [P, NG, seq], F32R)
        qa = [sb(f"qa{i}", [P, NG, seq], F32R) for i in range(2)]
        kw = [sb(f"kw{i}", [P, NG, seq], F32R) for i in range(2)]
        qb = [sb(f"qb{i}", [P, NG, seq], F32R) for i in range(2)]
        keysD = [sb(f"keysD{i}", [P, NG, HG, seq], F32R) for i in range(2)]
        vnew = sb("vnew", [P, seq])
        va = [sb(f"va{i}", [P, R, H, ROWS]) for i in range(2)]
        nmax, mx = sb("nmax", [P, NG, R, HG]), sb("mx", [P, R, H, ROWS])
        probs = [sb(f"probs{i}", [P, R, seq]) for i in range(2)]
        av = sb("av", [P, NG, seq])
        rden, on, onT = sb("rden", [P, R, H]), sb("on", [P, R, D]), sb("onT", [P, seq])
        tg, og = sb("tg", [P, seq]), sb("og", [P, seq])
        p1 = [ps(f"p1{i}", [P, 2, seq]) for i in range(2)]
        p2 = [ps(f"p2{i}", [P, R, seq]) for i in range(2)]
        pav = ps("pav", [P, NG, seq])
        pA = ps("pA", [P, 2, seq])
        pB = ps("pB", [P, 2, seq])
        s = c.enter_context(semaphores(nc, name, (
            "loaded", "set_chain", "pool_chain", "w_set", "zeros_set", "xn_ready", "xn_turned", "xT_ready", "z_done",
            "th_ready", "q_done", "qs_ready", "qr_ready", "qa_ready", "k_done", "kr_ready", "kw_ready", "keys_ready",
            "v_done", "v_ready", "va_ready", "smax_done", "nmax_done", "mx_ready", "mx_turned", "qb_ready",
            "scores_done", "exp_done", "av_done", "av_ready", "av_turned", "rden_ready", "on_ready", "on_turned",
            "onT_ready", "gate_done", "tg_ready", "og_ready", "attn_done", "y_written", "y_done", "turn", "pturn")))
        block = c.enter_context(nc.Block())
        LOADS = 16 * 7

        @block.sync
        def _(sp):
            sp.dma_start(raw[:, 0, :], T["L1_ffn_q_w"]).then_inc(s["loaded"], 16)
            sp.dma_start(raw[:, 1, :], T["L1_ffn_k_w"]).then_inc(s["loaded"], 16)
            sp.dma_start(wv[:], T["L1_ffn_v_w"]).then_inc(s["loaded"], 16)
            sp.dma_start(wo[:], T["L1_ffn_out_w"]).then_inc(s["loaded"], 16)
            sp.dma_start(wgate[:], T["L1_ffn_gate_w"]).then_inc(s["loaded"], 16)
            sp.dma_start(gb[:], T["L1_ffn_gate_b"].rearrange("(d a) -> d a", a=1)).then_inc(s["loaded"], 16)
            sp.dma_start(sw[:], T["L1_ffn_scale_w"].rearrange("(a h) d -> a h d", a=1).to_broadcast([P, H, HD])).then_inc(s["loaded"], 16)

        @block.gpsimd
        def _(pool):
            pool.memset(rows[:], 0.0)
            for k in range(2):
                pool.memset(keysD[k][:].bitcast(F32), 0.0)
                pool.memset(va[k][:], 0.0)
            pool.memset(mx[:], 0.0).then_inc(s["pool_chain"], 1)
            for h in range(HG):
                pool.wait_ge(s["pool_chain"], h + 1)
                pool.affine_select(out=rows[:], in_=rows[:], compare_op=ALU.not_equal, fill=1.0, base=-ROWS * h,
                                   pattern=[[-1, ROWS]], channel_multiplier=1).then_inc(s["pool_chain"], 1)

            def body(t, par, prev, cur, nxt, pre):
                for g in range(NG if pre else 0):
                    pool.wait_ge(s["kw_ready"], 2 * (t + 2) + g // 2 + 1)
                    after(pool, s["exp_done"], t * H + HG * (g + 1) if cur else 0)
                    pool.sem_inc(s["pturn"], 1)
                    for i in range(HG):
                        m = pool.tensor_copy(keysD[par][ROWS * i:ROWS * (i + 1), g, i, :],
                                             kw[par][ROWS * i:ROWS * (i + 1), g, :])
                    m.then_inc(s["keys_ready"], 1)

            slots(pool, n, body, ahead=2)

        assert H == 16 and NG * 4 == H

        @block.tensor
        def _(pe):
            def project(w, half):
                for g in range(2):
                    k = (2 * half + g) * HG
                    m = pe.matmul(pA[:, g, :], w[:, k:k + HG, :], xT[:], start=True, stop=True)
                return m

            def form_max(t, par, u):
                g, pair, r = u // 4, u // 2 % 2, u % 2
                if u % 4 == 0:
                    if g % 2 == 0:
                        pe.wait_ge(s["qa_ready"], 2 * t + g // 2 + 1)
                    pe.wait_ge(s["keys_ready"], NG * t + g + 1)
                after(pe, s["nmax_done"], t * 16 + u - 1)
                pe.matmul(p1[u % 2][:], qa[par][:, g, r * P:(r + 1) * P], keysD[par][:, g, 2 * pair:2 * pair + 2, :],
                          start=True, stop=True).then_inc(s["smax_done"], 1)

            def turn_max(t, g):
                pe.wait_ge(s["mx_ready"], t * NG + g + 1)
                for r in range(R):
                    m = pe.transpose(pB[:, 1, r * P:(r + 1) * P], mx[:, r, g * HG:(g + 1) * HG, :], K.ident[:])
                m.then_inc(s["mx_turned"], 1)

            def scores(t, par, h):
                g, i, k = h // HG, h % HG, t * H + h
                if i == 0:
                    pe.wait_ge(s["qb_ready"], t * NG + g + 1)
                after(pe, s["exp_done"], k - 1)
                for kt in range(R):
                    m = pe.matmul(p2[h % 2][:, kt, :], keysD[par][:, g, i, kt * P:(kt + 1) * P], qb[par][:, g, :],
                                  start=True, stop=True)
                m.then_inc(s["scores_done"], 1)

            def weigh(t, par, h):
                g, i, k = h // HG, h % HG, t * H + h
                pe.wait_ge(s["exp_done"], k + 1)
                if h == 0:
                    after(pe, s["av_ready"], t)
                    pe.wait_ge(s["va_ready"], t + 1)
                for kt in range(R):
                    m = pe.matmul(pav[ROWS * i:ROWS * (i + 1), g, :], va[par][:, kt, h, :], probs[h % 2][:, kt, :],
                                  start=(kt == 0), stop=(kt == R - 1))
                m.then_inc(s["av_done"], 1)

            def first_stage(t, b):
                if b == 1:
                    pe.wait_ge(s["xn_ready"], t + 1)
                    after(pe, s["v_ready"], t)
                    for r in range(R):
                        m = pe.transpose(pA[:, 0, r * P:(r + 1) * P], xn[:, r, :], K.ident[:])
                    m.then_inc(s["xn_turned"], 1)
                elif b in (2, 3):
                    pe.wait_ge(s["xT_ready"], t + 1) if b == 2 else pe.wait_ge(s["th_ready"], 2 * t + 1)
                    project(wz, b - 2).then_inc(s["z_done"], 1)
                elif b == 4:
                    pe.wait_ge(s["th_ready"], 2 * t + 2)
                    project(wq, 0).then_inc(s["q_done"], 1)
                elif b == 6:
                    pe.wait_ge(s["qs_ready"], 2 * t + 1)
                    project(wq, 1).then_inc(s["q_done"], 1)
                elif b == 8:
                    pe.wait_ge(s["qs_ready"], 2 * t + 2)
                    project(wk, 0).then_inc(s["k_done"], 1)
                elif b == 10:
                    pe.wait_ge(s["kw_ready"], 2 * t + 1)
                    project(wk, 1).then_inc(s["k_done"], 1)
                elif b == 12:
                    pe.wait_ge(s["kw_ready"], 2 * t + 2)
                    for r in range(R):
                        m = pe.matmul(pA[:, 0, r * P:(r + 1) * P], xT[:, r * P:(r + 1) * P], wv[:], start=True, stop=True)
                    m.then_inc(s["v_done"], 1)

            def last_stage(t, b):
                if b in (2, 3):
                    r = b - 2
                    pe.wait_ge(s["av_ready"], t + 1)
                    if b == 3:
                        pe.wait_ge(s["on_ready"], 2 * t + 1)
                    for g in range(NG):
                        m = pe.transpose(pB[:, g // 2, g % 2 * P:(g % 2 + 1) * P], av[:, g, r * P:(r + 1) * P], K.ident[:])
                    m.then_inc(s["av_turned"], 1)
                elif b == 4:
                    pe.wait_ge(s["on_ready"], 2 * t + 2)
                    for r in range(R):
                        m = pe.transpose(pB[:, 0, r * P:(r + 1) * P], on[:, r, :], K.ident[:])
                    m.then_inc(s["on_turned"], 1)
                elif b == 6:
                    pe.wait_ge(s["onT_ready"], t + 1)
                    pe.matmul(pB[:, 0, :], wgate[:], onT[:], start=True, stop=True).then_inc(s["gate_done"], 1)
                elif b == 8:
                    pe.wait_ge(s["og_ready"], t + 1)
                    for r in range(R):
                        m = pe.matmul(pB[:, 0, r * P:(r + 1) * P], og[:, r * P:(r + 1) * P], wo[:], start=True, stop=True)
                    m.then_inc(s["attn_done"], 1)

            def body(t, par, prev, cur, nxt, pre):
                for b in range(H):
                    if cur:
                        scores(t, par, b)
                    if nxt:
                        form_max(t + 1, 1 - par, b)
                    if cur and b >= 1:
                        weigh(t, par, b - 1)
                    if cur and b == 1:
                        after(pe, s["y_written"], t - 1)
                        pe.wait_ge(s["qb_ready"], NG * t + NG - 1)
                        turn_max(t, NG - 1)
                    if prev:
                        if b == 2:
                            if cur:
                                pe.wait_ge(s["qb_ready"], NG * (t + 1))
                            else:
                                pe.wait_ge(s["y_written"], t - 1)
                        if b == 6 and nxt:
                            pe.wait_ge(s["qb_ready"], NG * (t + 1) + 1)
                        last_stage(t - 1, b)
                    if nxt and b in (5, 9, 13):
                        if prev:
                            if b == 5:
                                pe.wait_ge(s["onT_ready"], t)
                            elif b == 9:
                                pe.wait_ge(s["y_written"], t)
                        after(pe, s["qb_ready"], NG * (t + 1) + (b - 5) // 4)
                        turn_max(t + 1, (b - 5) // 4)
                    if pre:
                        first_stage(t + 2, b)
                if cur:
                    weigh(t, par, H - 1)

            pe.wait_ge(s["loaded"], LOADS)
            pe.wait_ge(s["w_set"], 1)
            slots(pe, n, body, ahead=2)

        @block.scalar
        def _(act):
            act.wait_ge(s["w_set"], 1)

            def first_stage(t, b):
                if b == 1:
                    act.wait_ge(s["xn_turned"], t + 1)
                    after(act, s["v_done"], t)
                    act.copy(xT[:], pA[:, 0, :]).then_inc(s["xT_ready"], 1)
                elif b in (2, 3):
                    f = slice(2 * (b - 2), 2 * (b - 2) + 2)
                    act.wait_ge(s["z_done"], 2 * t + b - 1)
                    act.activation(th[:, f, :], pA[:], ACT.Tanh, scale=0.5).then_inc(s["th_ready"], 1)
                elif b in (5, 7):
                    half = (b - 5) // 2
                    act.wait_ge(s["qs_ready"], 2 * t + half + 1)
                    act.copy(qr[:, 2 * half:2 * half + 2, :], qs[:, 2 * half:2 * half + 2, :]).then_inc(s["qr_ready"], 1)
                elif b in (8, 10):
                    half = (b - 8) // 2
                    act.wait_ge(s["k_done"], 2 * t + half + 1)
                    act.activation(kr[:, 2 * half:2 * half + 2, :], pA[:], ACT.Identity, bias=one[:]).then_inc(s["kr_ready"], 1)

            def last_stage(t, b):
                if b == 0:
                    act.wait_ge(s["av_done"], (t + 1) * H)
                    after(act, s["av_turned"], 2 * t)
                    act.copy(av[:], pav[:]).then_inc(s["av_ready"], 1)
                elif b == 4:
                    act.wait_ge(s["on_turned"], t + 1)
                    act.copy(onT[:], pB[:, 0, :]).then_inc(s["onT_ready"], 1)
                elif b == 6:
                    act.wait_ge(s["gate_done"], t + 1)
                    act.activation(tg[:], pB[:, 0, :], ACT.Tanh, bias=gb[:], scale=0.5).then_inc(s["tg_ready"], 1)

            def body(t, par, prev, cur, nxt, pre):
                for b in range(H):
                    if prev:
                        last_stage(t - 1, b) if b == 0 else None
                    if cur:
                        k = t * H + b
                        act.wait_ge(s["scores_done"], k + 1)
                        after(act, s["av_done"], k - 1)
                        act.activation(probs[b % 2][:], p2[b % 2][:], ACT.Exp, scale=SM).then_inc(s["exp_done"], 1)
                    if prev and b:
                        last_stage(t - 1, b)
                    if pre:
                        first_stage(t + 2, b)

            slots(act, n, body, ahead=2)

        @block.vector
        def _(v):
            setup = Chain(v, s["set_chain"], 2)
            setup.begin(0)
            v.wait_ge(s["loaded"], LOADS)
            v.wait_ge(s["pool_chain"], HG + 1)
            v.memset(wq[:], 0.0)
            v.memset(wk[:], 0.0)
            v.memset(wz[:], 0.0)
            for i in range(2):
                v.memset(va[i][:, :, :, HD:HD + 1], 1.0)
            v.tensor_scalar(wo[:], wo[:], 0.5, None, ALU.mult)
            v.tensor_scalar(gb[:], gb[:], 0.5, None, ALU.mult)
            v.tensor_reduce(qlow[:], rows[:, HD:2 * HD], AX.X, ALU.add, negate=True)
            v.tensor_reduce(klow[:], rows[:, 2 * HD:3 * HD], AX.X, ALU.add, negate=True)
            v.tensor_copy(one[:], rows[:, MAXROW:MAXROW + 1])
            setup.step(v.tensor_tensor(swq[:], sw[:], raw[:, 0, :].rearrange("p (h d) -> p h d", h=H), ALU.mult))
            v.tensor_tensor(klow[:], klow[:], one[:], ALU.add)
            setup.step(v.tensor_reduce(swsum[:], swq[:], AX.X, ALU.add))
            for r in range(3):
                v.tensor_copy(wq[:, :, r * HD:(r + 1) * HD], raw[:, 0, :].rearrange("p (h d) -> p h d", h=H))
                v.tensor_copy(wk[:, :, r * HD:(r + 1) * HD], raw[:, 1, :].rearrange("p (h d) -> p h d", h=H))
                m = v.tensor_copy(wz[:, :, r * HD:(r + 1) * HD], swsum[:, :, None].to_broadcast([P, H, HD]))
            m.then_inc(s["w_set"], 1)

            def first_stage(t, par, b):
                if b == 0:
                    after(v, s["xn_turned"], t)
                    for r in range(R):
                        for dst in (Y[:, t * R + r, :], xn[:, r, :]):
                            m = v.tensor_scalar(dst, K.X[:, t * R + r, :], K.mean[:, t * R + r, :],
                                                K.rstd[:, t * R + r, :], ALU.subtract, ALU.mult)
                    m.then_inc(s["xn_ready"], 1)
                elif b in (4, 6):
                    i = (b - 4) // 2
                    v.wait_ge(s["q_done"], 2 * t + i + 1)
                    after(v, s["qr_ready"], 2 * t)
                    v.scalar_tensor_tensor(qs[:, 2 * i:2 * i + 2, :], th[:, 2 * i:2 * i + 2, :], 1.0, pA[:],
                                           ALU.add, ALU.mult).then_inc(s["qs_ready"], 1)
                elif b in (7, 10):
                    i = (b - 7) // 3
                    v.wait_ge(s["qr_ready"], 2 * t + i + 1)
                    after(v, s["qb_ready"], NG * (t - 1))
                    v.scalar_tensor_tensor(qa[par][:, 2 * i:2 * i + 2, :], qr[:, 2 * i:2 * i + 2, :].bitcast(F32), qlow[:],
                                           qs[:, 2 * i:2 * i + 2, :], ALU.mult, ALU.add).then_inc(s["qa_ready"], 1)
                elif b in (9, 11):
                    i = (b - 9) // 2
                    v.wait_ge(s["kr_ready"], 2 * t + i + 1)
                    after(v, s["keys_ready"], NG * (t - 1))
                    v.scalar_tensor_tensor(kw[par][:, 2 * i:2 * i + 2, :], kr[:, 2 * i:2 * i + 2, :].bitcast(F32), klow[:],
                                           pA[:], ALU.mult, ALU.add).then_inc(s["kw_ready"], 1)

            def values(t):
                v.wait_ge(s["v_done"], t + 1)
                after(v, s["va_ready"], t)
                v.tensor_copy(vnew[:], pA[:, 0, :]).then_inc(s["v_ready"], 1)

            def place_values(t, par):
                v.wait_ge(s["v_ready"], t + 1)
                after(v, s["av_done"], H * (t - 1))
                v.tensor_copy(va[par][:, :, :, 0:HD],
                              vnew[:].rearrange("p (r h d) -> p r h d", r=R, h=H)).then_inc(s["va_ready"], 1)

            def last_stage(t, b):
                if b in (2, 3):
                    r = b - 2
                    pv = pB[:].rearrange("p a (h w) -> p (a h) w", w=ROWS)
                    v.wait_ge(s["av_turned"], 2 * t + r + 1)
                    v.reciprocal(rden[:, r, :], pv[:, :, HD]).then_inc(s["rden_ready"], 1)
                    v.wait_ge(s["rden_ready"], 2 * t + r + 1)
                    v.tensor_tensor(on[:, r, :].rearrange("p (h d) -> p h d", h=H), pv[:, :, 0:HD],
                                    rden[:, r, :, None].to_broadcast([P, H, HD]), ALU.mult).then_inc(s["on_ready"], 1)
                elif b == 7:
                    v.wait_ge(s["tg_ready"], t + 1)
                    v.scalar_tensor_tensor(og[:], tg[:], 1.0, onT[:], ALU.add, ALU.mult).then_inc(s["og_ready"], 1)
                elif b == 8:
                    v.wait_ge(s["attn_done"], t + 1)
                    v.tensor_tensor(Y[:, bass.ds(t * R, R), :], pB[:, 0, :].rearrange("p (r d) -> p r d", r=R),
                                    Y[:, bass.ds(t * R, R), :], ALU.add).then_inc(s["y_written"], 1)
                elif b == 9:
                    v.wait_ge(s["y_written"], t + 1)
                    v.sem_inc(s["turn"], 1)
                    for r in range(R):
                        m = v.bn_stats(K.stats[:, t * R + r, :], Y[:, t * R + r, :])
                    m.then_inc(s["y_done"], 1)

            def maxima(t, u):
                g, pair, r = u // 4, u // 2 % 2, u % 2
                v.wait_ge(s["smax_done"], t * 16 + u + 1)
                v.tensor_reduce(nmax[:, g, r, 2 * pair:2 * pair + 2], p1[u % 2][:], AX.X, ALU.max,
                                negate=True).then_inc(s["nmax_done"], 1)
                if u % 4 == 3:
                    v.wait_ge(s["nmax_done"], t * 16 + u + 1)
                    after(v, s["mx_turned"], NG * (t - 1) + g + 1)
                    v.tensor_copy(mx[:, :, g * HG:(g + 1) * HG, MAXROW], nmax[:, g, :, :]).then_inc(s["mx_ready"], 1)

            def fill(t, par, g):
                v.wait_ge(s["mx_turned"], t * NG + g + 1)
                v.tensor_tensor(qb[par][:, g, :], pB[:, 1, :], qa[par][:, g, :].bitcast(F32), ALU.add).then_inc(s["qb_ready"], 1)

            def body(t, par, prev, cur, nxt, pre):
                for b in range(H):
                    if nxt:
                        maxima(t + 1, b)
                    if b == 1 and cur:
                        fill(t, par, NG - 1)
                    if b == 1 and nxt:
                        place_values(t + 1, 1 - par)
                    if prev:
                        last_stage(t - 1, b)
                    if nxt and b in (5, 9, 13):
                        fill(t + 1, 1 - par, (b - 5) // 4)
                    if pre:
                        first_stage(t + 2, par, b)
                        if b == 12:
                            values(t + 2)

            slots(v, n, body, ahead=2)


def l1_experts(nc, K, Y, T, name):
    E, _, F = T["L1_ffn_w1"].shape
    G = 4
    N = G * P
    n = K.tiles // G
    FC = F // P
    TABS = 3 * F + D + 1
    PAD = 6
    EC = 512 // F
    with ExitStack() as c:
        sb = lambda nm, s, dt=F32: c.enter_context(nc.sbuf_tensor(f"{nm}_{name}", s, dt))
        ps = lambda nm, s, dt=F32: c.enter_context(nc.psum_tensor(f"{nm}_{name}", s, dt))
        w1, w2 = sb("w1", [P, E, F]), sb("w2", [P, FC, E, D])
        wr, br = sb("wr", [P, E]), sb("br", [P, E])
        tabf = sb("tabf", [96, TABS])
        tab3 = sb("tab3", [96, TABS], BF16)
        n1g, n1b, n2g, n2b = (sb(k, [P, D]) for k in ("n1g", "n1b", "n2g", "n2b"))
        iota = sb("iota", [P, E])
        x1 = [sb(f"x1{i}", [P, G, D]) for i in range(2)]
        x1T = [sb(f"x1T{i}", [P, N]) for i in range(2)]
        logit, struck = sb("logit", [P, G, E + PAD]), sb("struck", [P, G, E + PAD])
        top8, index, chosen = sb("top8", [P, G, 8]), sb("index", [P, G, E]), sb("chosen", [P, G])
        dv, ev, den, wsum = sb("dv", [P, G]), sb("ev", [P, G]), sb("den", [P, G]), [sb(f"wsum{i}", [P, G]) for i in range(2)]
        hot = [sb(f"hot{i}", [P, G, E]) for i in range(2)]
        hot3 = sb("hot3", [P, G, 96], BF16)
        hotT = [sb(f"hotT{i}", [96, N], BF16) for i in range(2)]
        tab = [sb(f"tab{i}", [P, G, TABS]) for i in range(2)]
        h = sb("h", [P, G, F])
        hodd = [sb(f"hodd{i}", [P, F]) for i in range(2)]
        gl = sb("gl", [P, G, F])
        glT = sb("glT", [P, FC, N])
        st, mean, var, rstd, tt = sb("st", [P, G, 6]), sb("mean", [P, G, 1]), sb("var", [P, G, 1]), sb("rstd", [P, G, 1]), sb("tt", [P, G, 1])
        y, yodd = sb("y", [P, G, D]), [sb(f"yodd{i}", [P, D]) for i in range(2)]
        ph = [ps(f"ph{i}", [P, EC, F]) for i in range(2)]
        pt = ps("pt", [P, 2, 512])
        py = ps("py", [P, 2, 4, D])
        pm = ps("pm", [P, N])
        pmb = pm[:].bitcast(BF16)
        s = c.enter_context(semaphores(nc, name, (
            "loaded", "pool_chain", "set_chain", "w_set", "x1_ready", "x1_turned", "x1T_ready", "logits_done", "dv_ready",
            "ev_ready", "hot_ready", "hot_turned", "hotT_ready", "tab_done", "tab_ready", "h_done", "h_read", "h_chain",
            "h_ready", "gl_ready", "gl_turned", "glT_ready", "y_done", "y_read", "y_chain", "norm_chain", "route_chain",
            "fin_chain", "x_done", "turn", "hsum", "ysum", "pre_chain")))
        block = c.enter_context(nc.Block())
        tabs_d = [("L1_ffn_b1", 0, F), ("L1_ffn_ln_g", F, F), ("L1_ffn_ln_b", 2 * F, F), ("L1_ffn_b2", 3 * F, D)]
        LOADS = 16 * (4 + 3 * 5 + 5)

        @block.sync
        def _(sp):
            sp.dma_start(w1[:], T["L1_ffn_w1"].rearrange("e d f -> d e f")).then_inc(s["loaded"], 16)
            sp.dma_start(wr[:], T["L1_ffn_moe_gate_w"]).then_inc(s["loaded"], 16)
            sp.dma_start(w2[:, 0, :, :], T["L1_ffn_w2"][:, 0:P, :].rearrange("e f d -> f e d")).then_inc(s["loaded"], 16)
            for dst, k in ((br, "moe_gate_b"), (n1g, "n1_g"), (n1b, "n1_b"), (n2g, "n2_g"), (n2b, "n2_b")):
                sp.dma_start(dst[:], T[f"L1_ffn_{k}"].rearrange("(a d) -> a d", a=1).to_broadcast([P, dst.shape[1]])).then_inc(s["loaded"], 16)

        @block.gpsimd
        def _(pool):
            pool.memset(tabf[:], 0.0).then_inc(s["pool_chain"], 1)
            pool.memset(hot3[:], 0.0)
            pool.iota(iota[:], pattern=[[1, E]], base=0, channel_multiplier=0, allow_small_or_imprecise_dtypes=True).then_inc(s["pool_chain"], 1)

        @block.tensor
        def _(pe):
            pe.wait_ge(s["w_set"], 1)

            def first(t, par, j):
                after(pe, s["tab_ready"], t * G + j)
                if j == 0:
                    pe.wait_ge(s["hotT_ready"], t + 1)
                pe.matmul(pt[:, 0, :], hotT[par][:, j * P:(j + 1) * P], tab3[:, 0:512], start=True, stop=True)
                pe.matmul(pt[:, 1, 0:TABS - 512], hotT[par][:, j * P:(j + 1) * P], tab3[:, 512:TABS], start=True,
                          stop=True).then_inc(s["tab_done"], 1)
                for b in range(E // EC):
                    k = (t * G + j) * (E // EC) + b
                    after(pe, s["h_read"], k - 1)
                    pe.matmul(ph[b % 2][:], x1T[par][:, j * P:(j + 1) * P], w1[:, EC * b:EC * (b + 1), :], start=True,
                              stop=True).then_inc(s["h_done"], 1)

            def second(t, j):
                for b in range(2):
                    k = (t * G + j) * 2 + b
                    after(pe, s["y_read"], k - 1)
                    for k2 in range(FC):
                        m = pe.matmul(py[:, b, :, :], glT[:, k2, j * P:(j + 1) * P], w2[:, k2, 4 * b:4 * b + 4, :],
                                      start=(k2 == 0), stop=(k2 == FC - 1))
                    m.then_inc(s["y_done"], 1)

            def body(t, par, prev, cur, nxt):
                for j in range(G):
                    if cur:
                        first(t, par, j)
                    if prev and j == 0:
                        pe.wait_ge(s["gl_ready"], t)
                        after(pe, s["y_read"], (t - 1) * G * 2)
                        for k2 in range(FC):
                            for q in range(G):
                                m = pe.transpose(py[:, k2, q, :], gl[:, q, k2 * P:(k2 + 1) * P], K.ident[:])
                        m.then_inc(s["gl_turned"], 1)
                        pe.wait_ge(s["glT_ready"], t)
                    if prev and j < 2:
                        second(t - 1, 2 * j)
                        second(t - 1, 2 * j + 1)
                    if nxt and j == 2:
                        pe.wait_ge(s["x1_ready"], t + 2)
                        after(pe, s["hotT_ready"], t + 1)
                        for q in range(G):
                            m = pe.transpose(pm[:, q * P:(q + 1) * P], x1[1 - par][:, q, :], K.ident[:])
                        m.then_inc(s["x1_turned"], 1)
                if nxt:
                    pe.wait_ge(s["x1T_ready"], t + 2)
                    for q in range(G):
                        m = pe.matmul(pm[:, q * E:(q + 1) * E], x1T[1 - par][:, q * P:(q + 1) * P], wr[:], start=True, stop=True)
                    m.then_inc(s["logits_done"], 1)
                    pe.wait_ge(s["hot_ready"], t + 2)
                    for q in range(G):
                        m = pe.transpose(pmb[0:96, q * P:(q + 1) * P], hot3[:, q, :], K.identb[:])
                    m.then_inc(s["hot_turned"], 1)

            slots(pe, n, body)

        @block.scalar
        def _(act):
            act.dma_start(w2[:, 1, :, :], T["L1_ffn_w2"][:, P:2 * P, :].rearrange("e f d -> f e d")).then_inc(s["loaded"], 16)
            act.wait_ge(s["pool_chain"], 2)
            for q in range(3):
                for k, o, w in tabs_d:
                    act.dma_start(tabf[32 * q:32 * q + E, o:o + w], T[k]).then_inc(s["loaded"], 16)
                act.dma_start(tabf[32 * q:32 * q + E, TABS - 1:TABS], T["L1_ffn_res_scale"].rearrange("(e a) -> e a", a=1)).then_inc(s["loaded"], 16)

            def body(t, par, prev, cur, nxt):
                for j in range(G):
                    if cur:
                        act.wait_ge(s["tab_done"], t * G + j + 1)
                        act.copy(tab[par][:, j, 0:512], pt[:, 0, :])
                        act.copy(tab[par][:, j, 512:TABS], pt[:, 1, 0:TABS - 512]).then_inc(s["tab_ready"], 1)
                    if prev and j == 0:
                        act.wait_ge(s["gl_turned"], t)
                        after(act, s["y_done"], (t - 1) * G * 2)
                        act.copy(glT[:], py[:].rearrange("p c q d -> p c (q d)")).then_inc(s["glT_ready"], 1)
                    if nxt and j == 2:
                        act.wait_ge(s["x1_turned"], t + 2)
                        act.copy(x1T[1 - par][:], pm[:]).then_inc(s["x1T_ready"], 1)
                if nxt:
                    act.wait_ge(s["dv_ready"], t + 2)
                    act.activation(ev[:], dv[:], ACT.Exp).then_inc(s["ev_ready"], 1)
                    act.wait_ge(s["hot_turned"], t + 2)
                    act.copy(hotT[1 - par][:], pmb[0:96, 0:N]).then_inc(s["hotT_ready"], 1)
                if cur:
                    act.wait_ge(s["h_ready"], t + 1)
                    act.activation(gl[:], h[:], ACT.Gelu).then_inc(s["gl_ready"], 1)

            slots(act, n, body)

        @block.vector
        def _(v):
            v.memset(logit[:], BIG)
            v.wait_ge(s["loaded"], LOADS)
            setup = Chain(v, s["set_chain"], 4)
            setup.begin(0)
            v.wait_ge(s["pool_chain"], 2)
            lo, hi = slice(32, 64), slice(64, 96)
            setup.step(v.tensor_copy(tab3[:], tabf[:]))
            v.tensor_tensor(tabf[lo, :], tabf[lo, :], tab3[lo, :], ALU.subtract)
            setup.step(v.tensor_tensor(tabf[hi, :], tabf[hi, :], tab3[hi, :], ALU.subtract))
            v.tensor_copy(tab3[lo, :], tabf[lo, :])
            setup.step(v.tensor_copy(tab3[hi, :], tabf[hi, :]))
            setup.step(v.tensor_tensor(tabf[hi, :], tabf[hi, :], tab3[hi, :], ALU.subtract))
            v.tensor_copy(tab3[hi, :], tabf[hi, :]).then_inc(s["w_set"], 1)
            hch = Chain(v, s["norm_chain"], 1 + MOMENT_STEPS + RSQRT_STEPS + 2, s["turn"])
            fch = Chain(v, s["fin_chain"], 3 + MOMENT_STEPS + RSQRT_STEPS + 5, s["turn"])
            rch = Chain(v, s["route_chain"], 9, s["turn"])
            pch = Chain(v, s["pre_chain"], 2)

            def pick_h(t, par, j):
                v.wait_ge(s["tab_ready"], t * G + j + 1)
                if j == 0:
                    after(v, s["gl_ready"], t)
                for b in range(E // EC):
                    k = (t * G + j) * (E // EC) + b
                    v.wait_ge(s["h_done"], k + 1)
                    if b:
                        v.wait_ge(s["h_read"], k)
                    e = EC * b
                    src = ph[b % 2]
                    v.scalar_tensor_tensor(h[:, j, :], src[:, 0, :], hot[par][:, j, e:e + 1],
                                           tab[par][:, j, 0:F] if b == 0 else h[:, j, :], ALU.mult, ALU.add)
                    if b == 0:
                        m = v.tensor_scalar(hodd[j % 2][:], src[:, 1, :], hot[par][:, j, e + 1:e + 2], None, ALU.mult)
                    else:
                        m = v.scalar_tensor_tensor(hodd[j % 2][:], src[:, 1, :], hot[par][:, j, e + 1:e + 2], hodd[j % 2][:], ALU.mult, ALU.add)
                    m.then_inc(s["h_read"], 1)
                v.wait_ge(s["h_read"], (t * G + j + 1) * (E // EC))
                v.tensor_tensor(h[:, j, :], h[:, j, :], hodd[j % 2][:], ALU.add).then_inc(s["hsum"], 1)

            def pick_y(t, par, j):
                tb = tab[par]
                for b in range(2):
                    k = (t * G + j) * 2 + b
                    v.wait_ge(s["y_done"], k + 1)
                    for q in range(0, 4, 2):
                        e = 4 * b + q
                        first = b == 0 and q == 0
                        if not first:
                            v.wait_ge(s["y_chain"], (t * G + j) * 4 + 2 * b + q // 2)
                        v.scalar_tensor_tensor(y[:, j, :], py[:, b, q, :], hot[par][:, j, e:e + 1],
                                               tb[:, j, 3 * F:3 * F + D] if first else y[:, j, :], ALU.mult, ALU.add)
                        if first:
                            m = v.tensor_scalar(yodd[j % 2][:], py[:, b, q + 1, :], hot[par][:, j, e + 1:e + 2], None, ALU.mult)
                        else:
                            m = v.scalar_tensor_tensor(yodd[j % 2][:], py[:, b, q + 1, :], hot[par][:, j, e + 1:e + 2], yodd[j % 2][:], ALU.mult, ALU.add)
                        m.then_inc(s["y_chain"], 1)
                    v.wait_ge(s["y_chain"], (t * G + j) * 4 + 2 * b + 2)
                    if b == 0:
                        v.sem_inc(s["y_read"], 1)
                    else:
                        v.tensor_tensor(y[:, j, :], y[:, j, :], yodd[j % 2][:], ALU.add).then_inc(s["y_read"], 1)

            def inner_norm(t, par):
                hch.begin(t)
                v.wait_ge(s["hsum"], (t + 1) * G)
                for j in range(G):
                    m = v.bn_stats(st[:, j, :], h[:, j, :])
                hch.step(m)
                moments(v, hch.step, F, [st[:, :, i:i + 1] for i in range(6)], mean[:], var[:], tt[:])
                rsqrt(v, hch.step, rstd[:], var[:], tt[:])
                for j in range(G):
                    m = v.tensor_scalar(h[:, j, :], h[:, j, :], mean[:, j, :], rstd[:, j, :], ALU.subtract, ALU.mult)
                hch.step(m)
                hch.step(v.tensor_tensor(h[:], h[:], tab[par][:, :, F:2 * F], ALU.mult))
                v.tensor_tensor(h[:], h[:], tab[par][:, :, 2 * F:3 * F], ALU.add).then_inc(s["h_ready"], 1)
                hch.end()

            def finish(t, par):
                fch.begin(t)
                v.wait_ge(s["y_read"], (t + 1) * G * 2)
                for j in range(G):
                    m = v.scalar_tensor_tensor(y[:, j, :], y[:, j, :], tab[par][:, j, TABS - 1:TABS], x1[par][:, j, :], ALU.mult, ALU.add)
                fch.step(m)
                for j in range(G):
                    m = v.scalar_tensor_tensor(y[:, j, :], y[:, j, :], wsum[par][:, j:j + 1], x1[par][:, j, :], ALU.mult, ALU.add)
                fch.step_apart(m)
                for j in range(G):
                    m = v.bn_stats(st[:, j, :], y[:, j, :])
                fch.step(m)
                moments(v, fch.step, D, [st[:, :, i:i + 1] for i in range(6)], mean[:], var[:], tt[:])
                rsqrt(v, fch.step, rstd[:], var[:], tt[:])
                for j in range(G):
                    m = v.tensor_scalar(y[:, j, :], y[:, j, :], mean[:, j, :], rstd[:, j, :], ALU.subtract, ALU.mult)
                fch.step(m)
                fch.step(v.tensor_tensor(y[:], y[:], n2g[:, None, :].to_broadcast([P, G, D]), ALU.mult))
                fch.step(v.tensor_tensor(y[:], y[:], n2b[:, None, :].to_broadcast([P, G, D]), ALU.add))
                fch.step_apart(v.scalar_tensor_tensor(K.X[:, bass.ds(t * G, G), :], y[:], 0.5, K.X[:, bass.ds(t * G, G), :],
                                                      ALU.mult, ALU.add))
                for j in range(G):
                    m = v.bn_stats(K.stats[:, t * G + j, :], K.X[:, t * G + j, :])
                fch.step(m)
                fch.end()

            def norm1(t, par):
                pch.begin(t)
                for j in range(G):
                    m = v.tensor_scalar(x1[par][:, j, :], Y[:, t * G + j, :], K.mean[:, t * G + j, :],
                                        K.rstd[:, t * G + j, :], ALU.subtract, ALU.mult)
                pch.step(m)
                pch.step(v.tensor_tensor(x1[par][:], x1[par][:], n1g[:, None, :].to_broadcast([P, G, D]), ALU.mult))
                v.tensor_tensor(x1[par][:], x1[par][:], n1b[:, None, :].to_broadcast([P, G, D]), ALU.add).then_inc(s["x1_ready"], 1)
                pch.end()

            def top2(t, par):
                rch.begin(t)
                v.wait_ge(s["logits_done"], t + 1)
                rch.step_apart(v.tensor_tensor(logit[:, :, 0:E], pm[:, 0:G * E].rearrange("p (g e) -> p g e", g=G),
                                               br[:, None, :].to_broadcast([P, G, E]), ALU.add))
                for j in range(G):
                    m = v.max(top8[:, j, :], logit[:, j, :])
                rch.step_apart(m)
                for j in range(G):
                    m = v.match_replace(struck[:, j, :], top8[:, j, :], logit[:, j, :], -BIG)
                rch.step(m)
                v.tensor_tensor(dv[:], top8[:, :, 7], top8[:, :, 6], ALU.subtract).then_inc(s["dv_ready"], 1)
                rch.step(v.scalar_tensor_tensor(index[:], struck[:, :, 0:E], -BIG / 2, iota[:, None, :].to_broadcast([P, G, E]),
                                                ALU.is_le, ALU.mult))
                rch.step(v.tensor_reduce(chosen[:], index[:], AX.X, ALU.max))
                rch.step(v.tensor_tensor(hot[par][:], iota[:, None, :].to_broadcast([P, G, E]),
                                         chosen[:, :, None].to_broadcast([P, G, E]), ALU.is_equal))
                for q in range(3):
                    m = v.tensor_copy(hot3[:, :, 32 * q:32 * q + E], hot[par][:])
                m.then_inc(s["hot_ready"], 1)
                v.wait_ge(s["ev_ready"], t + 1)
                rch.step(v.tensor_scalar(den[:], ev[:], 1.0, None, ALU.add))
                rch.step(v.reciprocal(den[:], den[:]))
                rch.step(v.tensor_tensor(wsum[par][:], ev[:], den[:], ALU.mult))
                v.tensor_tensor(wsum[par][:], wsum[par][:], den[:], ALU.add)
                rch.end()

            def body(t, par, prev, cur, nxt):
                for j in range(G):
                    if cur:
                        pick_h(t, par, j)
                    if prev and j < 2:
                        pick_y(t - 1, 1 - par, 2 * j)
                        pick_y(t - 1, 1 - par, 2 * j + 1)
                    if prev and j == 1:
                        finish(t - 1, 1 - par)
                    if nxt and j == 1:
                        norm1(t + 1, 1 - par)
                if nxt:
                    top2(t + 1, 1 - par)
                if cur:
                    inner_norm(t, par)

            slots(v, n, body)



def macaron_kernel(nc, T, out):
    x = T["L0_attn_X"]
    B, S, _ = x.shape
    with ExitStack() as ctx:
        K = Core(nc, ctx, B * S // P)
        load_phase(nc, K, x)
        with ExitStack() as weights:
            l0_ffn_weights(nc, K, weights, T["L0_ffn_classifier_weight"], T["L0_ffn_e_score_correction_bias"],
                           T["L0_ffn_gate_up_proj"], T["L0_ffn_down_proj"])
            norm_phase(nc, K, "n1")
            l0_ffn(nc, K, "f1")
            norm_phase(nc, K, "n2")
            l0_attention(nc, K, T["L0_attn_Wq"], T["L0_attn_Wk"], T["L0_attn_Wv"], S, "a1")
            norm_phase(nc, K, "n3")
            l0_ffn(nc, K, "f2")
        norm_phase(nc, K, "n4")
        l1_ffn(nc, K, T, S, "g1")
        norm_phase(nc, K, "n5")
        rwkv(nc, K, T, S, "r1")
        norm_phase(nc, K, "n6")
        l1_ffn(nc, K, T, S, "g2")
        store_phase(nc, K, out)


def store_phase(nc, K, out):
    with ExitStack() as c:
        s = c.enter_context(semaphores(nc, "store", ("stored",)))
        block = c.enter_context(nc.Block())

        @block.sync
        def _(sp):
            sp.dma_start(out.rearrange("b (t p) d -> p (b t) d", p=P), K.X[:]).then_inc(s["stored"], 16)
            sp.wait_ge(s["stored"], 16)


_INS = ["L0_attn_X", "L0_attn_Wq", "L0_attn_Wk", "L0_attn_Wv", "L0_ffn_classifier_weight",
        "L0_ffn_e_score_correction_bias", "L0_ffn_gate_up_proj", "L0_ffn_down_proj", "L1_attn_xk", "L1_attn_xv",
        "L1_attn_time_decay", "L1_attn_time_first", "L1_attn_time_mix_k", "L1_attn_time_mix_v",
        "L1_attn_time_mix_r", "L1_attn_Wk", "L1_attn_Wv", "L1_attn_Wr", "L1_attn_Wo", "L1_ffn_q_w", "L1_ffn_k_w",
        "L1_ffn_v_w", "L1_ffn_out_w", "L1_ffn_gate_w", "L1_ffn_gate_b", "L1_ffn_scale_w", "L1_ffn_n1_g",
        "L1_ffn_n1_b", "L1_ffn_n2_g", "L1_ffn_n2_b", "L1_ffn_moe_gate_w", "L1_ffn_moe_gate_b", "L1_ffn_w1",
        "L1_ffn_b1", "L1_ffn_ln_g", "L1_ffn_ln_b", "L1_ffn_w2", "L1_ffn_b2", "L1_ffn_res_scale"]


def kernel(**inputs):
    import numpy as _np
    import concourse.bacc as _bacc
    from concourse import mybir as _mybir
    from concourse.bass_utils import run_bass_kernel_spmd as _run

    nc = _bacc.Bacc("TRN2", target_bir_lowering=False, num_devices=1)
    arrays, args = {}, {}
    for name in _INS:
        if name in ("L1_attn_xk", "L1_attn_xv"):
            continue
        a = _np.ascontiguousarray(inputs[name])
        arrays[f"in_{name}_dram"] = a
        args[name] = nc.dram_tensor(f"in_{name}_dram", a.shape, _mybir.dt.from_np(a.dtype), kind="ExternalInput").ap()
    shape = inputs["L0_attn_X"].shape
    out = nc.dram_tensor("out_0_dram", shape, _mybir.dt.float32, kind="ExternalOutput").ap()
    macaron_kernel(nc, args, out)
    r = _run(nc, [arrays], core_ids=[0])
    return r.results[0]["out_0_dram"]
```

```python
from contextlib import ExitStack, contextmanager

import concourse.bass as bass
from concourse import mybir

F32 = mybir.dt.float32
F32R = mybir.dt.float32r
BF16 = mybir.dt.bfloat16
I32 = mybir.dt.int32
ALU = mybir.AluOpType
ACT = mybir.ActivationFunctionType
AX = mybir.AxisListType

P = 128
D = 128
EPS = 1e-5
BIG = 3e38
RSQRT_SEED = 1597463007.0


def after(eng, sem, count):
    if isinstance(count, int) and count <= 0:
        return
    eng.wait_ge(sem, count)


@contextmanager
def semaphores(nc, phase, names):
    sems = [nc.alloc_semaphore(f"{k}_{phase}") for k in names]
    yield dict(zip(names, sems))
    nc.clear_and_free_semaphores(sems)
    nc.all_engine_barrier()


class Chain:

    def __init__(self, eng, sem, per, turn=None):
        self.eng, self.sem, self.per, self.turn = eng, sem, per, turn

    def begin(self, round_):
        self.base, self.n = round_ * self.per, 0

    def step(self, ins):
        self.n += 1
        ins.then_inc(self.sem, 1)
        self.eng.wait_ge(self.sem, self.base + self.n)

    def step_apart(self, ins):
        self.step(ins)
        self.eng.sem_inc(self.turn, 1)

    def end(self):
        assert self.n == self.per, (self.n, self.per)


PEELED = 3


def slots(eng, n, body, ahead=1):
    turns = max(0, (n - ahead - PEELED) // 2)
    looped = range(PEELED, PEELED + 2 * turns)
    more = (True,) * (ahead - 1)
    for t in range(-ahead, n + 1):
        if t not in looped:
            body(t, t % 2, t > 0, 0 <= t < n, *(0 <= t + k < n for k in range(1, ahead + 1)))
        elif t == PEELED:
            with eng.Fori(0, turns) as i:
                body(2 * i + PEELED, PEELED % 2, True, True, True, *more)
                body(2 * i + PEELED + 1, 1 - PEELED % 2, True, True, True, *more)


RSQRT_STEPS = 11


def rsqrt(v, step, y, a, t):
    step(v.tensor_scalar(t.bitcast(I32), a.bitcast(I32), 1, None, ALU.logical_shift_right))
    step(v.tensor_scalar(y.bitcast(I32), t.bitcast(I32), -1.0, RSQRT_SEED, ALU.mult, ALU.add))
    for _ in range(3):
        step(v.scalar_tensor_tensor(t, y, -0.5, y, ALU.mult, ALU.mult))
        step(v.tensor_tensor(t, t, a, ALU.mult))
        step(v.scalar_tensor_tensor(y, t, 1.5, y, ALU.add, ALU.mult))


def moments(v, step, n, st, mean, var, t):
    v.tensor_tensor(mean, st[1], st[4], ALU.add)
    v.tensor_tensor(t, st[1], st[4], ALU.subtract)
    step(v.tensor_tensor(var, st[2], st[5], ALU.add))
    v.scalar_tensor_tensor(t, t, 0.25, t, ALU.mult, ALU.mult)
    v.tensor_scalar(mean, mean, 0.5, None, ALU.mult)
    step(v.tensor_scalar(var, var, 1.0 / n, EPS, ALU.mult, ALU.add))
    step(v.tensor_tensor(var, var, t, ALU.add))


MOMENT_STEPS = 3


class Core:

    def __init__(self, nc, ctx, tiles):
        def sb(name, shape, dt=F32):
            return ctx.enter_context(nc.sbuf_tensor(name, shape, dt))

        self.nc, self.tiles = nc, tiles
        self.X = sb("X", [P, tiles, D])
        self.stats = sb("stats", [P, tiles, 6])
        self.mean = sb("mean", [P, tiles, 1])
        self.rstd = sb("rstd", [P, tiles, 1])
        self.ident = sb("ident", [P, P])
        self.identb = sb("identb", [P, P], BF16)


def load_phase(nc, K, x_dram):
    with ExitStack() as c:
        ones = c.enter_context(nc.sbuf_tensor("ones_sq", [P, P], F32))
        loads = 4 if K.tiles % 4 == 0 else 1
        s = c.enter_context(semaphores(nc, "load", ["ones_set", "ident_set"] + [f"x_loaded{i}" for i in range(loads)]))
        block = c.enter_context(nc.Block())
        per = K.tiles // loads
        xs = x_dram.rearrange("b (t p) d -> p (b t) d", p=P)

        @block.sync
        def _(sp):
            for i in range(loads):
                sp.dma_start(K.X[:, i * per:(i + 1) * per, :], xs[:, i * per:(i + 1) * per, :]).then_inc(s[f"x_loaded{i}"], 16)

        @block.gpsimd
        def _(pool):
            pool.memset(ones[:], 1.0).then_inc(s["ones_set"], 1)
            pool.wait_ge(s["ones_set"], 1)
            pool.affine_select(out=K.ident[:], in_=ones[:], compare_op=ALU.is_equal, fill=0.0, base=0,
                               pattern=[[-1, P]], channel_multiplier=1).then_inc(s["ident_set"], 1)
            pool.wait_ge(s["ident_set"], 1)
            pool.tensor_copy(K.identb[:], K.ident[:])

        @block.vector
        def _(v):
            for i in range(loads):
                v.wait_ge(s[f"x_loaded{i}"], 16)
                for t in range(i * per, (i + 1) * per):
                    v.bn_stats(K.stats[:, t, :], K.X[:, t, :])


def norm_phase(nc, K, name):
    with ExitStack() as c:
        var = c.enter_context(nc.sbuf_tensor(f"var_{name}", [P, K.tiles, 1], F32))
        t = c.enter_context(nc.sbuf_tensor(f"t_{name}", [P, K.tiles, 1], F32))
        s = c.enter_context(semaphores(nc, name, ("norm_chain",)))
        block = c.enter_context(nc.Block())

        @block.vector
        def _(v):
            ch = Chain(v, s["norm_chain"], MOMENT_STEPS + RSQRT_STEPS)
            ch.begin(0)
            st = [K.stats[:, :, i:i + 1] for i in range(6)]
            moments(v, ch.step, D, st, K.mean[:], var[:], t[:])
            rsqrt(v, ch.step, K.rstd[:], var[:], t[:])
            ch.end()



def l0_ffn_weights(nc, K, ctx, cls_w, cls_b, gate_up, down):
    ET, H = cls_w.shape
    ER, _, I = down.shape
    pairs = ER // 2

    def sb(name, shape, dt=F32):
        return ctx.enter_context(nc.sbuf_tensor(name, shape, dt))

    K.ER, K.ET, K.I, K.pairs = ER, ET, I, pairs
    K.wg = [sb(f"wg{k}", [P, ER, I], F32R) for k in "hl"]
    K.wu = [sb(f"wu{k}", [P, ER, I], F32R) for k in "hl"]
    K.wd = [sb(f"wd{k}", [P, pairs, D], F32R) for k in "hl"]
    K.wc = sb("wc", [P, ET])
    K.bias = sb("cls_bias", [P, ET])
    K.sel = sb("sel", [3 * ER, pairs, P], BF16)
    GB = 8
    with ExitStack() as c:
        raw_gu = c.enter_context(nc.sbuf_tensor("raw_gu", [P, ER, H], F32))
        raw_d = c.enter_context(nc.sbuf_tensor("raw_d", [P, ER, I], F32))
        raw_c = c.enter_context(nc.sbuf_tensor("raw_c", [ET, H], F32))
        ps = [c.enter_context(nc.psum_tensor(f"ps_w{i}", [P, 4, P], F32)) for i in range(2)]
        s = c.enter_context(semaphores(nc, "w0", ("gu_loaded", "d_loaded", "c_loaded", "b_loaded", "turned", "high_ready", "copied",
                                                  "sel_step")))
        block = c.enter_context(nc.Block())
        jobs = ER // 4 + pairs // 4 + 1

        @block.sync
        def _(sp):
            sp.dma_start(raw_gu[:], gate_up[0:ER].rearrange("e f d -> f e d")).then_inc(s["gu_loaded"], 16)
            sp.dma_start(raw_c[:], cls_w).then_inc(s["c_loaded"], 16)
            sp.dma_start(K.bias[:], cls_b.rearrange("(a e) -> a e", a=1).to_broadcast([P, ET])).then_inc(s["b_loaded"], 16)
            sp.wait_ge(s["b_loaded"], 16)

        @block.gpsimd
        def _(pool):
            pool.memset(K.sel[:], 0.0).then_inc(s["sel_step"], 1)
            v = K.sel[:].rearrange("k p (h m) -> k p h m", h=2)
            for b in range(3):
                pool.wait_ge(s["sel_step"], b + 1)
                pool.affine_select(out=v, in_=v, compare_op=ALU.not_equal, fill=1.0, base=-ER * b,
                                   pattern=[[-2, pairs], [-1, 2], [0, P // 2]], channel_multiplier=1).then_inc(s["sel_step"], 1)

        @block.tensor
        def _(pe):
            pe.wait_ge(s["gu_loaded"], 16)
            pe.wait_ge(s["d_loaded"], 16)
            pe.wait_ge(s["c_loaded"], 16)
            for j in range(jobs):
                after(pe, s["copied"], j - 1)
                for i in range(4):
                    if j < ER // 4:
                        m = pe.transpose(ps[j % 2][:, i, :], raw_gu[:, 4 * j + i, :], K.ident[:])
                    elif j < jobs - 1:
                        p = 4 * (j - ER // 4) + i
                        m = pe.transpose(ps[j % 2][:, i, :], raw_d[:, 2 * p:2 * p + 2, :].rearrange("p e f -> p (e f)"), K.ident[:])
                    elif i == 0:
                        m = pe.transpose(ps[j % 2][:, 0, 0:ET], raw_c[:], K.ident[0:ET, 0:ET])
                m.then_inc(s["turned"], 1)

        def places(k, j):
            if j < ER // 4:
                return ((K.wg[k][:, 4 * j:4 * j + 4, :], ps[j % 2][:, :, 0:I]),
                        (K.wu[k][:, 4 * j:4 * j + 4, :], ps[j % 2][:, :, I:2 * I]))
            p = 4 * (j - ER // 4)
            return ((K.wd[k][:, p:p + 4, :], ps[j % 2][:]),)

        @block.scalar
        def _(act):
            act.dma_start(raw_d[:], down.rearrange("e d f -> d e f")).then_inc(s["d_loaded"], 16)
            for j in range(jobs - 1):
                act.wait_ge(s["turned"], j + 1)
                for to, frm in places(0, j):
                    m = act.copy(to, frm)
                m.then_inc(s["high_ready"], 1)

        @block.vector
        def _(v):
            for j in range(jobs - 1):
                v.wait_ge(s["high_ready"], j + 1)
                for (to, frm), (high, _) in zip(places(1, j), places(0, j)):
                    m = v.tensor_tensor(to, frm, high.bitcast(F32), ALU.subtract)
                m.then_inc(s["copied"], 1)
            v.wait_ge(s["turned"], jobs)
            v.tensor_copy(K.wc[:], ps[(jobs - 1) % 2][:, 0, 0:ET]).then_inc(s["copied"], 1)


def l0_ffn(nc, K, name):
    ER, ET, pairs = K.ER, K.ET, K.pairs
    G = 4
    N = G * P
    n = K.tiles // G
    TOPK, SCALE = 6, 2.5
    HB, LAG = 4, 3
    PAD = 8 - TOPK
    with ExitStack() as c:
        sb = lambda nm, s, dt=F32: c.enter_context(nc.sbuf_tensor(f"{nm}_{name}", s, dt))
        ps = lambda nm, s, dt=F32: c.enter_context(nc.psum_tensor(f"{nm}_{name}", s, dt))
        xn = [sb(f"xn{i}", [P, G, D]) for i in range(2)]
        xT = [sb(f"xT{i}", [P, N]) for i in range(2)]
        xTh = [sb(f"xTh{i}", [P, N], F32R) for i in range(2)]
        xTl = [sb(f"xTl{i}", [P, N], F32R) for i in range(2)]
        wparts = sb("wparts", [P, G, 3 * ER], BF16)
        wT = [sb(f"wT{i}", [3 * ER, N], BF16) for i in range(2)]
        zero_w = [sb(f"zero_w{i}", [P, G]) for i in range(2)]
        logit, expd, score = sb("logit", [P, G, ET]), sb("expd", [P, G, ET]), sb("score", [P, G, ET])
        biased, struck = sb("biased", [P, G, ET + PAD]), sb("struck", [P, G, ET + PAD])
        top8, w, rest = sb("top8", [P, G, 8]), sb("w", [P, G, ET]), sb("rest", [P, G, ER])
        rmax, rsum, rinv = sb("rmax", [P, G]), sb("rsum", [P, G]), sb("rinv", [P, G])
        silu = [sb(f"silu{i}", [P, N]) for i in range(2)]
        gated = [sb(f"gated{i}", [P, N]) for i in range(2)]
        hid = [sb(f"hid{i}", [P, N]) for i in range(2)]
        hidh = [sb(f"hidh{i}", [P, N], F32R) for i in range(HB)]
        hidl = [sb(f"hidl{i}", [P, N], F32R) for i in range(HB)]
        outT, y, ysum = sb("outT", [P, N]), sb("y", [P, G, D]), sb("ysum", [P, G, D])
        pg = [ps(f"pg{i}", [P, N]) for i in range(2)]
        pu = [ps(f"pu{i}", [P, N]) for i in range(2)]
        pw = [ps(f"pw{i}", [P, N]) for i in range(2)]
        po, pm = ps("po", [P, N]), ps("pm", [P, N])
        pmb = pm[:].bitcast(BF16)
        s = c.enter_context(semaphores(nc, name, (
            "pad_set", "xn_ready", "xn_turned", "xT_ready", "logits_done", "logits_read", "exp_done", "parts_ready",
            "parts_turned", "wT_ready", "gate_done", "pair_done", "silu_done", "gated_done", "hid_done", "hidh_ready", "hidl_ready",
            "xTl_ready", "down_done",
            "outT_ready", "out_turned", "y_ready", "out_read", "route_chain", "out_chain", "turn")))
        block = c.enter_context(nc.Block())

        @block.gpsimd
        def _(pool):
            def body(t, par, prev, cur, nxt):
                for p in range(pairs):
                    if nxt and p == 3:
                        pool.wait_ge(s["xT_ready"], t + 2)
                        pool.tensor_tensor(xTl[1 - par][:], xT[1 - par][:], xTh[1 - par][:].bitcast(F32),
                                           ALU.subtract).then_inc(s["xTl_ready"], 1)
                    if cur:
                        k = t * pairs + p
                        pool.wait_ge(s["hidh_ready"], k + 1)
                        after(pool, s["down_done"], k - HB + 1)
                        pool.tensor_tensor(hidl[p % HB][:], hid[p % 2][:], hidh[p % HB][:].bitcast(F32),
                                           ALU.subtract).then_inc(s["hidl_ready"], 1)

            slots(pool, n, body)

        @block.tensor
        def _(pe):
            def product(to, w, x, start=True, stop=True):
                pe.matmul(to, w[0], x[0][:], start=start, stop=False)
                pe.matmul(to, w[0], x[1][:], start=False, stop=False)
                return pe.matmul(to, w[1], x[0][:], start=False, stop=stop)

            def body(t, par, prev, cur, nxt):
                for p in range(pairs):
                    if cur:
                        k = t * pairs + p
                        b = p % 2
                        x = (xTh[par], xTl[par])
                        pair = slice(2 * p, 2 * p + 2)
                        if p == 0:
                            pe.wait_ge(s["xTl_ready"], t + 1)
                            pe.wait_ge(s["wT_ready"], t + 1)
                        after(pe, s["silu_done"], k - 1)
                        product(pg[b][:], [w[:, pair, :] for w in K.wg], x).then_inc(s["gate_done"], 1)
                        after(pe, s["hid_done"], k - 1)
                        product(pu[b][:], [w[:, pair, :] for w in K.wu], x)
                        pe.matmul(pw[b][:], K.sel[:, p, :], wT[par][:], start=True,
                                  stop=True).then_inc(s["pair_done"], 1)
                        if p >= LAG:
                            if p == LAG:
                                after(pe, s["outT_ready"], t)
                            down(t, p - LAG)
                    if prev and p < LAG:
                        down(t - 1, pairs - LAG + p)
                    if nxt and p == 1:
                        pe.wait_ge(s["xn_ready"], t + 2)
                        after(pe, s["out_read"], t - 1)
                        for j in range(G):
                            m = pe.transpose(pm[:, j * P:(j + 1) * P], xn[1 - par][:, j, :], K.ident[:])
                        m.then_inc(s["xn_turned"], 1)
                    if nxt and p == 3:
                        pe.wait_ge(s["xT_ready"], t + 2)
                        for j in range(G):
                            m = pe.matmul(pm[:, j * ET:(j + 1) * ET], xT[1 - par][:, j * P:(j + 1) * P], K.wc[:],
                                          start=True, stop=True)
                        m.then_inc(s["logits_done"], 1)
                    if prev and p == 5:
                        pe.wait_ge(s["outT_ready"], t)
                        after(pe, s["logits_read"], t + 2 if nxt else 0)
                        for j in range(G):
                            m = pe.transpose(pm[:, j * P:(j + 1) * P], outT[:, j * P:(j + 1) * P], K.ident[:])
                        m.then_inc(s["out_turned"], 1)
                    if nxt and p == 14:
                        pe.wait_ge(s["parts_ready"], t + 2)
                        after(pe, s["out_read"], t if prev else 0)
                        for j in range(G):
                            m = pe.transpose(pmb[0:3 * ER, j * P:(j + 1) * P], wparts[:, j, :], K.identb[:])
                        m.then_inc(s["parts_turned"], 1)

            def down(t, p):
                k = t * pairs + p
                pe.wait_ge(s["hidl_ready"], k + 1)
                product(po[:], [w[:, p, :] for w in K.wd], (hidh[p % HB], hidl[p % HB]), start=(p == 0),
                        stop=(p == pairs - 1)).then_inc(s["down_done"], 1)

            slots(pe, n, body)

        @block.scalar
        def _(act):
            def high(t, p):
                k = t * pairs + p
                act.wait_ge(s["hid_done"], k + 1)
                after(act, s["down_done"], k - HB + 1)
                act.copy(hidh[p % HB][:], hid[p % 2][:]).then_inc(s["hidh_ready"], 1)

            def body(t, par, prev, cur, nxt):
                for p in range(pairs):
                    if prev and p == LAG:
                        act.wait_ge(s["down_done"], t * pairs)
                        after(act, s["out_turned"], t - 1)
                        act.copy(outT[:], po[:]).then_inc(s["outT_ready"], 1)
                    if cur:
                        k = t * pairs + p
                        act.wait_ge(s["gate_done"], k + 1)
                        after(act, s["gated_done"], k - 1)
                        act.activation(silu[p % 2][:], pg[p % 2][:], ACT.Silu).then_inc(s["silu_done"], 1)
                        if p:
                            high(t, p - 1)
                    if nxt and p == 2:
                        act.wait_ge(s["xn_turned"], t + 2)
                        act.copy(xTh[1 - par][:], pm[:])
                        act.copy(xT[1 - par][:], pm[:]).then_inc(s["xT_ready"], 1)
                    if nxt and p == 5:
                        act.wait_ge(s["logits_read"], t + 2)
                        act.activation(expd[:], logit[:], ACT.Exp).then_inc(s["exp_done"], 1)
                    if nxt and p == 15:
                        act.wait_ge(s["parts_turned"], t + 2)
                        act.copy(wT[1 - par][:], pmb[0:3 * ER, 0:N]).then_inc(s["wT_ready"], 1)
                if cur:
                    high(t, pairs - 1)

            slots(act, n, body)

        @block.vector
        def _(v):
            route = Chain(v, s["route_chain"], 13, s["turn"])
            out = Chain(v, s["out_chain"], 2, s["turn"])
            v.memset(biased[:], BIG).then_inc(s["pad_set"], 1)
            v.wait_ge(s["pad_set"], 1)

            def gate(t, p):
                k = t * pairs + p
                v.wait_ge(s["silu_done"], k + 1)
                v.wait_ge(s["pair_done"], k + 1)
                v.tensor_tensor(gated[p % 2][:], silu[p % 2][:], pu[p % 2][:], ALU.mult).then_inc(s["gated_done"], 1)

            def weigh(t, p):
                k = t * pairs + p
                v.wait_ge(s["gated_done"], k + 1)
                after(v, s["hidl_ready"], k - 1)
                v.tensor_tensor(hid[p % 2][:], gated[p % 2][:], pw[p % 2][:], ALU.mult).then_inc(s["hid_done"], 1)

            def zero_experts(t, par):
                after(v, s["out_read"], t)
                for j in range(G):
                    m = v.tensor_scalar(y[:, j, :], xn[par][:, j, :], zero_w[par][:, j:j + 1], None, ALU.mult)
                m.then_inc(s["y_ready"], 1)

            def finish(t):
                out.begin(t)
                v.wait_ge(s["out_turned"], t + 1)
                v.wait_ge(s["y_ready"], t + 1)
                v.tensor_tensor(ysum[:], y[:], pm[:].rearrange("p (g d) -> p g d", g=G), ALU.add).then_inc(s["out_read"], 1)
                v.wait_ge(s["out_read"], t + 1)

            def write(t):
                out.step_apart(v.scalar_tensor_tensor(K.X[:, bass.ds(t * G, G), :], ysum[:], 0.5 * SCALE,
                                                      K.X[:, bass.ds(t * G, G), :], ALU.mult, ALU.add))

            def new_stats(t):
                for j in range(G):
                    m = v.bn_stats(K.stats[:, t * G + j, :], K.X[:, t * G + j, :])
                out.step(m)
                out.end()

            def norm(t, par):
                for j in range(G):
                    m = v.tensor_scalar(xn[par][:, j, :], K.X[:, t * G + j, :], K.mean[:, t * G + j, :],
                                        K.rstd[:, t * G + j, :], ALU.subtract, ALU.mult)
                m.then_inc(s["xn_ready"], 1)

            def center(t):
                route.begin(t)
                pl = pm[:, 0:G * ET].rearrange("p (g e) -> p g e", g=G)
                v.wait_ge(s["logits_done"], t + 1)
                route.step(v.tensor_reduce(rmax[:], pl, AX.X, ALU.max))
                v.tensor_tensor(logit[:], pl, rmax[:, :, None].to_broadcast([P, G, ET]),
                                ALU.subtract).then_inc(s["logits_read"], 1)

            def softmax(t):
                v.wait_ge(s["exp_done"], t + 1)
                route.step(v.tensor_reduce(rsum[:], expd[:], AX.X, ALU.add))
                route.step(v.reciprocal(rinv[:], rsum[:]))
                route.step(v.tensor_tensor(score[:], expd[:], rinv[:, :, None].to_broadcast([P, G, ET]), ALU.mult))
                route.step_apart(v.tensor_tensor(biased[:, :, 0:ET], score[:],
                                                 K.bias[:, None, :].to_broadcast([P, G, ET]), ALU.add))

            def topk(t):
                for j in range(G):
                    m = v.max(top8[:, j, :], biased[:, j, :])
                route.step_apart(m)

            def strike(t):
                for j in range(G):
                    m = v.match_replace(struck[:, j, :], top8[:, j, :], biased[:, j, :], -BIG)
                route.step(m)
                route.step(v.scalar_tensor_tensor(w[:], struck[:, :, 0:ET], -BIG / 2, score[:], ALU.is_le, ALU.mult))

            def parts(t, par):
                route.step(v.tensor_reduce(zero_w[par][:], w[:, :, ER:ET], AX.X, ALU.add))
                route.step(v.tensor_copy(wparts[:, :, 0:ER], w[:, :, 0:ER]))
                route.step(v.tensor_tensor(rest[:], w[:, :, 0:ER], wparts[:, :, 0:ER], ALU.subtract))

            def low_parts(t):
                route.step(v.tensor_copy(wparts[:, :, ER:2 * ER], rest[:]))
                route.step(v.tensor_tensor(rest[:], rest[:], wparts[:, :, ER:2 * ER], ALU.subtract))
                v.tensor_copy(wparts[:, :, 2 * ER:3 * ER], rest[:]).then_inc(s["parts_ready"], 1)
                route.end()

            def body(t, par, prev, cur, nxt):
                for p in range(pairs):
                    if cur:
                        if p >= 1:
                            weigh(t, p - 1)
                        gate(t, p)
                    if nxt and p == 0:
                        norm(t + 1, 1 - par)
                    if nxt and p == 4:
                        center(t + 1)
                    if prev and p == 6:
                        finish(t - 1)
                    if prev and p == 7:
                        write(t - 1)
                    if prev and p == 8:
                        new_stats(t - 1)
                    if nxt and p == 9:
                        softmax(t + 1)
                    if nxt and p == 10:
                        topk(t + 1)
                    if nxt and p == 11:
                        strike(t + 1)
                    if nxt and p == 12:
                        parts(t + 1, 1 - par)
                    if nxt and p == 13:
                        low_parts(t + 1)
                    if cur and p == 14:
                        zero_experts(t, par)
                if cur:
                    weigh(t, pairs - 1)

            slots(v, n, body)



def l0_attention(nc, K, wq_d, wk_d, wv_d, seq, name):
    DQ = wq_d.shape[1]
    R = seq // P
    assert R == 2
    n = K.tiles // R
    W = P * (R * (R + 1) // 2)
    with ExitStack() as c:
        sb = lambda nm, s, dt=F32: c.enter_context(nc.sbuf_tensor(f"{nm}_{name}", s, dt))
        ps = lambda nm, s, dt=F32: c.enter_context(nc.psum_tensor(f"{nm}_{name}", s, dt))
        wq, wk, wv = sb("wq", [P, DQ]), sb("wk", [P, DQ]), sb("wv", [P, D])
        mask = sb("mask", [P, W])
        xn, xT = sb("xn", [P, R, D]), [sb(f"xT{i}", [P, seq]) for i in range(2)]
        qk = sb("qk", [DQ, 2, seq])
        val = [sb(f"val{i}", [P, R, D]) for i in range(2)]
        sc, probs, probsT = sb("sc", [P, W]), sb("probs", [P, W]), sb("probsT", [P, W])
        nmax, sums, rinv = sb("nmax", [P, R]), [sb(f"sums{i}", [P, R]) for i in range(2)], sb("rinv", [P, R])
        px, pqk, pv = ps("px", [P, seq]), ps("pqk", [DQ, 2, seq]), ps("pv", [P, R, D])
        pS, pT, pO = ps("pS", [P, W]), ps("pT", [P, W]), ps("pO", [P, R, D])
        s = c.enter_context(semaphores(nc, name, (
            "w_loaded", "mask_zero", "mask_set", "wq_scaled", "xn_ready", "xn_turned", "xT_ready", "qk_done", "v_done", "qk_ready",
            "v_ready", "scores_done", "masked", "max_ready", "exp_done", "probs_turned", "probsT_ready",
            "out_done", "inv_ready", "x_written", "turn")))
        block = c.enter_context(nc.Block())

        @block.sync
        def _(sp):
            sp.dma_start(wq[:], wq_d).then_inc(s["w_loaded"], 16)
            sp.dma_start(wk[:], wk_d).then_inc(s["w_loaded"], 16)
            sp.dma_start(wv[:], wv_d).then_inc(s["w_loaded"], 16)

        @block.gpsimd
        def _(pool):
            pool.memset(mask[:], 0.0).then_inc(s["mask_zero"], 1)
            pool.wait_ge(s["mask_zero"], 1)
            for col in (0, 2 * P):
                m = pool.affine_select(out=mask[:, col:col + P], in_=mask[:, col:col + P], compare_op=ALU.is_ge,
                                       fill=-BIG, base=0, pattern=[[-1, P]], channel_multiplier=1)
            m.then_inc(s["mask_set"], 1)

        @block.tensor
        def _(pe):
            def body(t, par, prev, cur, nxt, pre):
                if cur:
                    pe.wait_ge(s["qk_ready"], t + 1)
                    after(pe, s["masked"], t)
                    pe.matmul(pS[:, 0:P], qk[:, 0, 0:P], qk[:, 1, 0:P], start=True, stop=True)
                    pe.matmul(pS[:, P:W], qk[:, 0, P:seq], qk[:, 1, :], start=True,
                              stop=True).then_inc(s["scores_done"], 1)
                if prev:
                    pe.wait_ge(s["exp_done"], t)
                    after(pe, s["probsT_ready"], t - 1)
                    for j in range(W // P):
                        m = pe.transpose(pT[:, j * P:(j + 1) * P], probs[:, j * P:(j + 1) * P], K.ident[:])
                    m.then_inc(s["probs_turned"], 1)
                if pre:
                    pe.wait_ge(s["xn_ready"], t + 3)
                    after(pe, s["xT_ready"], t + 2)
                    for j in range(R):
                        m = pe.transpose(px[:, j * P:(j + 1) * P], xn[:, j, :], K.ident[:])
                    m.then_inc(s["xn_turned"], 1)
                if prev:
                    pe.wait_ge(s["probsT_ready"], t)
                    pe.wait_ge(s["v_ready"], t)
                    after(pe, s["x_written"], t - 1)
                    pe.matmul(pO[:, 0, :], probsT[:, 0:P], val[1 - par][:, 0, :], start=True, stop=True)
                    pe.matmul(pO[:, 1, :], probsT[:, P:2 * P], val[1 - par][:, 0, :], start=True, stop=False)
                    pe.matmul(pO[:, 1, :], probsT[:, 2 * P:W], val[1 - par][:, 1, :], start=False,
                              stop=True).then_inc(s["out_done"], 1)
                if nxt:
                    pe.wait_ge(s["xT_ready"], t + 2)
                    if isinstance(t, int) and t == -1:
                        pe.wait_ge(s["wq_scaled"], 1)
                    after(pe, s["qk_ready"], t + 1)
                    x = xT[1 - par]
                    pe.matmul(pqk[:, 0, :], wq[:], x[:], start=True, stop=True)
                    pe.matmul(pqk[:, 1, :], wk[:], x[:], start=True, stop=True).then_inc(s["qk_done"], 1)
                    after(pe, s["v_ready"], t + 1)
                    for j in range(R):
                        m = pe.matmul(pv[:, j, :], x[:, j * P:(j + 1) * P], wv[:], start=True, stop=True)
                    m.then_inc(s["v_done"], 1)

            slots(pe, n, body, ahead=2)

        @block.scalar
        def _(act):
            def body(t, par, prev, cur, nxt, pre):
                if prev:
                    act.wait_ge(s["probs_turned"], t)
                    after(act, s["out_done"], t - 1)
                    act.copy(probsT[:], pT[:]).then_inc(s["probsT_ready"], 1)
                if pre:
                    act.wait_ge(s["xn_turned"], t + 3)
                    after(act, s["v_done"], t + 1)
                    act.copy(xT[par][:], px[:]).then_inc(s["xT_ready"], 1)
                if cur:
                    act.wait_ge(s["max_ready"], t + 1)
                    after(act, s["probs_turned"], t)
                    after(act, s["inv_ready"], t - 1)
                    act.activation(probs[:, 0:P], sc[:, 0:P], ACT.Exp, bias=nmax[:, 0:1], accum_out=sums[par][:, 0:1])
                    act.activation(probs[:, P:W], sc[:, P:W], ACT.Exp, bias=nmax[:, 1:2],
                                   accum_out=sums[par][:, 1:2]).then_inc(s["exp_done"], 1)
                if nxt:
                    act.wait_ge(s["qk_done"], t + 2)
                    after(act, s["scores_done"], t + 1)
                    act.copy(qk[:], pqk[:]).then_inc(s["qk_ready"], 1)

            slots(act, n, body, ahead=2)

        @block.vector
        def _(v):
            v.wait_ge(s["w_loaded"], 48)
            v.tensor_scalar(wq[:], wq[:], float(DQ) ** -0.5, None, ALU.mult).then_inc(s["wq_scaled"], 1)
            v.wait_ge(s["mask_set"], 1)

            def body(t, par, prev, cur, nxt, pre):
                if pre:
                    after(v, s["xn_turned"], t + 2)
                    for j in range(R):
                        i = (t + 2) * R + j
                        m = v.tensor_scalar(xn[:, j, :], K.X[:, i, :], K.mean[:, i, :], K.rstd[:, i, :],
                                            ALU.subtract, ALU.mult)
                    m.then_inc(s["xn_ready"], 1)
                if cur:
                    v.wait_ge(s["scores_done"], t + 1)
                    after(v, s["exp_done"], t)
                    v.tensor_tensor(sc[:], pS[:], mask[:], ALU.add).then_inc(s["masked"], 1)
                    v.wait_ge(s["masked"], t + 1)
                    v.tensor_reduce(nmax[:, 0:1], sc[:, 0:P], AX.X, ALU.max, negate=True)
                    v.tensor_reduce(nmax[:, 1:2], sc[:, P:W], AX.X, ALU.max, negate=True).then_inc(s["max_ready"], 1)
                if prev:
                    v.wait_ge(s["exp_done"], t)
                    after(v, s["x_written"], t - 1)
                    v.reciprocal(rinv[:], sums[1 - par][:]).then_inc(s["inv_ready"], 1)
                    v.wait_ge(s["inv_ready"], t)
                    v.wait_ge(s["out_done"], t)
                    for j in range(R):
                        i = (t - 1) * R + j
                        m = v.scalar_tensor_tensor(K.X[:, i, :], pO[:, j, :], rinv[:, j:j + 1], K.X[:, i, :], ALU.mult, ALU.add)
                    m.then_inc(s["x_written"], 1)
                    v.wait_ge(s["x_written"], t)
                    v.sem_inc(s["turn"], 1)
                    for j in range(R):
                        v.bn_stats(K.stats[:, (t - 1) * R + j, :], K.X[:, (t - 1) * R + j, :])
                if nxt:
                    v.wait_ge(s["v_done"], t + 2)
                    after(v, s["out_done"], t)
                    v.tensor_copy(val[1 - par][:], pv[:]).then_inc(s["v_ready"], 1)

            slots(v, n, body, ahead=2)



def rwkv(nc, K, T, seq, name):
    R = seq // P
    n = K.tiles // R
    CLAMP, KEPS = 60.0, 1e-8
    with ExitStack() as c:
        sb = lambda nm, s, dt=F32: c.enter_context(nc.sbuf_tensor(f"{nm}_{name}", s, dt))
        ps = lambda nm, s, dt=F32: c.enter_context(nc.psum_tensor(f"{nm}_{name}", s, dt))
        raw = sb("raw", [P, 4, P])
        wT = sb("wT", [P, 4, P])
        mix, omix = sb("mix", [P, 3]), sb("omix", [P, 3])
        tdec, first, decay = sb("tdec", [P, 1]), sb("first", [P, 1]), sb("decay", [P, 1])
        decays = sb("decays", [P, seq])
        xn = sb("xn", [P, R, D])
        xs = [sb(f"xs{i}", [P, seq + 1]) for i in range(2)]
        wnow, wbefore = sb("wnow", [P, 3, P]), sb("wbefore", [P, 3, P])
        kmin, kv = sb("kmin", [P, seq]), sb("kv", [P, seq])
        kc, th, o = ([sb(f"{k}{i}", [P, seq]) for i in range(2)] for k in ("kc", "th", "o"))
        sk, skv = sb("sk", [P, seq + 1]), sb("skv", [P, seq + 1])
        den, num, inv = sb("den", [P, seq]), sb("num", [P, seq]), sb("inv", [P, seq])
        pkv = [ps(f"pkv{i}", [P, 2, seq]) for i in range(2)]
        px, pr, pO, pw = ps("px", [P, seq]), ps("pr", [P, seq]), ps("pO", [P, R, D]), ps("pw", [P, 4, P])
        s = c.enter_context(semaphores(nc, name, (
            "loaded", "w_turned", "w_ready", "setup", "set_chain", "xn_ready", "xn_turned", "xs_ready",
            "w_mixed", "proj_done", "kmin_ready", "kc_ready", "th_ready", "chain", "kv_ready", "o_ready", "out_done",
            "x_written", "turn")))
        block = c.enter_context(nc.Block())

        @block.sync
        def _(sp):
            for i, w in enumerate(("Wk", "Wv", "Wr", "Wo")):
                sp.dma_start(raw[:, i, :], T[f"L1_attn_{w}"]).then_inc(s["loaded"], 16)
            for i, w in enumerate(("k", "v", "r")):
                sp.dma_start(mix[:, i:i + 1], T[f"L1_attn_time_mix_{w}"].rearrange("a b c -> c (a b)")).then_inc(s["loaded"], 16)
            sp.dma_start(tdec[:], T["L1_attn_time_decay"]).then_inc(s["loaded"], 16)
            sp.dma_start(first[:], T["L1_attn_time_first"]).then_inc(s["loaded"], 16)

        LOADS = 16 * 9

        @block.tensor
        def _(pe):
            pe.wait_ge(s["loaded"], LOADS)
            for i in range(4):
                m = pe.transpose(pw[:, i, :], raw[:, i, :], K.ident[:])
            m.then_inc(s["w_turned"], 1)

            def body(t, par, prev, cur, nxt, pre):
                if nxt:
                    if isinstance(t, int) and t == -1:
                        pe.wait_ge(s["w_mixed"], 1)
                    pe.wait_ge(s["xs_ready"], t + 2)
                    after(pe, s["kv_ready"], t)
                    after(pe, s["th_ready"], t + 1)
                    x = xs[1 - par]
                    for i, to in enumerate((pkv[1 - par][:, 0, :], pkv[1 - par][:, 1, :], pr[:])):
                        pe.matmul(to, wnow[:, i, :], x[:, 1:seq + 1], start=True, stop=False)
                        m = pe.matmul(to, wbefore[:, i, :], x[:, 0:seq], start=False, stop=True)
                    m.then_inc(s["proj_done"], 1)
                if prev:
                    pe.wait_ge(s["o_ready"], t)
                    after(pe, s["x_written"], t - 1)
                    for j in range(R):
                        m = pe.matmul(pO[:, j, :], o[1 - par][:, j * P:(j + 1) * P], wT[:, 3, :], start=True, stop=True)
                    m.then_inc(s["out_done"], 1)
                if pre:
                    pe.wait_ge(s["xn_ready"], t + 3)
                    after(pe, s["xs_ready"], t + 2)
                    for j in range(R):
                        m = pe.transpose(px[:, j * P:(j + 1) * P], xn[:, j, :], K.ident[:])
                    m.then_inc(s["xn_turned"], 1)

            slots(pe, n, body, ahead=2)

        @block.scalar
        def _(act):
            act.wait_ge(s["loaded"], LOADS)
            act.activation(tdec[:], tdec[:], ACT.Exp).then_inc(s["set_chain"], 1)
            act.wait_ge(s["set_chain"], 1)
            act.activation(decay[:], tdec[:], ACT.Exp, scale=-1.0)
            act.activation(first[:], first[:], ACT.Exp).then_inc(s["setup"], 1)
            act.wait_ge(s["w_turned"], 1)
            act.copy(wT[:], pw[:]).then_inc(s["w_ready"], 1)

            def body(t, par, prev, cur, nxt, pre):
                if nxt:
                    act.wait_ge(s["proj_done"], t + 2)
                    after(act, s["o_ready"], t)
                    act.activation(th[1 - par][:], pr[:], ACT.Tanh, scale=0.5).then_inc(s["th_ready"], 1)
                    act.wait_ge(s["kmin_ready"], t + 2)
                    act.activation(kc[1 - par][:], kmin[:], ACT.Exp).then_inc(s["kc_ready"], 1)
                if pre:
                    act.wait_ge(s["xn_turned"], t + 3)
                    after(act, s["proj_done"], t + 1)
                    act.copy(xs[par][:, 1:seq + 1], px[:]).then_inc(s["xs_ready"], 1)

            slots(act, n, body, ahead=2)

        @block.vector
        def _(v):
            for i in range(2):
                v.memset(xs[i][:, 0:1], 0.0)
            v.memset(sk[:, 0:1], 0.0)
            v.memset(skv[:, 0:1], 0.0)
            v.wait_ge(s["loaded"], LOADS)
            v.tensor_scalar(omix[:], mix[:], -1.0, 1.0, ALU.mult, ALU.add)
            v.wait_ge(s["setup"], 1)
            v.tensor_copy(decays[:], decay[:].to_broadcast([P, seq])).then_inc(s["set_chain"], 1)
            v.wait_ge(s["set_chain"], 2)
            v.wait_ge(s["w_ready"], 1)
            for i in range(3):
                v.tensor_scalar(wnow[:, i, :], wT[:, i, :], mix[:, i:i + 1], None, ALU.mult)
                m = v.tensor_scalar(wbefore[:, i, :], wT[:, i, :], omix[:, i:i + 1], None, ALU.mult)
            m.then_inc(s["w_mixed"], 1)
            ch = Chain(v, s["chain"], 3)

            def body(t, par, prev, cur, nxt, pre):
                if pre:
                    after(v, s["xn_turned"], t + 2)
                    for j in range(R):
                        i = (t + 2) * R + j
                        m = v.tensor_scalar(xn[:, j, :], K.X[:, i, :], K.mean[:, i, :], K.rstd[:, i, :],
                                            ALU.subtract, ALU.mult)
                    m.then_inc(s["xn_ready"], 1)
                if cur:
                    ch.begin(t)
                    after(v, s["o_ready"], t)
                    v.wait_ge(s["kc_ready"], t + 1)
                    v.tensor_tensor_scan(sk[:, 1:seq + 1], decays[:], kc[par][:], 0.0, ALU.mult, ALU.add)
                    v.tensor_tensor(kv[:], kc[par][:], pkv[par][:, 1, :], ALU.mult).then_inc(s["kv_ready"], 1)
                    v.wait_ge(s["kv_ready"], t + 1)
                    v.scalar_tensor_tensor(den[:], kc[par][:], first[:], sk[:, 0:seq], ALU.mult, ALU.add)
                    ch.step(v.tensor_tensor_scan(skv[:, 1:seq + 1], decays[:], kv[:], 0.0, ALU.mult, ALU.add))
                if nxt:
                    v.wait_ge(s["proj_done"], t + 2)
                    after(v, s["kc_ready"], t + 1)
                    v.tensor_scalar(kmin[:], pkv[1 - par][:, 0, :], CLAMP, None, ALU.min).then_inc(s["kmin_ready"], 1)
                if cur:
                    v.tensor_scalar(den[:], den[:], KEPS, None, ALU.add)
                    ch.step(v.scalar_tensor_tensor(num[:], kv[:], first[:], skv[:, 0:seq], ALU.mult, ALU.add))
                    v.wait_ge(s["th_ready"], t + 1)
                    v.scalar_tensor_tensor(num[:], th[par][:], 1.0, num[:], ALU.add, ALU.mult)
                    ch.step(v.reciprocal(inv[:], den[:]))
                    after(v, s["out_done"], t - 1)
                    v.scalar_tensor_tensor(o[par][:], num[:], 0.5, inv[:], ALU.mult, ALU.mult).then_inc(s["o_ready"], 1)
                    ch.end()
                if prev:
                    v.wait_ge(s["out_done"], t)
                    v.tensor_tensor(K.X[:, bass.ds((t - 1) * R, R), :], pO[:], K.X[:, bass.ds((t - 1) * R, R), :],
                                    ALU.add).then_inc(s["x_written"], 1)
                    v.wait_ge(s["x_written"], t)
                    v.sem_inc(s["turn"], 1)
                    for j in range(R):
                        v.bn_stats(K.stats[:, (t - 1) * R + j, :], K.X[:, (t - 1) * R + j, :])

            slots(v, n, body, ahead=2)



HEADS_A_GROUP = 4
ROWS = P // HEADS_A_GROUP


def l1_ffn(nc, K, T, seq, name):
    with ExitStack() as c:
        Y = c.enter_context(nc.sbuf_tensor(f"Y_{name}", [P, K.tiles, D], F32))
        l1_attention(nc, K, Y, T, seq, name + "a")
        norm_phase(nc, K, name + "n")
        l1_experts(nc, K, Y, T, name + "e")


def l1_attention(nc, K, Y, T, seq, name):
    H, HD = T["L1_ffn_scale_w"].shape
    R = seq // P
    assert R == 2 and H * HD == D and 3 * HD < ROWS
    n = K.tiles // R
    NG = H // HEADS_A_GROUP
    HG = HEADS_A_GROUP
    MAXROW = 3 * HD
    PB, LAG = 4, 2
    SM = float(HD) ** -0.5
    with ExitStack() as c:
        sb = lambda nm, s, dt=F32: c.enter_context(nc.sbuf_tensor(f"{nm}_{name}", s, dt))
        ps = lambda nm, s, dt=F32: c.enter_context(nc.psum_tensor(f"{nm}_{name}", s, dt))
        raw = sb("raw", [P, 2, D])
        wq, wk, wz = sb("wq", [P, H, ROWS]), sb("wk", [P, H, ROWS]), sb("wz", [P, H, ROWS])
        wv, wo, wgate, gb = sb("wv", [P, D]), sb("wo", [P, D]), sb("wgate", [P, D]), sb("gb", [P, 1])
        sw, swq, swsum = sb("sw", [P, H, HD]), sb("swq", [P, H, HD]), sb("swsum", [P, H])
        rows = sb("rows", [P, ROWS])
        qlow, klow, one = sb("qlow", [P, 1]), sb("klow", [P, 1]), sb("one", [P, 1])
        xn, xT = sb("xn", [P, R, D]), sb("xT", [P, seq])
        th, qs = sb("th", [P, NG, seq]), sb("qs", [P, NG, seq])
        qr, kr = sb("qr", [P, NG, seq], F32R), sb("kr", [P, NG, seq], F32R)
        qa = [sb(f"qa{i}", [P, NG, seq], F32R) for i in range(2)]
        kw = [sb(f"kw{i}", [P, NG, seq], F32R) for i in range(2)]
        qb = [sb(f"qb{i}", [P, NG, seq], F32R) for i in range(2)]
        keysD = [sb(f"keysD{i}", [P, NG, HG, seq], F32R) for i in range(2)]
        vnew = sb("vnew", [P, seq])
        va = [sb(f"va{i}", [P, R, H, ROWS]) for i in range(2)]
        nmax, mx = sb("nmax", [P, NG, R, HG]), sb("mx", [P, R, H, ROWS])
        probs = [sb(f"probs{i}", [P, R, seq]) for i in range(PB)]
        av = sb("av", [P, NG, seq])
        rden, on, onT = sb("rden", [P, R, H]), sb("on", [P, R, D]), sb("onT", [P, seq])
        tg, og = sb("tg", [P, seq]), sb("og", [P, seq])
        p1 = [ps(f"p1{i}", [P, 2, seq]) for i in range(2)]
        p2 = [ps(f"p2{i}", [P, R, seq]) for i in range(2)]
        pav = ps("pav", [P, NG, seq])
        pA = ps("pA", [P, 2, seq])
        pB = ps("pB", [P, 2, seq])
        s = c.enter_context(semaphores(nc, name, (
            "loaded", "set_chain", "pool_chain", "w_set", "keys_zeroed", "xn_ready", "xn_turned", "xT_ready", "z_done",
            "th_ready", "q_done", "qs_ready", "qr_ready", "qa_ready", "k_done", "kr_ready", "kw_ready", "keys_ready",
            "v_done", "v_ready", "va_ready", "smax_done", "nmax_done", "mx_ready", "mx_turned", "qb_ready",
            "scores_done", "exp_done", "av_done", "av_ready", "av_turned", "rden_ready", "on_ready", "on_turned",
            "onT_ready", "gate_done", "tg_ready", "og_ready", "attn_done", "y_written", "turn", "pturn")))
        block = c.enter_context(nc.Block())
        LOADS = 16 * 7

        @block.sync
        def _(sp):
            sp.dma_start(raw[:, 0, :], T["L1_ffn_q_w"]).then_inc(s["loaded"], 16)
            sp.dma_start(raw[:, 1, :], T["L1_ffn_k_w"]).then_inc(s["loaded"], 16)
            sp.dma_start(wv[:], T["L1_ffn_v_w"]).then_inc(s["loaded"], 16)
            sp.dma_start(wo[:], T["L1_ffn_out_w"]).then_inc(s["loaded"], 16)
            sp.dma_start(wgate[:], T["L1_ffn_gate_w"]).then_inc(s["loaded"], 16)
            sp.dma_start(gb[:], T["L1_ffn_gate_b"].rearrange("(d a) -> d a", a=1)).then_inc(s["loaded"], 16)
            sp.dma_start(sw[:], T["L1_ffn_scale_w"].rearrange("(a h) d -> a h d", a=1).to_broadcast([P, H, HD])).then_inc(s["loaded"], 16)

        @block.gpsimd
        def _(pool):
            pool.memset(rows[:], 0.0)
            for k in range(2):
                pool.memset(va[k][:], 0.0)
            pool.memset(mx[:], 0.0).then_inc(s["pool_chain"], 1)
            for h in range(HG):
                pool.wait_ge(s["pool_chain"], h + 1)
                pool.affine_select(out=rows[:], in_=rows[:], compare_op=ALU.not_equal, fill=1.0, base=-ROWS * h,
                                   pattern=[[-1, ROWS]], channel_multiplier=1).then_inc(s["pool_chain"], 1)
            pool.memset(keysD[0][:].bitcast(F32), 0.0).then_inc(s["keys_zeroed"], 1)
            pool.wait_ge(s["keys_zeroed"], 2)

            def body(t, par, prev, cur, nxt, pre):
                for g in range(NG if pre else 0):
                    pool.wait_ge(s["kw_ready"], 2 * (t + 2) + g // 2 + 1)
                    after(pool, s["exp_done"], t * H + HG * (g + 1) if cur else 0)
                    pool.sem_inc(s["pturn"], 1)
                    for i in range(HG):
                        m = pool.tensor_copy(keysD[par][ROWS * i:ROWS * (i + 1), g, i, :],
                                             kw[par][ROWS * i:ROWS * (i + 1), g, :])
                    m.then_inc(s["keys_ready"], 1)

            slots(pool, n, body, ahead=2)

        assert H == 16 and NG * 4 == H

        @block.tensor
        def _(pe):
            def project(w, half):
                for g in range(2):
                    k = (2 * half + g) * HG
                    m = pe.matmul(pA[:, g, :], w[:, k:k + HG, :], xT[:], start=True, stop=True)
                return m

            def form_max(t, par, u):
                g, pair, r = u // 4, u // 2 % 2, u % 2
                if u % 4 == 0:
                    if g % 2 == 0:
                        pe.wait_ge(s["qa_ready"], 2 * t + g // 2 + 1)
                    pe.wait_ge(s["keys_ready"], NG * t + g + 1)
                after(pe, s["nmax_done"], t * 16 + u - 1)
                pe.matmul(p1[u % 2][:], qa[par][:, g, r * P:(r + 1) * P], keysD[par][:, g, 2 * pair:2 * pair + 2, :],
                          start=True, stop=True).then_inc(s["smax_done"], 1)

            def turn_max(t, g):
                pe.wait_ge(s["mx_ready"], t * NG + g + 1)
                for r in range(R):
                    m = pe.transpose(pB[:, 1, r * P:(r + 1) * P], mx[:, r, g * HG:(g + 1) * HG, :], K.ident[:])
                m.then_inc(s["mx_turned"], 1)

            def scores(t, par, h):
                g, i, k = h // HG, h % HG, t * H + h
                if i == 0:
                    pe.wait_ge(s["qb_ready"], t * NG + g + 1)
                after(pe, s["exp_done"], k - 1)
                for kt in range(R):
                    m = pe.matmul(p2[h % 2][:, kt, :], keysD[par][:, g, i, kt * P:(kt + 1) * P], qb[par][:, g, :],
                                  start=True, stop=True)
                m.then_inc(s["scores_done"], 1)

            def weigh(t, par, h):
                g, i, k = h // HG, h % HG, t * H + h
                pe.wait_ge(s["exp_done"], k + 1)
                if h == 0:
                    after(pe, s["av_ready"], t)
                    pe.wait_ge(s["va_ready"], t + 1)
                for kt in range(R):
                    m = pe.matmul(pav[ROWS * i:ROWS * (i + 1), g, :], va[par][:, kt, h, :], probs[h % PB][:, kt, :],
                                  start=(kt == 0), stop=(kt == R - 1))
                m.then_inc(s["av_done"], 1)

            def first_stage(t, b):
                if b == 2:
                    pe.wait_ge(s["xn_ready"], t + 1)
                    after(pe, s["v_ready"], t)
                    for r in range(R):
                        m = pe.transpose(pA[:, 0, r * P:(r + 1) * P], xn[:, r, :], K.ident[:])
                    m.then_inc(s["xn_turned"], 1)
                elif b in (3, 4):
                    pe.wait_ge(s["xT_ready"], t + 1) if b == 3 else pe.wait_ge(s["th_ready"], 2 * t + 1)
                    project(wz, b - 3).then_inc(s["z_done"], 1)
                elif b == 5:
                    pe.wait_ge(s["th_ready"], 2 * t + 2)
                    project(wq, 0).then_inc(s["q_done"], 1)
                elif b == 7:
                    pe.wait_ge(s["qs_ready"], 2 * t + 1)
                    project(wq, 1).then_inc(s["q_done"], 1)
                elif b == 9:
                    pe.wait_ge(s["qs_ready"], 2 * t + 2)
                    project(wk, 0).then_inc(s["k_done"], 1)
                elif b == 11:
                    pe.wait_ge(s["kw_ready"], 2 * t + 1)
                    project(wk, 1).then_inc(s["k_done"], 1)
                elif b == 14:
                    pe.wait_ge(s["kw_ready"], 2 * t + 2)
                    for r in range(R):
                        m = pe.matmul(pA[:, 0, r * P:(r + 1) * P], xT[:, r * P:(r + 1) * P], wv[:], start=True, stop=True)
                    m.then_inc(s["v_done"], 1)

            def last_stage(t, b):
                if b in (2, 3):
                    r = b - 2
                    pe.wait_ge(s["av_ready"], t + 1)
                    if b == 3:
                        pe.wait_ge(s["on_ready"], 2 * t + 1)
                    for g in range(NG):
                        m = pe.transpose(pB[:, g // 2, g % 2 * P:(g % 2 + 1) * P], av[:, g, r * P:(r + 1) * P], K.ident[:])
                    m.then_inc(s["av_turned"], 1)
                elif b == 4:
                    pe.wait_ge(s["on_ready"], 2 * t + 2)
                    for r in range(R):
                        m = pe.transpose(pB[:, 0, r * P:(r + 1) * P], on[:, r, :], K.ident[:])
                    m.then_inc(s["on_turned"], 1)
                elif b == 6:
                    pe.wait_ge(s["onT_ready"], t + 1)
                    pe.matmul(pB[:, 0, :], wgate[:], onT[:], start=True, stop=True).then_inc(s["gate_done"], 1)
                elif b == 10:
                    pe.wait_ge(s["og_ready"], t + 1)
                    for r in range(R):
                        m = pe.matmul(pB[:, 0, r * P:(r + 1) * P], og[:, r * P:(r + 1) * P], wo[:], start=True, stop=True)
                    m.then_inc(s["attn_done"], 1)

            def body(t, par, prev, cur, nxt, pre):
                for b in range(H):
                    if cur:
                        scores(t, par, b)
                    if nxt:
                        form_max(t + 1, 1 - par, b)
                    if cur and b >= LAG:
                        weigh(t, par, b - LAG)
                    if cur and b == 1:
                        after(pe, s["y_written"], t - 1)
                        pe.wait_ge(s["qb_ready"], NG * t + NG - 1)
                        turn_max(t, NG - 1)
                    if prev:
                        if b == 2:
                            if cur:
                                pe.wait_ge(s["qb_ready"], NG * (t + 1))
                            else:
                                pe.wait_ge(s["y_written"], t - 1)
                        if b == 6 and nxt:
                            pe.wait_ge(s["qb_ready"], NG * (t + 1) + 1)
                        if b == 10 and nxt:
                            pe.wait_ge(s["qb_ready"], NG * (t + 1) + 2)
                        last_stage(t - 1, b)
                    if nxt and b in (5, 9, 13):
                        if prev:
                            if b == 5:
                                pe.wait_ge(s["onT_ready"], t)
                            elif b == 9:
                                pe.wait_ge(s["tg_ready"], t)
                            else:
                                pe.wait_ge(s["y_written"], t)
                        after(pe, s["qb_ready"], NG * (t + 1) + (b - 5) // 4)
                        turn_max(t + 1, (b - 5) // 4)
                    if pre:
                        first_stage(t + 2, b)
                if cur:
                    for h in range(H - LAG, H):
                        weigh(t, par, h)

            pe.wait_ge(s["loaded"], LOADS)
            pe.wait_ge(s["w_set"], 1)
            slots(pe, n, body, ahead=2)

        @block.scalar
        def _(act):
            act.wait_ge(s["w_set"], 1)

            def first_stage(t, b):
                if b == 2:
                    act.wait_ge(s["xn_turned"], t + 1)
                    after(act, s["v_done"], t)
                    act.copy(xT[:], pA[:, 0, :]).then_inc(s["xT_ready"], 1)
                elif b in (3, 4):
                    f = slice(2 * (b - 3), 2 * (b - 3) + 2)
                    act.wait_ge(s["z_done"], 2 * t + b - 2)
                    act.activation(th[:, f, :], pA[:], ACT.Tanh, scale=0.5).then_inc(s["th_ready"], 1)
                elif b in (7, 10):
                    half = (b - 7) // 3
                    act.wait_ge(s["qs_ready"], 2 * t + half + 1)
                    act.copy(qr[:, 2 * half:2 * half + 2, :], qs[:, 2 * half:2 * half + 2, :]).then_inc(s["qr_ready"], 1)
                elif b in (9, 11):
                    half = (b - 9) // 2
                    act.wait_ge(s["k_done"], 2 * t + half + 1)
                    act.activation(kr[:, 2 * half:2 * half + 2, :], pA[:], ACT.Identity, bias=one[:]).then_inc(s["kr_ready"], 1)

            def last_stage(t, b):
                if b == 0:
                    act.wait_ge(s["av_done"], (t + 1) * H)
                    after(act, s["av_turned"], 2 * t)
                    act.copy(av[:], pav[:]).then_inc(s["av_ready"], 1)
                elif b == 4:
                    act.wait_ge(s["on_turned"], t + 1)
                    act.copy(onT[:], pB[:, 0, :]).then_inc(s["onT_ready"], 1)
                elif b == 6:
                    act.wait_ge(s["gate_done"], t + 1)
                    act.activation(tg[:], pB[:, 0, :], ACT.Tanh, bias=gb[:], scale=0.5).then_inc(s["tg_ready"], 1)

            def body(t, par, prev, cur, nxt, pre):
                for b in range(H):
                    if cur:
                        k = t * H + b
                        act.wait_ge(s["scores_done"], k + 1)
                        after(act, s["av_done"], k - PB + 1)
                        act.activation(probs[b % PB][:], p2[b % 2][:], ACT.Exp, scale=SM).then_inc(s["exp_done"], 1)
                    if prev:
                        last_stage(t - 1, b)
                    if pre:
                        first_stage(t + 2, b)

            slots(act, n, body, ahead=2)

        @block.vector
        def _(v):
            setup = Chain(v, s["set_chain"], 2)
            setup.begin(0)
            v.memset(keysD[1][:].bitcast(F32), 0.0).then_inc(s["keys_zeroed"], 1)
            v.wait_ge(s["loaded"], LOADS)
            v.wait_ge(s["pool_chain"], HG + 1)
            v.memset(wq[:], 0.0)
            v.memset(wk[:], 0.0)
            v.memset(wz[:], 0.0)
            for i in range(2):
                v.memset(va[i][:, :, :, HD:HD + 1], 1.0)
            v.tensor_scalar(wo[:], wo[:], 0.5, None, ALU.mult)
            v.tensor_scalar(gb[:], gb[:], 0.5, None, ALU.mult)
            v.tensor_reduce(qlow[:], rows[:, HD:2 * HD], AX.X, ALU.add, negate=True)
            v.tensor_reduce(klow[:], rows[:, 2 * HD:3 * HD], AX.X, ALU.add, negate=True)
            v.tensor_copy(one[:], rows[:, MAXROW:MAXROW + 1])
            setup.step(v.tensor_tensor(swq[:], sw[:], raw[:, 0, :].rearrange("p (h d) -> p h d", h=H), ALU.mult))
            v.tensor_tensor(klow[:], klow[:], one[:], ALU.add)
            setup.step(v.tensor_reduce(swsum[:], swq[:], AX.X, ALU.add))
            for r in range(3):
                v.tensor_copy(wq[:, :, r * HD:(r + 1) * HD], raw[:, 0, :].rearrange("p (h d) -> p h d", h=H))
                v.tensor_copy(wk[:, :, r * HD:(r + 1) * HD], raw[:, 1, :].rearrange("p (h d) -> p h d", h=H))
                m = v.tensor_copy(wz[:, :, r * HD:(r + 1) * HD], swsum[:, :, None].to_broadcast([P, H, HD]))
            m.then_inc(s["w_set"], 1)

            def first_stage(t, par, b):
                if b == 0:
                    after(v, s["xn_turned"], t)
                    for r in range(R):
                        for dst in (Y[:, t * R + r, :], xn[:, r, :]):
                            m = v.tensor_scalar(dst, K.X[:, t * R + r, :], K.mean[:, t * R + r, :],
                                                K.rstd[:, t * R + r, :], ALU.subtract, ALU.mult)
                    m.then_inc(s["xn_ready"], 1)
                elif b in (6, 8):
                    i = (b - 6) // 2
                    v.wait_ge(s["q_done"], 2 * t + i + 1)
                    after(v, s["qr_ready"], 2 * t)
                    v.scalar_tensor_tensor(qs[:, 2 * i:2 * i + 2, :], th[:, 2 * i:2 * i + 2, :], 1.0, pA[:],
                                           ALU.add, ALU.mult).then_inc(s["qs_ready"], 1)
                elif b in (9, 11):
                    i = (b - 9) // 2
                    v.wait_ge(s["qr_ready"], 2 * t + i + 1)
                    after(v, s["qb_ready"], NG * (t - 1))
                    v.scalar_tensor_tensor(qa[par][:, 2 * i:2 * i + 2, :], qr[:, 2 * i:2 * i + 2, :].bitcast(F32), qlow[:],
                                           qs[:, 2 * i:2 * i + 2, :], ALU.mult, ALU.add).then_inc(s["qa_ready"], 1)
                elif b in (10, 12):
                    i = (b - 10) // 2
                    v.wait_ge(s["kr_ready"], 2 * t + i + 1)
                    after(v, s["keys_ready"], NG * (t - 1))
                    v.scalar_tensor_tensor(kw[par][:, 2 * i:2 * i + 2, :], kr[:, 2 * i:2 * i + 2, :].bitcast(F32), klow[:],
                                           pA[:], ALU.mult, ALU.add).then_inc(s["kw_ready"], 1)

            def values(t):
                v.wait_ge(s["v_done"], t + 1)
                after(v, s["va_ready"], t)
                v.tensor_copy(vnew[:], pA[:, 0, :]).then_inc(s["v_ready"], 1)

            def place_values(t, par):
                v.wait_ge(s["v_ready"], t + 1)
                after(v, s["av_done"], H * (t - 1))
                v.tensor_copy(va[par][:, :, :, 0:HD],
                              vnew[:].rearrange("p (r h d) -> p r h d", r=R, h=H)).then_inc(s["va_ready"], 1)

            def last_stage(t, b):
                if b in (2, 3):
                    r = b - 2
                    pv = pB[:].rearrange("p a (h w) -> p (a h) w", w=ROWS)
                    v.wait_ge(s["av_turned"], 2 * t + r + 1)
                    v.reciprocal(rden[:, r, :], pv[:, :, HD]).then_inc(s["rden_ready"], 1)
                    v.wait_ge(s["rden_ready"], 2 * t + r + 1)
                    v.tensor_tensor(on[:, r, :].rearrange("p (h d) -> p h d", h=H), pv[:, :, 0:HD],
                                    rden[:, r, :, None].to_broadcast([P, H, HD]), ALU.mult).then_inc(s["on_ready"], 1)
                elif b == 7:
                    v.wait_ge(s["tg_ready"], t + 1)
                    v.scalar_tensor_tensor(og[:], tg[:], 1.0, onT[:], ALU.add, ALU.mult).then_inc(s["og_ready"], 1)
                elif b == 11:
                    v.wait_ge(s["attn_done"], t + 1)
                    v.tensor_tensor(Y[:, bass.ds(t * R, R), :], pB[:, 0, :].rearrange("p (r d) -> p r d", r=R),
                                    Y[:, bass.ds(t * R, R), :], ALU.add).then_inc(s["y_written"], 1)
                elif b == 14:
                    v.wait_ge(s["y_written"], t + 1)
                    v.sem_inc(s["turn"], 1)
                    for r in range(R):
                        v.bn_stats(K.stats[:, t * R + r, :], Y[:, t * R + r, :])

            def maxima(t, u):
                g, pair, r = u // 4, u // 2 % 2, u % 2
                v.wait_ge(s["smax_done"], t * 16 + u + 1)
                v.tensor_reduce(nmax[:, g, r, 2 * pair:2 * pair + 2], p1[u % 2][:], AX.X, ALU.max,
                                negate=True).then_inc(s["nmax_done"], 1)
                if u % 4 == 3:
                    v.wait_ge(s["nmax_done"], t * 16 + u + 1)
                    after(v, s["mx_turned"], NG * (t - 1) + g + 1)
                    v.tensor_copy(mx[:, :, g * HG:(g + 1) * HG, MAXROW], nmax[:, g, :, :]).then_inc(s["mx_ready"], 1)

            def fill(t, par, g):
                v.wait_ge(s["mx_turned"], t * NG + g + 1)
                v.tensor_tensor(qb[par][:, g, :], pB[:, 1, :], qa[par][:, g, :].bitcast(F32), ALU.add).then_inc(s["qb_ready"], 1)

            def body(t, par, prev, cur, nxt, pre):
                for b in range(H):
                    if nxt:
                        maxima(t + 1, b)
                    if b == 1 and cur:
                        fill(t, par, NG - 1)
                    if b == 1 and nxt:
                        place_values(t + 1, 1 - par)
                    if prev:
                        last_stage(t - 1, b)
                    if nxt and b in (5, 9, 13):
                        fill(t + 1, 1 - par, (b - 5) // 4)
                    if pre:
                        first_stage(t + 2, par, b)
                        if b == 15:
                            values(t + 2)

            slots(v, n, body, ahead=2)


def l1_expert_weights(nc, K, W, T, name):
    E, F, FC = W.E, W.F, W.FC
    with ExitStack() as c:
        sb = lambda nm, s, dt=F32: c.enter_context(nc.sbuf_tensor(f"{nm}_{name}", s, dt))
        w1f, w2f = sb("w1f", [P, E, F]), sb("w2f", [P, FC, E, D])
        tabf = sb("tabf", [96, 3 * F])
        b2f = sb("b2f", [96, E * D])
        s = c.enter_context(semaphores(nc, name, ("loaded", "pool_chain", "set_chain", "high_set")))
        block = c.enter_context(nc.Block())
        LOADS = 16 * (3 + 3 * 4 + 7)

        @block.sync
        def _(sp):
            sp.dma_start(w1f[:], T["L1_ffn_w1"].rearrange("e d f -> d e f")).then_inc(s["loaded"], 16)
            for k in range(FC):
                sp.dma_start(w2f[:, k, :, :],
                             T["L1_ffn_w2"][:, k * P:(k + 1) * P, :].rearrange("e f d -> f e d")).then_inc(s["loaded"], 16)
            sp.dma_start(W.wr[:], T["L1_ffn_moe_gate_w"]).then_inc(s["loaded"], 16)
            for dst, k in ((W.br, "moe_gate_b"), (W.rs, "res_scale"), (W.n1g, "n1_g"), (W.n1b, "n1_b"), (W.n2g, "n2_g"),
                           (W.n2b, "n2_b")):
                sp.dma_start(dst[:], T[f"L1_ffn_{k}"].rearrange("(a d) -> a d", a=1).to_broadcast([P, dst.shape[1]])).then_inc(s["loaded"], 16)

        @block.scalar
        def _(act):
            act.wait_ge(s["pool_chain"], 2)
            for q in range(3):
                for i, k in enumerate(("b1", "ln_g", "ln_b")):
                    act.dma_start(tabf[32 * q:32 * q + E, i * F:(i + 1) * F], T[f"L1_ffn_{k}"]).then_inc(s["loaded"], 16)
                act.dma_start(b2f[32 * q:32 * q + 1, :], T["L1_ffn_b2"].rearrange("(a e) d -> a (e d)", a=1)).then_inc(s["loaded"], 16)
            act.wait_ge(s["loaded"], LOADS)
            act.copy(W.w1h[:], w1f[:])
            act.copy(W.w2h[:], w2f[:]).then_inc(s["high_set"], 1)

        @block.gpsimd
        def _(pool):
            pool.memset(tabf[:], 0.0).then_inc(s["pool_chain"], 1)
            pool.memset(b2f[:], 0.0).then_inc(s["pool_chain"], 1)
            pool.iota(W.iota[:], pattern=[[1, E]], base=0, channel_multiplier=0, allow_small_or_imprecise_dtypes=True)
            pool.memset(W.sel[:], 0.0).then_inc(s["pool_chain"], 1)
            pool.wait_ge(s["pool_chain"], 3)
            pool.affine_select(out=W.sel[:], in_=W.sel[:], compare_op=ALU.not_equal, fill=1.0, base=0,
                               pattern=[[-1, E], [0, P]], channel_multiplier=1)

        @block.vector
        def _(v):
            v.memset(W.ones[:], 1.0)
            v.wait_ge(s["loaded"], LOADS)
            v.wait_ge(s["pool_chain"], 2)
            ch = Chain(v, s["set_chain"], 4)
            ch.begin(0)
            lo, hi = slice(32, 64), slice(64, 96)
            pairs = ((W.tab3, tabf), (W.b23, b2f))
            for t3, tf in pairs:
                m = v.tensor_copy(t3[:], tf[:])
            ch.step(m)
            for r in (lo, hi):
                for t3, tf in pairs:
                    m = v.tensor_tensor(tf[r, :], tf[r, :], t3[r, :], ALU.subtract)
            ch.step(m)
            for r in (lo, hi):
                for t3, tf in pairs:
                    m = v.tensor_copy(t3[r, :], tf[r, :])
            ch.step(m)
            for t3, tf in pairs:
                m = v.tensor_tensor(tf[hi, :], tf[hi, :], t3[hi, :], ALU.subtract)
            ch.step(m)
            for t3, tf in pairs:
                v.tensor_copy(t3[hi, :], tf[hi, :])
            v.wait_ge(s["high_set"], 1)
            v.tensor_tensor(W.w1l[:], w1f[:], W.w1h[:].bitcast(F32), ALU.subtract)
            v.tensor_tensor(W.w2l[:], w2f[:], W.w2h[:].bitcast(F32), ALU.subtract)
            ch.end()


class ExpertWeights:
    def __init__(self, nc, c, T, name):
        self.E, _, self.F = T["L1_ffn_w1"].shape
        E, F = self.E, self.F
        self.FC = F // P
        sb = lambda nm, s, dt=F32: c.enter_context(nc.sbuf_tensor(f"{nm}_{name}", s, dt))
        self.w1h, self.w1l = sb("w1h", [P, E, F], F32R), sb("w1l", [P, E, F], F32R)
        self.w2h, self.w2l = sb("w2h", [P, self.FC, E, D], F32R), sb("w2l", [P, self.FC, E, D], F32R)
        self.tab3, self.b23 = sb("tab3", [96, 3 * F], BF16), sb("b23", [96, E * D], BF16)
        self.sel, self.ones = sb("sel", [96, E, P], BF16), sb("ones", [96, P], BF16)
        self.wr, self.br, self.rs, self.iota = sb("wr", [P, E]), sb("br", [P, E]), sb("rs", [P, E]), sb("iota", [P, E])
        self.n1g, self.n1b, self.n2g, self.n2b = (sb(k, [P, D]) for k in ("n1g", "n1b", "n2g", "n2b"))


def l1_experts(nc, K, Y, T, name):
    G = 4
    N = G * P
    n = K.tiles // G
    PAD = 6
    with ExitStack() as c:
        W = ExpertWeights(nc, c, T, name)
        l1_expert_weights(nc, K, W, T, name + "w")
        E, F, FC = W.E, W.F, W.FC
        sb = lambda nm, s, dt=F32: c.enter_context(nc.sbuf_tensor(f"{nm}_{name}", s, dt))
        ps = lambda nm, s, dt=F32: c.enter_context(nc.psum_tensor(f"{nm}_{name}", s, dt))
        hot, wsum, rscale = sb("hot", [P, K.tiles, E]), sb("wsum", [P, K.tiles, 1]), sb("rscale", [P, K.tiles, 1])
        x1 = sb("x1", [P, G, D])
        x1T, x1h = sb("x1T", [P, N]), sb("x1h", [P, N], F32R)
        x1l = [sb(f"x1l{i}", [P, N], F32R) for i in range(2)]
        xmh, xml = sb("xmh", [P, E, N], F32R), sb("xml", [P, E, N], F32R)
        mask = sb("mask", [P, E, N], BF16)
        logit, struck = sb("logit", [P, G, E + PAD]), sb("struck", [P, G, E + PAD])
        top8, index, chosen = sb("top8", [P, G, 8]), sb("index", [P, G, E]), sb("chosen", [P, G])
        hot_new, rs_all = sb("hot_new", [P, G, E]), sb("rs_all", [P, G, E])
        dv, ev, den, wv = sb("dv", [P, G]), sb("ev", [P, G]), sb("den", [P, G]), sb("wv", [P, G])
        hot3 = sb("hot3", [P, G, 96], BF16)
        hotT = [sb(f"hotT{i}", [96, N], BF16) for i in range(2)]
        tab = [sb(f"tab{i}", [P, G, 2, F]) for i in range(2)]
        h, gl = sb("h", [P, G, F]), sb("gl", [P, G, F])
        gTh, gTl = sb("gTh", [P, FC, N], F32R), sb("gTl", [P, FC, N], F32R)
        st, mean, var, rstd, tt = sb("st", [P, G, 6]), sb("mean", [P, G, 1]), sb("var", [P, G, 1]), sb("rstd", [P, G, 1]), sb("tt", [P, G, 1])
        y, ym = sb("y", [P, G, D]), [sb(f"ym{i}", [P, E, D]) for i in range(2)]
        ph = [ps(f"ph{i}", [P, F]) for i in range(2)]
        py = ps("py", [P, 2, 4, D])
        pk = [ps(f"pk{i}", [P, N]) for i in range(2)]
        pt = ps("pt", [P, 2, F])
        pm = ps("pm", [P, N])
        pmb = pm[:].bitcast(BF16)
        s = c.enter_context(semaphores(nc, name, (
            "x1_ready", "x1_kept", "x1_turned", "x1T_ready", "split_ready", "logits_done", "dv_ready",
            "ev_ready", "hot_ready", "hot_turned", "hotT_ready", "tab_done", "tab_ready", "mask_done", "mask_ready",
            "xmh_ready", "xml_ready", "h_done", "h_copied", "h_ready", "gl_ready", "gl_turned", "gTh_ready", "gTl_ready",
            "y_done", "y_read", "sum_chain", "picked", "y_full", "norm_chain", "pre_chain", "route_chain", "fin_chain", "set0",
            "pturn", "turn")))
        block = c.enter_context(nc.Block())

        @block.gpsimd
        def _(pool):
            pool.memset(hot3[:], 0.0).then_inc(s["set0"], 1)

            def sum_experts(t, j):
                i, m = t * G + j, ym[j % 2]
                pool.wait_ge(s["y_read"], (i + 1) * 2)
                pool.tensor_tensor(m[:, 0:4, :], m[:, 0:4, :], m[:, 4:8, :], ALU.add).then_inc(s["sum_chain"], 1)
                pool.wait_ge(s["sum_chain"], 2 * i + 1)
                pool.tensor_tensor(m[:, 0:2, :], m[:, 0:2, :], m[:, 2:4, :], ALU.add).then_inc(s["sum_chain"], 1)
                pool.wait_ge(s["sum_chain"], 2 * i + 2)
                if j == 0:
                    after(pool, s["y_full"], t)
                pool.tensor_tensor(y[:, j, :], m[:, 0, :], m[:, 1, :], ALU.add).then_inc(s["picked"], 1)

            def body(t, par, prev, cur, nxt, pre):
                i = t + 2
                if pre:
                    pool.wait_ge(s["x1_ready"], i + 1)
                    pool.sem_inc(s["pturn"], 1)
                    pool.tensor_copy(Y[:, bass.ds(i * G, G), :], x1[:]).then_inc(s["x1_kept"], 1)
                if cur:
                    for j in range(2):
                        sum_experts(t, j)
                for e in range(E):
                    if pre:
                        pool.wait_ge(s["mask_ready"], i * E + e + 1)
                        if e == 0:
                            pool.wait_ge(s["split_ready"], i + 1)
                            after(pool, s["h_done"], i * G)
                        pool.tensor_tensor(xml[:, e, :], x1l[par][:].bitcast(F32), mask[:, e, :], ALU.mult).then_inc(s["xml_ready"], 1)
                    if cur and e in (3, 7):
                        sum_experts(t, 2 + e // 4)

            slots(pool, n, body, ahead=2)

        @block.tensor
        def _(pe):
            def first(t, par, j):
                after(pe, s["h_copied"], t * G + j - 1)
                tok = slice(j * P, (j + 1) * P)
                pe.matmul(ph[j % 2][:], hotT[par][:, tok], W.tab3[:, 0:F], start=True, stop=False)
                for e in range(E):
                    if j == 0:
                        pe.wait_ge(s["xmh_ready"], t * E + e + 1)
                        pe.wait_ge(s["xml_ready"], t * E + e + 1)
                    pe.matmul(ph[j % 2][:], xmh[:, e, tok], W.w1h[:, e, :], start=False, stop=False)
                    pe.matmul(ph[j % 2][:], xmh[:, e, tok], W.w1l[:, e, :], start=False, stop=False)
                    m = pe.matmul(ph[j % 2][:], xml[:, e, tok], W.w1h[:, e, :], start=False, stop=(e == E - 1))
                m.then_inc(s["h_done"], 1)

            def second(t, j):
                tok = slice(j * P, (j + 1) * P)
                for b in range(2):
                    k = (t * G + j) * 2 + b
                    if j or b:
                        after(pe, s["y_read"], k - 1)
                    pe.matmul(py[:, b, :, :], W.ones[:], W.b23[:, 512 * b:512 * (b + 1)], start=True, stop=False)
                    for k2 in range(FC):
                        ex = slice(4 * b, 4 * b + 4)
                        pe.matmul(py[:, b, :, :], gTh[:, k2, tok], W.w2h[:, k2, ex, :], start=False, stop=False)
                        pe.matmul(py[:, b, :, :], gTh[:, k2, tok], W.w2l[:, k2, ex, :], start=False, stop=False)
                        m = pe.matmul(py[:, b, :, :], gTl[:, k2, tok], W.w2h[:, k2, ex, :], start=False, stop=(k2 == FC - 1))
                    m.then_inc(s["y_done"], 1)

            def route(t, j, par):
                if j == 0:
                    pe.wait_ge(s["x1_ready"], t + 1)
                    after(pe, s["hotT_ready"], t)
                    for q in range(G):
                        m = pe.transpose(pm[:, q * P:(q + 1) * P], x1[:, q, :], K.ident[:])
                    m.then_inc(s["x1_turned"], 1)
                if j == 2:
                    pe.wait_ge(s["x1T_ready"], t + 1)
                    pe.wait_ge(s["split_ready"], t + 1)
                    for q in range(G):
                        m = pe.matmul(pm[:, q * E:(q + 1) * E], x1T[:, q * P:(q + 1) * P], W.wr[:], start=True, stop=True)
                    m.then_inc(s["logits_done"], 1)
                if j == 3:
                    pe.wait_ge(s["hot_ready"], t + 1)
                    for q in range(G):
                        m = pe.transpose(pmb[0:96, q * P:(q + 1) * P], hot3[:, q, :], K.identb[:])
                    m.then_inc(s["hot_turned"], 1)

            def spread(t, par, j):
                k = t * E + 2 * j
                if j == 0:
                    pe.wait_ge(s["hotT_ready"], t + 1)
                after(pe, s["tab_ready"], t * G + j)
                pe.matmul(pt[:], hotT[par][:, j * P:(j + 1) * P], W.tab3[:, F:3 * F], start=True,
                          stop=True).then_inc(s["tab_done"], 1)
                for i in range(2):
                    after(pe, s["mask_ready"], k + i - 1)
                    pe.matmul(pk[i][:], W.sel[:, 2 * j + i, :], hotT[par][:], start=True, stop=True).then_inc(s["mask_done"], 1)

            def body(t, par, prev, cur, nxt, pre):
                if nxt:
                    first(t + 1, 1 - par, 0)
                if pre:
                    route(t + 2, 0, par)
                if cur:
                    pe.wait_ge(s["gl_ready"], t + 1)
                    after(pe, s["y_read"], t * G * 2)
                    for k2 in range(FC):
                        for q in range(G):
                            m = pe.transpose(py[:, k2, q, :], gl[:, q, k2 * P:(k2 + 1) * P], K.ident[:])
                    m.then_inc(s["gl_turned"], 1)
                if nxt:
                    first(t + 1, 1 - par, 1)
                    first(t + 1, 1 - par, 2)
                if cur:
                    pe.wait_ge(s["gTh_ready"], t + 1)
                    pe.wait_ge(s["gTl_ready"], t + 1)
                    second(t, 0)
                if pre:
                    route(t + 2, 2, par)
                if cur:
                    second(t, 1)
                if nxt:
                    first(t + 1, 1 - par, 3)
                if pre:
                    route(t + 2, 3, par)
                    spread(t + 2, par, 0)
                    spread(t + 2, par, 1)
                if cur:
                    second(t, 2)
                if pre:
                    spread(t + 2, par, 2)
                    spread(t + 2, par, 3)
                if cur:
                    second(t, 3)

            slots(pe, n, body, ahead=2)

        @block.scalar
        def _(act):
            def spread(t, par, j):
                act.wait_ge(s["tab_done"], t * G + j + 1)
                act.copy(tab[par][:, j, :, :], pt[:]).then_inc(s["tab_ready"], 1)
                for i in range(2):
                    e = 2 * j + i
                    act.wait_ge(s["mask_done"], t * E + e + 1)
                    if e == 0:
                        after(act, s["xml_ready"], t * E)
                        after(act, s["xmh_ready"], t * E)
                    act.copy(mask[:, e, :], pk[i][:]).then_inc(s["mask_ready"], 1)

            def body(t, par, prev, cur, nxt, pre):
                for j in range(G):
                    if nxt:
                        act.wait_ge(s["h_done"], (t + 1) * G + j + 1)
                        if j == 0:
                            after(act, s["gl_ready"], t + 1)
                        act.copy(h[:, j, :], ph[j % 2][:]).then_inc(s["h_copied"], 1)
                    if pre and j == 0:
                        act.wait_ge(s["x1_turned"], t + 3)
                        after(act, s["xmh_ready"], (t + 2) * E)
                        act.copy(x1h[:], pm[:])
                        act.copy(x1T[:], pm[:]).then_inc(s["x1T_ready"], 1)
                    if cur and j == 0:
                        act.wait_ge(s["gl_turned"], t + 1)
                        after(act, s["y_done"], t * G * 2)
                        act.copy(gTh[:], py[:].rearrange("p c q d -> p c (q d)")).then_inc(s["gTh_ready"], 1)
                if pre:
                    act.wait_ge(s["hot_turned"], t + 3)
                    act.copy(hotT[par][:], pmb[0:96, 0:N]).then_inc(s["hotT_ready"], 1)
                    for j in range(G):
                        spread(t + 2, par, j)
                    act.wait_ge(s["dv_ready"], t + 3)
                    act.activation(ev[:], dv[:], ACT.Exp).then_inc(s["ev_ready"], 1)
                if nxt:
                    act.wait_ge(s["h_ready"], t + 2)
                    after(act, s["gl_turned"], t + 1)
                    act.activation(gl[:], h[:], ACT.Gelu).then_inc(s["gl_ready"], 1)

            slots(act, n, body, ahead=2)

        @block.vector
        def _(v):
            v.memset(logit[:], BIG).then_inc(s["set0"], 1)
            v.wait_ge(s["set0"], 2)
            pch = Chain(v, s["pre_chain"], 2)
            rch = Chain(v, s["route_chain"], 11, s["turn"])
            hch = Chain(v, s["norm_chain"], 1 + MOMENT_STEPS + RSQRT_STEPS + 2)
            fch = Chain(v, s["fin_chain"], MOMENT_STEPS + RSQRT_STEPS + 6, s["turn"])

            def norm1(t):
                pch.begin(t)
                if not (isinstance(t, int) and t == 0):
                    v.wait_ge(s["x1_kept"], t)
                    v.wait_ge(s["x1_turned"], t)
                for j in range(G):
                    m = v.tensor_scalar(x1[:, j, :], Y[:, t * G + j, :], K.mean[:, t * G + j, :],
                                        K.rstd[:, t * G + j, :], ALU.subtract, ALU.mult)
                pch.step(m)
                pch.step(v.tensor_tensor(x1[:], x1[:], W.n1g[:, None, :].to_broadcast([P, G, D]), ALU.mult))
                v.tensor_tensor(x1[:], x1[:], W.n1b[:, None, :].to_broadcast([P, G, D]), ALU.add).then_inc(s["x1_ready"], 1)
                pch.end()

            def split(t, par):
                v.wait_ge(s["x1T_ready"], t + 1)
                after(v, s["xml_ready"], (t - 1) * E)
                v.tensor_tensor(x1l[par][:], pm[:], x1h[:].bitcast(F32), ALU.subtract).then_inc(s["split_ready"], 1)

            def top2(t):
                rch.begin(t)
                v.wait_ge(s["logits_done"], t + 1)
                rch.step_apart(v.tensor_tensor(logit[:, :, 0:E], pm[:, 0:G * E].rearrange("p (g e) -> p g e", g=G),
                                               W.br[:, None, :].to_broadcast([P, G, E]), ALU.add))
                for j in range(G):
                    m = v.max(top8[:, j, :], logit[:, j, :])
                rch.step_apart(m)
                for j in range(G):
                    m = v.match_replace(struck[:, j, :], top8[:, j, :], logit[:, j, :], -BIG)
                rch.step(m)
                v.tensor_tensor(dv[:], top8[:, :, 7], top8[:, :, 6], ALU.subtract).then_inc(s["dv_ready"], 1)
                rch.step(v.scalar_tensor_tensor(index[:], struck[:, :, 0:E], -BIG / 2, W.iota[:, None, :].to_broadcast([P, G, E]),
                                                ALU.is_le, ALU.mult))
                rch.step(v.tensor_reduce(chosen[:], index[:], AX.X, ALU.max))
                rch.step(v.tensor_tensor(hot_new[:], W.iota[:, None, :].to_broadcast([P, G, E]),
                                         chosen[:, :, None].to_broadcast([P, G, E]), ALU.is_equal))
                for q in range(3):
                    m = v.tensor_copy(hot3[:, :, 32 * q:32 * q + E], hot_new[:])
                m.then_inc(s["hot_ready"], 1)
                v.tensor_copy(hot[:, bass.ds(t * G, G), :], hot_new[:])
                rch.step(v.tensor_tensor(rs_all[:], hot_new[:], W.rs[:, None, :].to_broadcast([P, G, E]), ALU.mult))
                rch.step(v.tensor_reduce(rscale[:, bass.ds(t * G, G), 0], rs_all[:], AX.X, ALU.add))

            def weight_sum(t):
                v.wait_ge(s["ev_ready"], t + 1)
                rch.step(v.tensor_scalar(den[:], ev[:], 1.0, None, ALU.add))
                rch.step(v.reciprocal(den[:], den[:]))
                rch.step(v.tensor_tensor(wv[:], ev[:], den[:], ALU.mult))
                v.tensor_tensor(wsum[:, bass.ds(t * G, G), 0], wv[:], den[:], ALU.add)
                rch.end()

            def inner_norm(t, par):
                hch.begin(t)
                v.wait_ge(s["h_copied"], (t + 1) * G)
                for j in range(G):
                    m = v.bn_stats(st[:, j, :], h[:, j, :])
                hch.step(m)
                moments(v, hch.step, F, [st[:, :, i:i + 1] for i in range(6)], mean[:], var[:], tt[:])
                rsqrt(v, hch.step, rstd[:], var[:], tt[:])
                for j in range(G):
                    m = v.tensor_scalar(h[:, j, :], h[:, j, :], mean[:, j, :], rstd[:, j, :], ALU.subtract, ALU.mult)
                hch.step(m)
                v.wait_ge(s["tab_ready"], (t + 1) * G)
                hch.step(v.tensor_tensor(h[:], h[:], tab[par][:, :, 0, :], ALU.mult))
                v.tensor_tensor(h[:], h[:], tab[par][:, :, 1, :], ALU.add).then_inc(s["h_ready"], 1)
                hch.end()

            def pick(t, j):
                i = t * G + j
                for b in range(2):
                    k = i * 2 + b
                    v.wait_ge(s["y_done"], k + 1)
                    if b == 0:
                        after(v, s["picked"], i - 1)
                    v.tensor_tensor(ym[j % 2][:, 4 * b:4 * b + 4, :], py[:, b, :, :],
                                    hot[:, bass.ds(i, 1), 4 * b:4 * b + 4].rearrange("p a e -> p (a e)")[:, :, None].to_broadcast([P, 4, D]),
                                    ALU.mult).then_inc(s["y_read"], 1)

            def finish(t):
                fch.begin(t)
                v.wait_ge(s["picked"], (t + 1) * G)
                for op, w in ((0, rscale), (1, wsum)):
                    for j in range(G):
                        m = v.scalar_tensor_tensor(y[:, j, :], y[:, j, :], w[:, t * G + j, :], Y[:, t * G + j, :], ALU.mult, ALU.add)
                    fch.step(m) if op == 0 else fch.step_apart(m)
                for j in range(G):
                    m = v.bn_stats(st[:, j, :], y[:, j, :])
                fch.step(m)
                moments(v, fch.step, D, [st[:, :, i:i + 1] for i in range(6)], mean[:], var[:], tt[:])
                rsqrt(v, fch.step, rstd[:], var[:], tt[:])

            def finish_end(t):
                for j in range(G):
                    m = v.tensor_scalar(y[:, j, :], y[:, j, :], mean[:, j, :], rstd[:, j, :], ALU.subtract, ALU.mult)
                fch.step(m)
                fch.step(v.tensor_tensor(y[:], y[:], W.n2g[:, None, :].to_broadcast([P, G, D]), ALU.mult))
                fch.step(v.tensor_tensor(y[:], y[:], W.n2b[:, None, :].to_broadcast([P, G, D]), ALU.add))
                v.scalar_tensor_tensor(K.X[:, bass.ds(t * G, G), :], y[:], 0.5, K.X[:, bass.ds(t * G, G), :],
                                       ALU.mult, ALU.add).then_inc(s["y_full"], 1)
                fch.end()

            def new_stats(t):
                v.wait_ge(s["y_full"], t + 1)
                v.sem_inc(s["turn"], 1)
                for j in range(G):
                    m = v.bn_stats(K.stats[:, t * G + j, :], K.X[:, t * G + j, :])
                return m

            def body(t, par, prev, cur, nxt, pre):
                if pre:
                    norm1(t + 2)
                if prev:
                    finish(t - 1)
                if pre:
                    split(t + 2, par)
                if cur:
                    v.wait_ge(s["gTh_ready"], t + 1)
                    after(v, s["y_done"], t * G * 2)
                    v.tensor_tensor(gTl[:], py[:].rearrange("p c q d -> p c (q d)"), gTh[:].bitcast(F32),
                                    ALU.subtract).then_inc(s["gTl_ready"], 1)
                if prev:
                    finish_end(t - 1)
                if cur:
                    pick(t, 0)
                if pre:
                    top2(t + 2)
                if cur:
                    pick(t, 1)
                if prev:
                    new_stats(t - 1)
                if nxt:
                    inner_norm(t + 1, 1 - par)
                if cur:
                    pick(t, 2)
                if pre:
                    for e in range(E):
                        v.wait_ge(s["mask_ready"], (t + 2) * E + e + 1)
                        if e == 0:
                            after(v, s["h_done"], (t + 2) * G)
                        v.tensor_tensor(xmh[:, e, :], x1h[:].bitcast(F32), mask[:, e, :], ALU.mult).then_inc(s["xmh_ready"], 1)
                if cur:
                    pick(t, 3)
                if pre:
                    weight_sum(t + 2)

            slots(v, n, body, ahead=2)



def macaron_kernel(nc, T, out):
    x = T["L0_attn_X"]
    B, S, _ = x.shape
    with ExitStack() as ctx:
        K = Core(nc, ctx, B * S // P)
        load_phase(nc, K, x)
        with ExitStack() as weights:
            l0_ffn_weights(nc, K, weights, T["L0_ffn_classifier_weight"], T["L0_ffn_e_score_correction_bias"],
                           T["L0_ffn_gate_up_proj"], T["L0_ffn_down_proj"])
            norm_phase(nc, K, "n1")
            l0_ffn(nc, K, "f1")
            norm_phase(nc, K, "n2")
            l0_attention(nc, K, T["L0_attn_Wq"], T["L0_attn_Wk"], T["L0_attn_Wv"], S, "a1")
            norm_phase(nc, K, "n3")
            l0_ffn(nc, K, "f2")
        norm_phase(nc, K, "n4")
        l1_ffn(nc, K, T, S, "g1")
        norm_phase(nc, K, "n5")
        rwkv(nc, K, T, S, "r1")
        norm_phase(nc, K, "n6")
        l1_ffn(nc, K, T, S, "g2")
        store_phase(nc, K, out)


def store_phase(nc, K, out):
    with ExitStack() as c:
        s = c.enter_context(semaphores(nc, "store", ("stored",)))
        block = c.enter_context(nc.Block())

        @block.sync
        def _(sp):
            sp.dma_start(out.rearrange("b (t p) d -> p (b t) d", p=P), K.X[:]).then_inc(s["stored"], 16)
            sp.wait_ge(s["stored"], 16)


_INS = ["L0_attn_X", "L0_attn_Wq", "L0_attn_Wk", "L0_attn_Wv", "L0_ffn_classifier_weight",
        "L0_ffn_e_score_correction_bias", "L0_ffn_gate_up_proj", "L0_ffn_down_proj", "L1_attn_xk", "L1_attn_xv",
        "L1_attn_time_decay", "L1_attn_time_first", "L1_attn_time_mix_k", "L1_attn_time_mix_v",
        "L1_attn_time_mix_r", "L1_attn_Wk", "L1_attn_Wv", "L1_attn_Wr", "L1_attn_Wo", "L1_ffn_q_w", "L1_ffn_k_w",
        "L1_ffn_v_w", "L1_ffn_out_w", "L1_ffn_gate_w", "L1_ffn_gate_b", "L1_ffn_scale_w", "L1_ffn_n1_g",
        "L1_ffn_n1_b", "L1_ffn_n2_g", "L1_ffn_n2_b", "L1_ffn_moe_gate_w", "L1_ffn_moe_gate_b", "L1_ffn_w1",
        "L1_ffn_b1", "L1_ffn_ln_g", "L1_ffn_ln_b", "L1_ffn_w2", "L1_ffn_b2", "L1_ffn_res_scale"]


def kernel(**inputs):
    import numpy as _np
    import concourse.bacc as _bacc
    from concourse import mybir as _mybir
    from concourse.bass_utils import run_bass_kernel_spmd as _run

    nc = _bacc.Bacc("TRN2", target_bir_lowering=False, num_devices=1)
    arrays, args = {}, {}
    for name in _INS:
        if name in ("L1_attn_xk", "L1_attn_xv"):
            continue
        a = _np.ascontiguousarray(inputs[name])
        arrays[f"in_{name}_dram"] = a
        args[name] = nc.dram_tensor(f"in_{name}_dram", a.shape, _mybir.dt.from_np(a.dtype), kind="ExternalInput").ap()
    shape = inputs["L0_attn_X"].shape
    out = nc.dram_tensor("out_0_dram", shape, _mybir.dt.float32, kind="ExternalOutput").ap()
    macaron_kernel(nc, args, out)
    r = _run(nc, [arrays], core_ids=[0])
    return r.results[0]["out_0_dram"]
```
